# Optimizing a Trainium2 kernel written in Bass

```python
import numpy as np
import jax
import jax.numpy as jnp

def _softmax(x, axis=-1):
    return jax.nn.softmax(x, axis=axis)

def _gelu(x):
    return jax.nn.gelu(x, approximate=True)

def _silu(x):
    return jax.nn.silu(x)

def _sigmoid(x):
    return jax.nn.sigmoid(x)

def _layernorm(x, axis=-1, eps=1e-05):
    m = jnp.mean(x, axis=axis, keepdims=True)
    v = jnp.var(x, axis=axis, keepdims=True)
    return (x - m) / jnp.sqrt(v + eps)

def _scatter_add(tgt, idx, src, axis=0):
    return tgt.at[idx].add(src)

def _segment_sum(src, seg, n):
    return jax.ops.segment_sum(src, seg, n)
kernel_name = 'mk_gnn_preln_d4_gnn_r16_8765eb'

def setup_inputs(seed: int=0):
    np.random.seed(seed)
    _w = jnp.asarray

    def _rec_inputs():
        import jax
        import jax.numpy as jnp
        _gk = jax.random.key(seed)
        x = -0.000202 + 1 * jax.random.normal(jax.random.fold_in(_gk, 1), (3125, 128), jnp.float32)
        _s = jax.random.randint(jax.random.fold_in(_gk, 2), (50000,), 0, 3125, jnp.int32)
        _d = jax.random.randint(jax.random.fold_in(_gk, 3), (50000,), 0, 3125, jnp.int32)
        _loop = jnp.arange(3125, dtype=jnp.int32)
        src = jnp.concatenate([_s, _d, _loop])
        dst = jnp.concatenate([_d, _s, _loop])
        _o = jnp.argsort(dst, stable=True)
        src = src[_o]
        dst = dst[_o]
        edge_attr_64 = -9.77346e-05 + 0.999888 * jax.random.normal(jax.random.fold_in(_gk, 12), (103125, 64), jnp.float32)
        edge_weight = jax.random.uniform(jax.random.fold_in(_gk, 14), (103125,), jnp.float32, 0.0, 0.999999)
        return (x, src, dst, edge_attr_64, edge_weight)
    x, src, dst, edge_attr_64, edge_weight = _rec_inputs()

    def _L0_gnn_setup():
        import jax, jax.numpy as jnp
        import numpy as np
        N_NODES = 3125
        N_EDGES = 50000
        NODE_F = 128
        EDGE_F = 64
        GRAPH_F = 128

        def leaky_relu(x):
            return jax.nn.leaky_relu(x, negative_slope=0.01)

        def segment_softmax(logits, seg, num_segments):
            m = jax.ops.segment_max(logits, seg, num_segments=num_segments)
            m = jnp.where(jnp.isfinite(m), m, 0.0)
            ex = jnp.exp(logits - m[seg])
            s = jax.ops.segment_sum(ex, seg, num_segments=num_segments)
            return ex / s[seg]

        def _lin(key, fan_in, fan_out):
            k1, k2 = jax.random.split(key)
            bound = 1.0 / np.sqrt(fan_in)
            W = jax.random.uniform(k1, (fan_in, fan_out), minval=-bound, maxval=bound, dtype=jnp.float32)
            b = jax.random.uniform(k2, (fan_out,), minval=-bound, maxval=bound, dtype=jnp.float32)
            return (W, b)
        key = jax.random.key(seed)
        ks = jax.random.split(key, 12)
        node_feats = jax.random.normal(ks[0], (N_NODES, NODE_F), dtype=jnp.float32)
        edge_feats = jax.random.normal(ks[1], (N_EDGES, EDGE_F), dtype=jnp.float32)
        src = jax.random.randint(ks[2], (N_EDGES,), 0, N_NODES, dtype=jnp.int32)
        dst = jax.random.randint(ks[3], (N_EDGES,), 0, N_NODES, dtype=jnp.int32)
        Wn, bn = _lin(ks[4], NODE_F, GRAPH_F)
        We1, be1 = _lin(ks[5], NODE_F + EDGE_F, GRAPH_F)
        We2, be2 = _lin(ks[6], 2 * GRAPH_F, 1)
        Wet, bet = _lin(ks[7], GRAPH_F, GRAPH_F)
        W1, b1 = _lin(ks[8], 2 * GRAPH_F, GRAPH_F)
        W2, b2 = _lin(ks[9], GRAPH_F, GRAPH_F)
        return dict(node_feats=node_feats, edge_feats=edge_feats, src=src, dst=dst, Wn=Wn, bn=bn, We1=We1, be1=be1, We2=We2, be2=be2, Wet=Wet, bet=bet, W1=W1, b1=b1, W2=W2, b2=b2)
    _L0_gnn_all = _L0_gnn_setup()
    _L0_gnn_in = {k: v for k, v in _L0_gnn_all.items() if k in ('Wn', 'bn', 'We1', 'be1', 'We2', 'be2', 'Wet', 'bet', 'W1', 'b1', 'W2', 'b2')}
    del _L0_gnn_all

    def _L1_gnn_setup():
        import jax, jax.numpy as jnp
        import numpy as np
        N_NODES = 6250
        N_EDGES = 100000
        D_IN = 128
        D_HID = 128

        def gcn_layer(x, src, dst, ew, W, b, n):
            h = x @ W
            deg = jax.ops.segment_sum(ew, dst, num_segments=n) + 1.0
            dis = jnp.where(deg > 0, jax.lax.rsqrt(deg), 0.0)
            norm = dis[src] * ew * dis[dst]
            agg = jax.ops.segment_sum(norm[:, None] * h[src], dst, num_segments=n)
            agg = agg + (dis * dis)[:, None] * h
            return agg + b

        def prelu(x, alpha):
            return jnp.where(x >= 0, x, alpha * x)
        key = jax.random.key(seed)
        ks = jax.random.split(key, 12)
        x = jax.random.normal(ks[0], (N_NODES, D_IN), dtype=jnp.float32)
        edge_index = jax.random.randint(ks[1], (2, N_EDGES), 0, N_NODES, dtype=jnp.int64)
        edge_weight = jax.random.uniform(ks[2], (N_EDGES,), dtype=jnp.float32)
        s1 = 1.0 / np.sqrt(D_IN)
        s2 = 1.0 / np.sqrt(D_HID)
        params = {'W1': jax.random.normal(ks[3], (D_IN, D_HID), dtype=jnp.float32) * s1, 'b1': jnp.zeros((D_HID,), dtype=jnp.float32), 'a1': jnp.full((D_HID,), 0.25, dtype=jnp.float32), 'W2': jax.random.normal(ks[4], (D_HID, D_HID), dtype=jnp.float32) * s2, 'b2': jnp.zeros((D_HID,), dtype=jnp.float32), 'a2': jnp.full((D_HID,), 0.25, dtype=jnp.float32), 'W3': jax.random.normal(ks[5], (D_HID, D_HID), dtype=jnp.float32) * s2, 'b3': jnp.zeros((D_HID,), dtype=jnp.float32), 'a3': jnp.full((D_HID,), 0.25, dtype=jnp.float32)}
        return {'x': x, 'edge_index': edge_index, 'edge_weight': edge_weight, **params}
    _L1_gnn_all = _L1_gnn_setup()
    _L1_gnn_in = {k: v for k, v in _L1_gnn_all.items() if k in ('W1', 'b1', 'a1', 'W2', 'b2', 'a2', 'W3', 'b3', 'a3')}
    del _L1_gnn_all

    def _L2_gnn_setup():
        import jax, jax.numpy as jnp
        import numpy as np
        N_NODES = 3125
        N_EDGES = 50000
        F_IN = 128
        HID = 128

        def _gcn_conv(h, W, b, row, col, num_nodes, dinv):
            hw = h @ W
            norm = dinv[row] * dinv[col]
            msg = hw[row] * norm[:, None]
            out = jax.ops.segment_sum(msg, col, num_segments=num_nodes)
            return out + b
        key = jax.random.key(seed)
        ks = jax.random.split(key, 8)
        x = jax.random.normal(ks[0], (N_NODES, F_IN), dtype=jnp.float32)
        edge_index = jax.random.randint(ks[1], (2, N_EDGES), 0, N_NODES, dtype=jnp.int32)

        def glorot(k, fan_in, fan_out):
            s = jnp.sqrt(6.0 / (fan_in + fan_out))
            return jax.random.uniform(k, (fan_in, fan_out), jnp.float32, -s, s)
        W0 = glorot(ks[2], F_IN, HID)
        W1 = glorot(ks[3], HID, HID)
        W2 = glorot(ks[4], HID, HID)
        b0 = jnp.zeros((HID,), jnp.float32)
        b1 = jnp.zeros((HID,), jnp.float32)
        b2 = jnp.zeros((HID,), jnp.float32)
        return {'x': x, 'edge_index': edge_index, 'W0': W0, 'b0': b0, 'W1': W1, 'b1': b1, 'W2': W2, 'b2': b2}
    _L2_gnn_all = _L2_gnn_setup()
    _L2_gnn_in = {k: v for k, v in _L2_gnn_all.items() if k in ('W0', 'b0', 'W1', 'b1', 'W2', 'b2')}
    del _L2_gnn_all

    def _L3_gnn_setup():
        import jax, jax.numpy as jnp
        import numpy as np
        N = 6250
        E = 200000
        D = 128
        K = 3
        key = jax.random.key(seed)
        k1, k2, k3, k4, k5 = jax.random.split(key, 5)
        x = jax.random.normal(k1, (N, D), dtype=jnp.float32)
        edge_row = jax.random.randint(k2, (E,), 0, N, dtype=jnp.int32)
        edge_col = jax.random.randint(k3, (E,), 0, N, dtype=jnp.int32)
        edge_val = jax.random.uniform(k4, (E,), dtype=jnp.float32)
        alpha_logits = jax.random.normal(k5, (K + 1,), dtype=jnp.float32)
        return {'x': x, 'edge_row': edge_row, 'edge_col': edge_col, 'edge_val': edge_val, 'alpha_logits': alpha_logits}
    _L3_gnn_all = _L3_gnn_setup()
    _L3_gnn_in = {k: v for k, v in _L3_gnn_all.items() if k in ('alpha_logits',)}
    del _L3_gnn_all
    return {'x': x, 'src': src, 'dst': dst, 'edge_attr_64': edge_attr_64, 'edge_weight': edge_weight, 'L0_gnn_Wn': _L0_gnn_in['Wn'], 'L0_gnn_bn': _L0_gnn_in['bn'], 'L0_gnn_We1': _L0_gnn_in['We1'], 'L0_gnn_be1': _L0_gnn_in['be1'], 'L0_gnn_We2': _L0_gnn_in['We2'], 'L0_gnn_be2': _L0_gnn_in['be2'], 'L0_gnn_Wet': _L0_gnn_in['Wet'], 'L0_gnn_bet': _L0_gnn_in['bet'], 'L0_gnn_W1': _L0_gnn_in['W1'], 'L0_gnn_b1': _L0_gnn_in['b1'], 'L0_gnn_W2': _L0_gnn_in['W2'], 'L0_gnn_b2': _L0_gnn_in['b2'], 'L1_gnn_W1': _L1_gnn_in['W1'], 'L1_gnn_b1': _L1_gnn_in['b1'], 'L1_gnn_a1': _L1_gnn_in['a1'], 'L1_gnn_W2': _L1_gnn_in['W2'], 'L1_gnn_b2': _L1_gnn_in['b2'], 'L1_gnn_a2': _L1_gnn_in['a2'], 'L1_gnn_W3': _L1_gnn_in['W3'], 'L1_gnn_b3': _L1_gnn_in['b3'], 'L1_gnn_a3': _L1_gnn_in['a3'], 'L2_gnn_W0': _L2_gnn_in['W0'], 'L2_gnn_b0': _L2_gnn_in['b0'], 'L2_gnn_W1': _L2_gnn_in['W1'], 'L2_gnn_b1': _L2_gnn_in['b1'], 'L2_gnn_W2': _L2_gnn_in['W2'], 'L2_gnn_b2': _L2_gnn_in['b2'], 'L3_gnn_alpha_logits': _L3_gnn_in['alpha_logits']}

def reference(x, src, dst, edge_attr_64, edge_weight, L0_gnn_Wn, L0_gnn_bn, L0_gnn_We1, L0_gnn_be1, L0_gnn_We2, L0_gnn_be2, L0_gnn_Wet, L0_gnn_bet, L0_gnn_W1, L0_gnn_b1, L0_gnn_W2, L0_gnn_b2, L1_gnn_W1, L1_gnn_b1, L1_gnn_a1, L1_gnn_W2, L1_gnn_b2, L1_gnn_a2, L1_gnn_W3, L1_gnn_b3, L1_gnn_a3, L2_gnn_W0, L2_gnn_b0, L2_gnn_W1, L2_gnn_b1, L2_gnn_W2, L2_gnn_b2, L3_gnn_alpha_logits):
    import jax
    import jax.numpy as jnp

    def _L0_gnn_ref(node_feats, edge_feats, src, dst, Wn, bn, We1, be1, We2, be2, Wet, bet, W1, b1, W2, b2):
        import jax, jax.numpy as jnp
        import numpy as np
        N_NODES = 3125
        N_EDGES = 50000
        NODE_F = 128
        EDGE_F = 64
        GRAPH_F = 128

        def leaky_relu(x):
            return jax.nn.leaky_relu(x, negative_slope=0.01)

        def segment_softmax(logits, seg, num_segments):
            m = jax.ops.segment_max(logits, seg, num_segments=num_segments)
            m = jnp.where(jnp.isfinite(m), m, 0.0)
            ex = jnp.exp(logits - m[seg])
            s = jax.ops.segment_sum(ex, seg, num_segments=num_segments)
            return ex / s[seg]

        def _lin(key, fan_in, fan_out):
            k1, k2 = jax.random.split(key)
            bound = 1.0 / np.sqrt(fan_in)
            W = jax.random.uniform(k1, (fan_in, fan_out), minval=-bound, maxval=bound, dtype=jnp.float32)
            b = jax.random.uniform(k2, (fan_out,), minval=-bound, maxval=bound, dtype=jnp.float32)
            return (W, b)
        n = node_feats.shape[0]
        hv_new = leaky_relu(node_feats @ Wn + bn)
        he1 = leaky_relu(jnp.concatenate([node_feats[src], edge_feats], axis=1) @ We1 + be1)
        he2 = jnp.concatenate([hv_new[dst], he1], axis=1)
        logits = leaky_relu(he2 @ We2 + be2)
        a = segment_softmax(logits, dst, n)
        e = a * (he1 @ Wet + bet)
        c = jax.ops.segment_sum(e, dst, num_segments=n)
        context = jax.nn.elu(c)
        h = jnp.concatenate([context, hv_new], axis=1) @ W1 + b1
        h = jax.nn.relu(h) @ W2 + b2
        return jax.nn.relu(h)

    def _L1_gnn_ref(x, edge_index, edge_weight, W1, b1, a1, W2, b2, a2, W3, b3, a3):
        import jax, jax.numpy as jnp
        import numpy as np
        N_NODES = 6250
        N_EDGES = 100000
        D_IN = 128
        D_HID = 128

        def gcn_layer(x, src, dst, ew, W, b, n):
            h = x @ W
            deg = jax.ops.segment_sum(ew, dst, num_segments=n) + 1.0
            dis = jnp.where(deg > 0, jax.lax.rsqrt(deg), 0.0)
            norm = dis[src] * ew * dis[dst]
            agg = jax.ops.segment_sum(norm[:, None] * h[src], dst, num_segments=n)
            agg = agg + (dis * dis)[:, None] * h
            return agg + b

        def prelu(x, alpha):
            return jnp.where(x >= 0, x, alpha * x)
        src, dst = (edge_index[0], edge_index[1])
        n = x.shape[0]
        h = prelu(gcn_layer(x, src, dst, edge_weight, W1, b1, n), a1)
        h = prelu(gcn_layer(h, src, dst, edge_weight, W2, b2, n), a2)
        h = prelu(gcn_layer(h, src, dst, edge_weight, W3, b3, n), a3)
        return h

    def _L2_gnn_ref(x, edge_index, W0, b0, W1, b1, W2, b2):
        import jax, jax.numpy as jnp
        import numpy as np
        N_NODES = 3125
        N_EDGES = 50000
        F_IN = 128
        HID = 128

        def _gcn_conv(h, W, b, row, col, num_nodes, dinv):
            hw = h @ W
            norm = dinv[row] * dinv[col]
            msg = hw[row] * norm[:, None]
            out = jax.ops.segment_sum(msg, col, num_segments=num_nodes)
            return out + b
        n = x.shape[0]
        loops = jnp.arange(n, dtype=edge_index.dtype)
        row = jnp.concatenate([edge_index[0], loops])
        col = jnp.concatenate([edge_index[1], loops])
        deg = jax.ops.segment_sum(jnp.ones_like(col, dtype=x.dtype), col, num_segments=n)
        dinv = jnp.where(deg > 0, jax.lax.rsqrt(deg), 0.0)
        h = jax.nn.relu(_gcn_conv(x, W0, b0, row, col, n, dinv))
        for W, b in ((W1, b1), (W2, b2)):
            h = jax.nn.relu(_gcn_conv(h, W, b, row, col, n, dinv))
        return h

    def _L3_gnn_ref(x, edge_row, edge_col, edge_val, alpha_logits):
        import jax, jax.numpy as jnp
        import numpy as np
        N = 6250
        E = 200000
        D = 128
        K = 3
        n = x.shape[0]
        alpha = jax.nn.softmax(alpha_logits)

        def spmm(X):
            return jax.ops.segment_sum(edge_val[:, None] * X[edge_col], edge_row, num_segments=n)
        Yk = x
        Y = alpha[0] * Yk
        for k in range(1, alpha.shape[0]):
            Yk = spmm(Yk)
            Y = Y + alpha[k] * Yk
        return Y
    edge_index = jnp.stack([src, dst])
    h = jnp.maximum(_layernorm(x, axis=-1), 0.0)
    x = x + _L0_gnn_ref(h, edge_attr_64, src, dst, L0_gnn_Wn, L0_gnn_bn, L0_gnn_We1, L0_gnn_be1, L0_gnn_We2, L0_gnn_be2, L0_gnn_Wet, L0_gnn_bet, L0_gnn_W1, L0_gnn_b1, L0_gnn_W2, L0_gnn_b2)
    h = jnp.maximum(_layernorm(x, axis=-1), 0.0)
    x = x + _L1_gnn_ref(h, edge_index, edge_weight, L1_gnn_W1, L1_gnn_b1, L1_gnn_a1, L1_gnn_W2, L1_gnn_b2, L1_gnn_a2, L1_gnn_W3, L1_gnn_b3, L1_gnn_a3)
    h = jnp.maximum(_layernorm(x, axis=-1), 0.0)
    x = x + _L2_gnn_ref(h, edge_index, L2_gnn_W0, L2_gnn_b0, L2_gnn_W1, L2_gnn_b1, L2_gnn_W2, L2_gnn_b2)
    h = jnp.maximum(_layernorm(x, axis=-1), 0.0)
    x = x + _L3_gnn_ref(h, src, dst, edge_weight, L3_gnn_alpha_logits)
    return x

_drawn_inputs = setup_inputs


def setup_inputs(seed=0):
    import zlib

    import numpy as np

    out = dict(_drawn_inputs(seed))
    spreads = {'L1_gnn_b1': (0.0, 0.8),
     'L1_gnn_a1': (0.25, 0.6),
     'L1_gnn_b2': (0.0, 0.8),
     'L1_gnn_a2': (0.25, 0.6),
     'L1_gnn_b3': (0.0, 0.8),
     'L1_gnn_a3': (0.25, 0.6),
     'L2_gnn_b0': (0.0, 0.8),
     'L2_gnn_b1': (0.0, 0.8),
     'L2_gnn_b2': (0.0, 0.8)}
    factors = {'edge_attr_64': 8.0,
     'L0_gnn_Wn': 9.995,
     'L0_gnn_bn': 56.901,
     'L0_gnn_We1': 6.183,
     'L0_gnn_be1': 29.181,
     'L0_gnn_We2': 8.0,
     'L0_gnn_Wet': 5.139,
     'L0_gnn_bet': 50.581,
     'L0_gnn_W1': 2.806,
     'L0_gnn_b1': 50.917,
     'x': 5.206,
     'L0_gnn_b2': 8.0,
     'L2_gnn_W0': 2.901,
     'L2_gnn_W1': 2.99}
    for name, (base, spread) in spreads.items():
        noise = np.random.default_rng([zlib.crc32(name.encode()), seed]).standard_normal(out[name].shape)
        drawn = base * np.exp(spread * noise) if base else spread * noise
        out[name] = jnp.asarray(drawn.astype(out[name].dtype))
    for name, factor in factors.items():
        out[name] = (out[name] * factor).astype(out[name].dtype)
    return out
```

```python
from contextlib import ExitStack

import numpy as np

import concourse.bass as bass
from concourse import mybir

F32 = mybir.dt.float32
BF16 = mybir.dt.bfloat16
I32 = mybir.dt.int32
ALU = mybir.AluOpType
ACT = mybir.ActivationFunctionType
AX_X = mybir.AxisListType.X

P = 128
N = 3125
E = 103125
EF = 64
NT = -(-N // P)
NP = NT * P
BANK = 512
CH = -(-E // BANK)
EP = CH * BANK
TPC = BANK // P
ET = EP // P
SEQ = EP // P
GROUPS = [(g * BANK, min(BANK, NP - g * BANK)) for g in range(-(-NP // BANK))]
DUMP = NP * NP
FAR = 1e30
EPS = 1e-5
SLOPE = 0.01

WEIGHTS = ["L0_gnn_Wn", "We1_node", "L0_gnn_Wet", "W1_context", "W1_node", "L0_gnn_W2",
           "L1_gnn_W1", "L1_gnn_W2", "L1_gnn_W3", "L2_gnn_W0", "L2_gnn_W1", "L2_gnn_W2"]
BIAS_COLUMNS = ["L0_gnn_bn", "L0_gnn_be1", "L0_gnn_b1", "We2_node", "We2_edge"]
BIAS_ROWS = ["L0_gnn_b2", "L1_gnn_b1", "L1_gnn_b2", "L1_gnn_b3", "L1_gnn_a1", "L1_gnn_a2", "L1_gnn_a3",
             "L2_gnn_b0", "L2_gnn_b1", "L2_gnn_b2"]


class Queue:

    def __init__(self, sem):
        self.sem, self.count, self.ops, self.seen = sem, 0, [], {}

    def wait(self, *after):
        for tok in after:
            if tok is None:
                continue
            if isinstance(tok, list):
                self.wait(*tok)
                continue
            sem, value = tok
            if self.seen.get(id(sem), 0) < value:
                self.seen[id(sem)] = value
                self.ops.append(lambda e, s=sem, v=value: e.wait_ge(s, v))

    def do(self, issue, *after, mark=True):
        self.wait(*after)
        if not mark:
            self.ops.append(issue)
            return None
        self.count += 1
        self.ops.append(lambda e: issue(e).then_inc(self.sem, 1))
        return (self.sem, self.count)

    def dma(self, arrival, out, in_, *after, **kw):
        self.wait(*after)
        arrival.value += 16
        self.ops.append(lambda e: e.dma_start(out, in_, **kw).then_inc(arrival.sem, 16))
        return (arrival.sem, arrival.value)

    def gather(self, arrival, out, table, index, *after):
        self.wait(*after)
        arrival.value += 16
        self.ops.append(lambda e: e.indirect_dma_start(
            out, None, table, bass.IndirectOffsetOnAxis(ap=index, axis=0)).then_inc(arrival.sem, 16))
        return (arrival.sem, arrival.value)

    def scatter(self, arrival, table, index, in_, *after, add=False):
        self.wait(*after)
        arrival.value += 16
        kw = dict(compute_op=ALU.add) if add else {}
        self.ops.append(lambda e: e.indirect_dma_start(
            table, bass.IndirectOffsetOnAxis(ap=index, axis=0), in_, None, **kw).then_inc(arrival.sem, 16))
        return (arrival.sem, arrival.value)

    def last(self):
        return (self.sem, self.count) if self.count else None


class Arrival:

    def __init__(self, sem):
        self.sem, self.value = sem, 0


class Slots:

    def __init__(self, buffers):
        self.buffers, self.free, self.at = buffers, [[] for _ in buffers], -1

    def take(self):
        self.at = (self.at + 1) % len(self.buffers)
        after, self.free[self.at] = self.free[self.at], []
        return self.buffers[self.at], self.free[self.at], after


def along(ap, n):
    return ap.unsqueeze(1).broadcast_to([ap.shape[0], n, ap.shape[1]])


def across(ap, n):
    return ap.unsqueeze(2).broadcast_to([ap.shape[0], ap.shape[1], n])


def build(nc, given, out):
    with ExitStack() as ctx:
        def sb(name, shape, dt=F32):
            return ctx.enter_context(nc.sbuf_tensor(name, shape, dt))

        def dram(name, shape, dt=F32):
            return nc.dram_tensor(name, shape, dt, kind="Internal").ap()

        def arrival(name):
            return Arrival(ctx.enter_context(nc.semaphore(name)))

        pe, act, dve, pool, sp = (Queue(ctx.enter_context(nc.semaphore(f"done_{n}")))
                                  for n in ("pe", "act", "dve", "pool", "sp"))
        bank = [ctx.enter_context(nc.psum_tensor(f"bank{i}", [P, BANK], F32)) for i in range(8)]
        bank_free = [[] for _ in bank]

        node_table = dram("node_table", [NP, P])
        he_d = dram("he_d", [CH, P, BANK])
        z_d = dram("z_d", [EP, 1])
        key_d = dram("key_d", [EP])
        zmax_d = dram("zmax_d", [EP, 1])
        begin_d = dram("begin_d", [EP + NP, 2])
        ex_d = dram("ex_d", [EP])
        keep_d = dram("keep_d", [EP], BF16)
        exsum_d = dram("exsum_d", [EP, 1])
        hesum_d = dram("hesum_d", [EP, P])
        adj = dram("adj", [NP * NP + EP, 2])
        weight_t = dram("weight_t", [NP, NP])
        count_t = dram("count_t", [NP, NP])
        weight_n = dram("weight_n", [NP, NP])

        ident = sb("ident", [P, P])
        tri_incl = sb("tri_incl", [P, P])
        tri_less = sb("tri_less", [P, P])
        ones = sb("ones", [P, P])
        ones_bf = sb("ones_bf", [1, P], BF16)
        iota_i = sb("iota_i", [P, P], I32)
        iota_f = sb("iota_f", [P, P])
        eps_col = sb("eps_col", [P, 1])
        W = {n: sb(n, [P, P]) for n in WEIGHTS}
        We1_edge = sb("We1_edge", [EF, P])
        col = {n: sb("c_" + n, [P, 1]) for n in BIAS_COLUMNS}
        row = {n: sb("r_" + n, [P, P]) for n in BIAS_ROWS}
        be2_col = sb("be2_col", [P, 1])
        bet_row = sb("bet_row", [1, P])
        alpha = sb("alpha", [P, 4])
        x = sb("x", [P, NT, P])
        h = sb("h", [P, NT, P])
        featT = sb("featT", [P, NP])
        hvT = sb("hvT", [P, NP])
        stats = sb("stats", [P, NT, 6])
        moments = sb("moments", [P, NT, 2])
        rstd = sb("rstd", [P, NT])
        shift = sb("shift", [P, NT])
        dis = sb("dis", [P, NT])
        dinv = sb("dinv", [P, NT])
        has = sb("has", [P, NT])
        small = sb("small", [P, 8, NT])
        end_i = sb("end_i", [P, NT], I32)
        begin_i = sb("begin_i", [P, NT], I32)
        work = sb("work", [P, 2, BANK])

        ARENA = 26500
        arena = sb("arena", [P, ARENA])
        used = [0]

        def carve(n):
            used[0] += n
            assert used[0] <= ARENA, used[0]
            return arena[:, used[0] - n:used[0]]

        src_c = carve(ET).bitcast(I32)
        dst_c = carve(ET).bitcast(I32)
        w1_c = carve(2 * ET).rearrange("p (t c) -> p t c", c=2)
        key_c = carve(ET)
        lo_c = carve(ET)
        hi_c = carve(ET)
        later_c = carve(ET)
        pair_c = carve(2 * ET).rearrange("p (t c) -> p t c", c=2)
        target = carve(ET).bitcast(I32)
        z_c = carve(ET)
        z_t = carve(7 * P).rearrange("p (g e) -> p g e", e=P)
        dst_s = carve(SEQ).bitcast(I32)
        prev_s = carve(SEQ).bitcast(I32)
        keep_s = carve(SEQ)
        reset_s = carve(SEQ)
        a_s = carve(SEQ)
        b_s = carve(SEQ)
        z_s = carve(SEQ)
        tl_s = carve(2 * SEQ).rearrange("p (t c) -> p t c", c=2)
        keep_bf = carve(SEQ // 2).bitcast(BF16)
        EDGE_COLS = 1024
        edge_space = carve(2 * EDGE_COLS)
        edge_in = Slots([edge_space[0:EF, i * EDGE_COLS:(i + 1) * EDGE_COLS] for i in range(2)])
        key_row = Slots([carve(EDGE_COLS)[0:1, :] for _ in range(2)])

        gath = Slots([sb(f"gath{i}", [P, TPC, P]) for i in range(3)])
        he = Slots([sb(f"he{i}", [P, BANK]) for i in range(3)])
        onehot = Slots([carve(BANK).rearrange("p (a b) -> p a b", b=P) for _ in range(2)])
        tile_hot = Slots([carve(TPC * 2 * NT).rearrange("p (a c b) -> p a c b", c=2, b=NT) for _ in range(2)])
        same = Slots([carve(P) for _ in range(4)])
        rows1 = sb("rows1", [1, 2 * P])
        carry_row = sb("carry_row", [1, P + 1])
        carry_col = sb("carry_col", [P, 1])
        ends = sb("ends", [P, 2])
        flag_row = sb("flag_row", [1, 3, ET])
        flag_f = sb("flag_f", [1, 1])
        flag_i = sb("flag_i", [1, 1], I32)
        node_iota = sb("node_iota", [P, NT], I32)

        loaded = {}

        def load(name, dst_ap, src_ap, q=None, **kw):
            loaded[name] = (q or sp).dma(arrival("ld_" + name), dst_ap, src_ap, **kw)
            return loaded[name]

        in_x = load("x", x[:, :, :], given["x"].rearrange("(t p) f -> p t f", p=P))
        load("src_c", src_c, given["src_c"])
        load("dst_c", dst_c, given["dst_c"])
        load("w1_c", w1_c, given["w1_c"].rearrange("p (t c) -> p t c", c=2))
        small_load = arrival("ld_small")
        for n in WEIGHTS:
            tok_small = act.dma(small_load, W[n][:, :], given[n])
        act.dma(small_load, We1_edge[:, :], given["We1_edge"])
        for n in BIAS_COLUMNS:
            act.dma(small_load, col[n][:, :], given[n])
        for n in BIAS_ROWS:
            act.dma(small_load, row[n][:, :], given[n].broadcast_to([P, P]))
        act.dma(small_load, be2_col[:, :], given["L0_gnn_be2"].broadcast_to([P, 1]))
        act.dma(small_load, bet_row[:, :], given["L0_gnn_bet"])
        tok_small = act.dma(small_load, alpha[:, :], given["L3_gnn_alpha_logits"].broadcast_to([P, 4]))
        load("dst_s", dst_s, given["dst"][1:EP + 1].rearrange("(p c) -> p c", p=P))
        load("prev_s", prev_s, given["dst"][0:EP].rearrange("(p c) -> p c", p=P))

        c0 = pool.do(lambda e: e.memset(ident[:, :], 0.0))
        c_ones = pool.do(lambda e: e.memset(ones[:, :], 1.0))
        c1 = pool.do(lambda e: e.affine_select(out=ident[:, :], in_=ident[:, :], compare_op=ALU.not_equal, fill=1.0,
                                               base=0, pattern=[[-1, P]], channel_multiplier=1), c0, c_ones)
        pool.do(lambda e: e.affine_select(out=tri_incl[:, :], in_=ones[:, :], compare_op=ALU.is_ge, fill=0.0,
                                          base=0, pattern=[[1, P]], channel_multiplier=-1))
        pool.do(lambda e: e.affine_select(out=tri_less[:, :], in_=ones[:, :], compare_op=ALU.is_gt, fill=0.0,
                                          base=0, pattern=[[1, P]], channel_multiplier=-1))
        pool.do(lambda e: e.iota(iota_i[:, :], pattern=[[1, P]], base=0, channel_multiplier=0))
        consts = pool.do(lambda e: e.iota(node_iota[:, :], pattern=[[P, NT]], base=EP, channel_multiplier=1))
        dve.do(lambda e: e.tensor_copy(iota_f[:, :], iota_i[:, :]), consts)
        dve.do(lambda e: e.memset(ones_bf[:, :], 1.0))
        v_consts = dve.do(lambda e: e.memset(eps_col[:, :], EPS))

        ZC = 6400
        zeros = carve(ZC // 4)
        z0 = dve.do(lambda e: e.memset(zeros[:, :], 0.0))
        cleared = arrival("cleared")
        adj_flat = adj.rearrange("n c -> (n c)")
        for i in range(4 * NT):
            span = P * ZC // 4
            tok_adj0 = sp.dma(cleared, adj_flat[i * span:(i + 1) * span].rearrange("(p k) -> p k", p=P), zeros[:, :], z0)
        tok_adj0 = sp.dma(cleared, adj[DUMP:DUMP + EP, :].rearrange("(p k) c -> p (k c)", p=P), zeros[:, 0:2 * SEQ], z0) \
            if 2 * SEQ <= ZC // 4 else None
        if tok_adj0 is None:
            for c in range(2):
                tok_adj0 = sp.dma(cleared, adj_flat[2 * DUMP + c * EP:2 * DUMP + (c + 1) * EP].rearrange("(p k) -> p k", p=P),
                                  zeros[:, 0:SEQ], z0)
        begin_flat = begin_d.rearrange("n c -> (n c)")
        begin0 = arrival("begin0")
        for c in range(2):
            tok_begin0 = sp.dma(begin0, begin_flat[c * EP:(c + 1) * EP].rearrange("(p k) -> p k", p=P), zeros[:, 0:SEQ], z0)

        def layernorm(after_x, after_h):
            for t in range(NT):
                a = dve.do(lambda e, t=t: e.bn_stats(stats[:, t, :], x[:, t, :]), after_x)
            for t in range(NT):
                b = dve.do(lambda e, t=t: e.bn_aggr(moments[:, t, :], stats[:, t, :]), a)
            s = act.do(lambda e: e.activation(rstd[:, :], moments[:, :, 1], ACT.Sqrt, bias=eps_col[:, 0:1]), b, v_consts)
            r = dve.do(lambda e: e.reciprocal(rstd[:, :], rstd[:, :]), s)
            m = dve.do(lambda e: e.scalar_tensor_tensor(out=shift[:, :], in0=moments[:, :, 0], scalar=-1.0,
                                                        in1=rstd[:, :], op0=ALU.mult, op1=ALU.mult), r)
            for t in range(NT):
                o = act.do(lambda e, t=t: e.activation(h[:, t, :], x[:, t, :], ACT.Relu, bias=shift[:, t:t + 1],
                                                       scale=rstd[:, t:t + 1]), m, after_h)
            return o

        def leaky(ap, *after):
            return dve.do(lambda e: e.scalar_tensor_tensor(out=ap, in0=ap, scalar=SLOPE, in1=ap, op0=ALU.mult, op1=ALU.max),
                          *after)

        def flip(out_ap, in_ap, *after, mark=False):
            k = in_ap.shape[0]
            return pe.do(lambda e: e.transpose(out_ap, in_ap, ident[0:k, 0:k]), consts, *after, mark=mark)

        h_ok = layernorm([in_x], [])
        for g, (c, w) in enumerate(GROUPS):
            b = g % 2
            for j in range(w // P):
                t = flip(bank[b][:, j * P:(j + 1) * P], h[:, c // P + j, :], h_ok, bank_free[b], mark=(j == w // P - 1))
            hT_ok = act.do(lambda e, b=b, c=c, w=w: e.copy(featT[:, c:c + w], bank[b][:, 0:w]), t)
            bank_free[b] = [hT_ok]
        table_st = [arrival(f"table_st{i}") for i in range(2)]
        gslot = Slots([he.buffers[0], he.buffers[1]])
        for g, (c, w) in enumerate(GROUPS):
            b = 2 + g % 2
            for j in range(w // P):
                t = pe.do(lambda e, b=b, j=j, c=c: e.matmul(bank[b][:, j * P:(j + 1) * P], featT[:, c + j * P:c + (j + 1) * P],
                                                            W["We1_node"][:, :], start=True, stop=True),
                          hT_ok, tok_small, bank_free[b], mark=(j == w // P - 1))
            buf, free, after = gslot.take()
            s = dve.do(lambda e, b=b, w=w, buf=buf: e.tensor_copy(buf[:, 0:w], bank[b][:, 0:w]), t, after)
            bank_free[b] = [s]
            free.append(sp.dma(table_st[g % 2], node_table[c:c + w, :].rearrange("(j p) f -> p j f", p=P),
                               buf[:, 0:w].rearrange("p (j f) -> p j f", f=P), s))
        table_ok = [(s.sem, s.value) for s in table_st]
        he.free[0], he.free[1] = [table_ok], [table_ok]
        for g, (c, w) in enumerate(GROUPS):
            b = 4 + g % 2
            t = pe.do(lambda e, b=b, c=c, w=w: e.matmul(bank[b][:, 0:w], W["L0_gnn_Wn"][:, :], featT[:, c:c + w],
                                                        start=True, stop=True), bank_free[b])
            a = act.do(lambda e, b=b, c=c, w=w: e.activation(hvT[:, c:c + w], bank[b][:, 0:w], ACT.Identity,
                                                             bias=col["L0_gnn_bn"][:, 0:1]), t, tok_small)
            bank_free[b] = [a]
            hv_ok = leaky(hvT[:, c:c + w], a)
        t_node = small[:, 0, :]
        for i in range(NT):
            t = pe.do(lambda e, i=i: e.matmul(bank[6][:, i:i + 1], hvT[:, i * P:(i + 1) * P], col["We2_node"][:, 0:1],
                                              start=True, stop=True), hv_ok, mark=(i == NT - 1))
        tn_ok = dve.do(lambda e: e.tensor_scalar(t_node, bank[6][:, 0:NT], be2_col[:, 0:1], None, ALU.add), t, tok_small)
        bank_free[6] = [tn_ok]

        gather_ok, gather_sem = [], [arrival(f"gath{i}") for i in range(3)]

        for n, a in (("src_c", src_c), ("dst_c", dst_c)):
            pass
        kf = dve.do(lambda e: e.tensor_copy(hi_c, dst_c), loaded["dst_c"])
        sf = dve.do(lambda e: e.tensor_copy(lo_c, src_c), loaded["src_c"])
        key_ok = dve.do(lambda e: e.scalar_tensor_tensor(out=key_c, in0=lo_c, scalar=float(NP), in1=hi_c,
                                                         op0=ALU.mult, op1=ALU.add), kf, sf)
        lo_i = later_c.bitcast(I32)
        a = dve.do(lambda e: e.tensor_scalar(lo_i, dst_c, P - 1, None, ALU.bitwise_and))
        b_ = dve.do(lambda e: e.tensor_copy(lo_c, lo_i), a, key_ok)
        a = dve.do(lambda e: e.tensor_scalar(lo_i, dst_c, 7, None, ALU.arith_shift_right), b_)
        hilo_ok = dve.do(lambda e: e.tensor_copy(hi_c, lo_i), a)
        seq_st = arrival("seq_st")

        def to_edge_order(c_ap, table, after, store):
            done = None
            for g in range(-(-ET // P)):
                w = min(P, ET - g * P)
                b = 7
                t = flip(bank[b][0:w, 0:P], c_ap[:, g * P:g * P + w], after, bank_free[b], mark=True)
                s = dve.do(lambda e, g=g, w=w: e.tensor_copy(z_t[0:w, g, :], bank[7][0:w, 0:P]), t, seq_done)
                bank_free[b] = [s]
            full = ET // P
            sp.dma(store, table[0:full * P * P].rearrange("(g p e) -> p g e", p=P, e=P), z_t[:, 0:full, :], s)
            return sp.dma(store, table[full * P * P:EP].rearrange("(p e) -> p e", e=P), z_t[0:ET - full * P, full, :], s)

        seq_done = []
        keyd_ok = to_edge_order(key_c, key_d, key_ok, seq_st)
        seq_done = [keyd_ok]

        edge_sem = [arrival(f"edge{i}") for i in range(2)]
        keyrow_sem = [arrival(f"keyrow{i}") for i in range(2)]
        he_st = [arrival(f"he_st{i}") for i in range(3)]
        big = {}
        LOADC = EDGE_COLS // BANK

        def load_edges(k):
            c = k * EDGE_COLS
            w = min(EDGE_COLS, EP - c)
            buf, free, after = edge_in.take()
            t1 = sp.dma(edge_sem[k % 2], buf[:, 0:w], given["edgeT"][:, c:c + w], after)
            rbuf, rfree, rafter = key_row.take()
            t2 = sp.dma(keyrow_sem[k % 2], rbuf[:, 0:w], key_d[c:c + w].unsqueeze(0), rafter, keyd_ok)
            big[k] = (buf, free, t1, rbuf, rfree, t2)

        def gathers(c):
            buf, free, after = gath.take()
            for j in range(TPC):
                t = pool.gather(gather_sem[c % 3], buf[:, j, :], node_table, src_c[:, c * TPC + j:c * TPC + j + 1],
                                after, table_ok, loaded["src_c"])
            gather_ok.append((buf, free, t))

        NBIG = -(-EP // EDGE_COLS)
        load_edges(0)
        load_edges(1)
        for c in range(3):
            gathers(c)
        w1_ok = loaded["w1_c"]
        merged = Slots([bank[7][:, i * P:(i + 1) * P] for i in range(4)])
        for f in merged.free:
            f.extend(bank_free[7])
        MT = 16
        he_stored = None
        for c in range(CH):
            k = c // LOADC
            if c % LOADC == 0 and 0 < k and k + 1 < NBIG:
                load_edges(k + 1)
            ebuf, efree, e_ok, rbuf, rfree, r_ok = big[k]
            eo = (c % LOADC) * BANK
            b = c % 2
            gbuf, gfree, g_ok = gather_ok[c]
            t0 = pe.do(lambda e, b=b, ebuf=ebuf, eo=eo: e.matmul(bank[b][:, :], We1_edge[:, :], ebuf[:, eo:eo + BANK],
                                                                 start=True, stop=False),
                       e_ok, tok_small, bank_free[b])
            for j in range(TPC):
                t = pe.do(lambda e, b=b, j=j, gbuf=gbuf: e.matmul(bank[b][:, j * P:(j + 1) * P], gbuf[:, j, :], ident[:, :],
                                                                  start=False, stop=(j == TPC - 1)),
                          g_ok, mark=(j == TPC - 1))
            gfree.append(t)
            efree[:] = [t]
            hbuf, hfree, hafter = he.take()
            a = act.do(lambda e, b=b, hbuf=hbuf: e.activation(hbuf[:, :], bank[b][:, :], ACT.Identity,
                                                              bias=col["L0_gnn_be1"][:, 0:1]), t, hafter)
            bank_free[b] = [a]
            he_ok = leaky(hbuf[:, :], a)
            hfree.append(act.dma(he_st[c % 3], he_d[c], hbuf[:, :], he_ok))
            kb = 5 + c % 2
            t = pe.do(lambda e, kb=kb, rbuf=rbuf, eo=eo: e.matmul(bank[kb][:, :], ones[0:1, :], rbuf[0:1, eo:eo + BANK],
                                                                  start=True, stop=True), r_ok, bank_free[kb])
            rfree[:] = [t]
            if c % 4 == 0:
                mcols, mfree, mafter = merged.take()
            for j in range(TPC):
                i = c * TPC + j
                sbuf, sfree, safter = same.take()
                u = dve.do(lambda e, kb=kb, j=j, i=i, sbuf=sbuf: e.scalar_tensor_tensor(
                    out=sbuf[:, :], in0=bank[kb][:, j * P:(j + 1) * P], scalar=key_c[:, i:i + 1], in1=tri_incl[:, :],
                    op0=ALU.is_equal, op1=ALU.mult, accum_out=later_c[:, i:i + 1]), t, safter, hilo_ok)
                q = (c % 4) * 2 * TPC + 2 * j
                m = pe.do(lambda e, sbuf=sbuf, mcols=mcols, q=q, i=i: e.matmul(mcols[:, q:q + 2], sbuf[:, :], w1_c[:, i, :],
                                                                               start=True, stop=True), u, w1_ok, mafter)
                sfree.append(m)
            bank_free[kb] = [u]
            if c % 4 == 3 or c == CH - 1:
                i0, ni = (c // 4) * 4 * TPC, (c % 4 + 1) * TPC
                pair_ok = dve.do(lambda e, mcols=mcols, i0=i0, ni=ni: e.tensor_copy(
                    pair_c[:, i0:i0 + ni, :], mcols[:, 0:2 * ni].rearrange("p (t c) -> p t c", c=2)), m)
                mfree.append(pair_ok)
            obuf, ofree, oafter = onehot.take()
            tbuf, tfree, tafter = tile_hot.take()
            i0 = c * TPC
            o1 = dve.do(lambda e, obuf=obuf, i0=i0: e.tensor_tensor(obuf[:, :, :], along(iota_f[:, :], TPC),
                                                                    across(lo_c[:, i0:i0 + TPC], P), ALU.is_equal),
                        oafter, hilo_ok, v_consts)
            o2 = dve.do(lambda e, tbuf=tbuf, i0=i0: e.tensor_tensor(tbuf[:, :, 0, :], along(iota_f[:, 0:NT], TPC),
                                                                    across(hi_c[:, i0:i0 + TPC], NT), ALU.is_equal), tafter)
            o3 = dve.do(lambda e, tbuf=tbuf, i0=i0: e.tensor_tensor(tbuf[:, :, 1, :], tbuf[:, :, 0, :],
                                                                    across(w1_c[:, i0:i0 + TPC, 0], NT), ALU.mult), o2, w1_ok)
            for j in range(TPC):
                d = pe.do(lambda e, obuf=obuf, tbuf=tbuf, j=j, c=c: e.matmul(
                    bank[4][:, 0:2 * NT], obuf[:, j, :], tbuf[:, j, :, :].rearrange("p a b -> p (a b)"),
                    start=(c == 0 and j == 0), stop=(c == CH - 1 and j == TPC - 1)), o1, o3, bank_free[4] if c == 0 else None,
                    mark=(j == TPC - 1))
            ofree.append(d)
            tfree.append(d)
            for j in range(TPC):
                i = c * TPC + j
                zb = 2 + i // BANK
                zt = pe.do(lambda e, hbuf=hbuf, j=j, i=i, zb=zb: e.matmul(
                    bank[zb][:, i % BANK:i % BANK + 1], hbuf[:, j * P:(j + 1) * P], col["We2_edge"][:, 0:1],
                    start=True, stop=True), he_ok, bank_free[zb] if i % BANK == 0 else None, mark=(j == TPC - 1))
            hfree.append(zt)
            if c + 3 < CH:
                gathers(c + 3)
        for zb in range(2):
            w = min(BANK, ET - zb * BANK)
            zc_ok = dve.do(lambda e, zb=zb, w=w: e.tensor_copy(z_c[:, zb * BANK:zb * BANK + w], bank[2 + zb][:, 0:w]), zt)
            bank_free[2 + zb] = [zc_ok]
        bank_free[7] = [pair_ok]
        zd_ok = to_edge_order(z_c, z_d.rearrange("e c -> (e c)"), zc_ok, seq_st)
        zs_ld = arrival("zs_ld")
        zs_ok = sp.dma(zs_ld, z_s, z_d.rearrange("(p c) o -> p (c o)", p=P), zd_ok)

        cnt, wdeg, tot, pre = small[:, 1, :], small[:, 2, :], small[:, 3, :], small[:, 4, :]
        s1 = dve.do(lambda e: e.tensor_copy(cnt, bank[4][:, 0:NT]), d)
        s2 = dve.do(lambda e: e.tensor_scalar(wdeg, bank[4][:, NT:2 * NT], 1.0, None, ALU.add))
        bank_free[4] = [s2]
        t = pe.do(lambda e: e.matmul(bank[4][:, 0:NT], ones[:, :], cnt, start=True, stop=True), s1, s2)
        t2 = pe.do(lambda e: e.matmul(bank[4][:, NT:2 * NT], tri_less[:, :], cnt, start=True, stop=True))
        s3 = dve.do(lambda e: e.tensor_copy(tot, bank[4][:, 0:NT]), t2)
        s4 = dve.do(lambda e: e.tensor_copy(pre, bank[4][:, NT:2 * NT]))
        bank_free[4] = [s4]
        inc, w5, w6 = small[:, 5, :], small[:, 6, :], small[:, 7, :]
        s5 = dve.do(lambda e: e.tensor_tensor_scan(inc, ones[:, 0:NT], tot, 0.0, ALU.mult, ALU.add), s3)
        s6 = dve.do(lambda e: e.tensor_tensor(inc, inc, tot, ALU.subtract), s5)
        s7 = dve.do(lambda e: e.tensor_tensor(inc, inc, pre, ALU.add), s6, s4)
        s8 = dve.do(lambda e: e.tensor_scalar(has[:, :], cnt, 0.0, None, ALU.is_gt), s1)
        s9 = dve.do(lambda e: e.tensor_tensor(w5, inc, cnt, ALU.add), s7)
        s10 = dve.do(lambda e: e.tensor_scalar(w5, w5, -1.0, 0.0, ALU.add, ALU.max), s9)
        end_ok = dve.do(lambda e: e.tensor_copy(end_i[:, :], w5), s10)
        s11 = dve.do(lambda e: e.tensor_copy(w6, node_iota[:, :]), consts)
        s12 = dve.do(lambda e: e.tensor_tensor(inc, inc, w6, ALU.subtract), s11, s9)
        s13 = dve.do(lambda e: e.tensor_tensor(inc, inc, has[:, :], ALU.mult), s12, s8)
        s14 = dve.do(lambda e: e.tensor_tensor(inc, inc, w6, ALU.add), s13)
        begin_ok = dve.do(lambda e: e.tensor_copy(begin_i[:, :], inc), s14)
        s15 = dve.do(lambda e: e.tensor_scalar(dinv[:, :], cnt, 1.0, None, ALU.add), s14)
        s16 = dve.do(lambda e: e.tensor_scalar(w5, wdeg, 0.0, None, ALU.is_gt), s2, end_ok)
        s17 = dve.do(lambda e: e.tensor_scalar(wdeg, wdeg, 1e-30, None, ALU.max), s16)
        s18 = act.do(lambda e: e.activation(dinv[:, :], dinv[:, :], ACT.Sqrt), s15)
        s19 = act.do(lambda e: e.activation(wdeg, wdeg, ACT.Sqrt), s17)
        s20 = dve.do(lambda e: e.reciprocal(dinv[:, :], dinv[:, :]), s18)
        s21 = dve.do(lambda e: e.reciprocal(dis[:, :], wdeg), s19)
        dis_ok = dve.do(lambda e: e.tensor_tensor(dis[:, :], dis[:, :], w5, ALU.mult), s21)

        dump_i = z_t.rearrange("p g e -> p (g e)")[:, 0:ET].bitcast(I32)
        dump_f = lo_c
        q0 = pool.do(lambda e: e.iota(dump_i, pattern=[[P, ET]], base=DUMP, channel_multiplier=1), zd_ok)
        q1 = dve.do(lambda e: e.tensor_copy(dump_f, dump_i), q0, o1)
        q2 = dve.do(lambda e: e.tensor_scalar(later_c, later_c, 1.0, None, ALU.is_equal), u)
        q3 = dve.do(lambda e: e.tensor_tensor(key_c, key_c, dump_f, ALU.subtract), q1)
        q4 = dve.do(lambda e: e.tensor_tensor(key_c, key_c, later_c, ALU.mult), q2, q3)
        q5 = dve.do(lambda e: e.tensor_tensor(key_c, key_c, dump_f, ALU.add), q4)
        target_ok = dve.do(lambda e: e.tensor_copy(target, key_c), q5)
        fl = arrival("fl")
        dst0 = given["dst"][1:EP + 1].rearrange("(t p) -> t p", p=P)
        fi = flag_row[:, 2, :].bitcast(I32)
        pc = Arrival(seq_st.sem)
        f1 = sp.dma(fl, flag_row[:, 0, :].bitcast(I32), given["tile_first"])
        f1 = sp.dma(fl, flag_row[:, 1, :].bitcast(I32), given["tile_last"])
        f2 = dve.do(lambda e: e.tensor_copy(flag_row[:, 2, :], flag_row[:, 0, :].bitcast(I32)), f1)
        f3 = dve.do(lambda e: e.tensor_copy(flag_row[:, 0, :], flag_row[:, 1, :].bitcast(I32)), f2)
        f4 = dve.do(lambda e: e.tensor_tensor(flag_row[:, 1, 0:ET - 2], flag_row[:, 0, 0:ET - 2], flag_row[:, 2, 2:ET],
                                              ALU.is_equal), f3)
        f5 = dve.do(lambda e: e.tensor_reduce(flag_f[:, :], flag_row[:, 1, 0:ET - 2], AX_X, ALU.max), f4)
        flag_ok = dve.do(lambda e: e.tensor_copy(flag_i[:, :], flag_f[:, :]), f5)

        k0 = dve.do(lambda e: e.tensor_copy(a_s, dst_s), loaded["dst_s"])
        k1 = dve.do(lambda e: e.tensor_copy(b_s, prev_s), loaded["prev_s"])
        k2 = dve.do(lambda e: e.tensor_tensor(keep_s, a_s, b_s, ALU.is_equal), k0, k1)
        k3 = dve.do(lambda e: e.tensor_copy(keep_bf, keep_s), k2)
        keepst = arrival("keepst")
        keepd_ok = sp.dma(keepst, keep_d.rearrange("(p c) -> p c", p=P), keep_bf, k3)
        k4 = dve.do(lambda e: e.tensor_scalar(reset_s, keep_s, -1.0, FAR, ALU.add, ALU.mult), k2)

        def segscan(out_ap, data0, data1, op0, op1, neutral, *after):
            i = after
            s = dve.do(lambda e: e.tensor_tensor_scan(out_ap, data0, data1, neutral, op0, op1), k4, *i)
            s = dve.do(lambda e: e.tensor_copy(ends[:, 0:1], out_ap[:, SEQ - 1:SEQ]), s)
            s = dve.do(lambda e: e.tensor_reduce(ends[:, 1:2], data0, AX_X, ALU.min))
            t = pe.do(lambda e: e.matmul(bank[7][0:1, 0:P], ends[:, 0:1], ident[:, :], start=True, stop=True), s, bank_free[7])
            t = pe.do(lambda e: e.matmul(bank[7][0:1, P:2 * P], ends[:, 1:2], ident[:, :], start=True, stop=True))
            s = dve.do(lambda e: e.tensor_copy(rows1[:, :], bank[7][0:1, 0:2 * P]), t)
            s0 = dve.do(lambda e: e.memset(carry_row[:, 0:1], neutral))
            s = dve.do(lambda e: e.tensor_tensor_scan(carry_row[:, 1:P + 1], rows1[:, P:2 * P], rows1[:, 0:P], neutral, op0, op1), s)
            t = pe.do(lambda e: e.matmul(bank[7][:, 2 * P:2 * P + 1], carry_row[0:1, 0:P], ones[0:1, 0:1],
                                         start=True, stop=True), s, s0)
            s = dve.do(lambda e: e.tensor_copy(carry_col[:, :], bank[7][:, 2 * P:2 * P + 1]), t)
            bank_free[7] = [s]
            return dve.do(lambda e: e.tensor_tensor_scan(out_ap, data0, data1, carry_col[:, 0:1], op0, op1), s)

        zm_ok = segscan(a_s, reset_s, z_s, ALU.add, ALU.max, -FAR, zs_ok, k2)
        zmst = arrival("zmst")
        zmd_ok = sp.dma(zmst, zmax_d.rearrange("(p c) o -> p (c o)", p=P), a_s, zm_ok)
        zmg = arrival("zmg")
        z_node = small[:, 5, :]
        for i in range(NT):
            zg_ok = pool.gather(zmg, z_node[:, i:i + 1], zmax_d, end_i[:, i:i + 1], zmd_ok, end_ok, begin_ok)
        pair_n = sb("pair_n", [P, NT, 2])
        n1 = dve.do(lambda e: e.tensor_copy(pair_n[:, :, 0], t_node), tn_ok)
        n2 = dve.do(lambda e: e.tensor_tensor(z_node, z_node, t_node, ALU.add), zg_ok, n1)
        n3 = dve.do(lambda e: e.scalar_tensor_tensor(out=pair_n[:, :, 1], in0=z_node, scalar=SLOPE, in1=z_node,
                                                     op0=ALU.mult, op1=ALU.max), n2)
        bst = arrival("bst")
        for i in range(NT):
            bd_ok = pool.scatter(bst, begin_d, begin_i[:, i:i + 1], pair_n[:, i, :], n3, n1, begin_ok, tok_begin0)
        tls = arrival("tls")
        tl_ok = sp.dma(tls, tl_s, begin_d[0:EP, :].rearrange("(p k) c -> p k c", p=P), bd_ok)
        tnode_s = segscan(b_s, keep_s, tl_s[:, :, 0], ALU.mult, ALU.add, 0.0, tl_ok)
        e1 = dve.do(lambda e: e.tensor_tensor(z_s, z_s, b_s, ALU.add), tnode_s)
        e2 = leaky(z_s, e1)
        lmax_s = segscan(b_s, keep_s, tl_s[:, :, 1], ALU.mult, ALU.add, 0.0, e1)
        e3 = dve.do(lambda e: e.tensor_tensor(z_s, z_s, b_s, ALU.subtract), lmax_s, e2)
        e4 = act.do(lambda e: e.activation(z_s, z_s, ACT.Exp), e3)
        exst = arrival("exst")
        exd_ok = sp.dma(exst, ex_d.rearrange("(p c) -> p c", p=P), z_s, e4)
        es_ok = segscan(b_s, keep_s, z_s, ALU.mult, ALU.add, 0.0, e4)
        esst = arrival("esst")
        esd_ok = sp.dma(esst, exsum_d.rearrange("(p c) o -> p (c o)", p=P), b_s, es_ok)

        adj_done = arrival("adj_done")
        flag_reg = []

        def scatter_tile(i, first_of_half):
            before = adj_done.value
            if first_of_half:
                if before:
                    pool.wait((adj_done.sem, before))
            elif before:
                def guarded(e, v=before):
                    with e.If(flag_reg[0] > 0):
                        e.wait_ge(adj_done.sem, v)
                pool.ops.append(guarded)
            return pool.scatter(adj_done, adj, target[:, i:i + 1], pair_c[:, i, :], target_ok, pair_ok, tok_adj0, flag_ok,
                                add=True)

        pool.wait(flag_ok)
        pool.ops.append(lambda e: flag_reg.append(e.value_load(flag_i[0:1, 0:1], min_val=0, max_val=1)))
        evens, odds = list(range(0, ET, 2)), list(range(1, ET, 2))
        for i in evens:
            scatter_tile(i, i == 0)
        for i in odds[:200]:
            scatter_tile(i, i == 1)

        he_in = Slots([gath.buffers[0].rearrange("p a b -> p (a b)"), gath.buffers[1].rearrange("p a b -> p (a b)"),
                       gath.buffers[2].rearrange("p a b -> p (a b)"), onehot.buffers[0].rearrange("p a b -> p (a b)")])
        for i in range(3):
            he_in.free[i] = [gather_ok[c][1] for c in range(CH - 3, CH)]
        he_in.free[3] = [d]
        he_in_sem = [arrival(f"he_in{i}") for i in range(4)]
        prod = Slots([sb(f"prod{i}", [P, BANK]) for i in range(2)])
        run = Slots([edge_space[:, i * BANK:(i + 1) * BANK] for i in range(3)])
        run.free = [[edge_in.free[0], edge_in.free[1]] for _ in range(3)]
        flipped = Slots([b[:, :] for b in he.buffers])
        for i in range(3):
            flipped.free[i] = [he.free[0], he.free[1], he.free[2]]
        fl_st = [arrival(f"fl_st{i}") for i in range(3)]
        ex_row, keep_row = Slots([b for b in key_row.buffers]), Slots([sb(f"keep_row{i}", [1, EDGE_COLS], BF16) for i in range(2)])
        for i in range(2):
            ex_row.free[i] = [key_row.free[0], key_row.free[1]]
        exr_sem = [arrival(f"exr{i}") for i in range(2)]
        kpr_sem = [arrival(f"kpr{i}") for i in range(2)]
        rows, fetched, spread = {}, {}, {}
        he_all = [(s.sem, s.value) for s in he_st]

        def fetch_rows(k):
            c = k * EDGE_COLS
            w = min(EDGE_COLS, EP - c)
            a, afree, aafter = ex_row.take()
            t1 = sp.dma(exr_sem[k % 2], a[:, 0:w], ex_d[c:c + w].unsqueeze(0), aafter, exd_ok)
            b, bfree, bafter = keep_row.take()
            t2 = sp.dma(kpr_sem[k % 2], b[:, 0:w], keep_d[c:c + w].unsqueeze(0), bafter, keepd_ok)
            rows[k] = (a, afree, t1, b, bfree, t2)

        def fetch_he(c):
            buf, free, after = he_in.take()
            fetched[c] = (buf, free, sp.dma(he_in_sem[c % 4], buf, he_d[c], after, he_all))

        def spread_rows(c):
            a, afree, t1, b, bfree, t2 = rows[c // LOADC]
            o = (c % LOADC) * BANK
            eb, kb = c % 2, 2 + c % 2
            u = pe.do(lambda e: e.matmul(bank[eb][:, :], ones[0:1, :], a[0:1, o:o + BANK], start=True, stop=True), t1, bank_free[eb])
            v = pe.do(lambda e: e.matmul(bank[kb][:, :], ones_bf[0:1, :], b[0:1, o:o + BANK], start=True, stop=True), t2, bank_free[kb])
            afree[:] = [u]
            bfree[:] = [v]
            spread[c] = (eb, kb, u, v)

        fetch_rows(0)
        fetch_rows(1)
        for c in range(3):
            fetch_he(c)
        spread_rows(0)
        last_run = None
        for c in range(CH):
            k = c // LOADC
            if c % LOADC == 0 and 0 < k and k + 1 < NBIG:
                fetch_rows(k + 1)
            if c + 3 < CH:
                fetch_he(c + 3)
            if c + 1 < CH:
                spread_rows(c + 1)
            hbuf, hfree, h_in = fetched[c]
            eb, kb, u, v = spread[c]
            pbuf, pfree, pafter = prod.take()
            m = dve.do(lambda e, pbuf=pbuf, hbuf=hbuf, eb=eb: e.tensor_tensor(pbuf[:, :], bank[eb][:, :], hbuf, ALU.mult), u, h_in, pafter)
            hfree.append(m)
            bank_free[eb] = [m]
            rb, rfree2, rafter = run.take()
            init = 0.0 if last_run is None else last_run[:, BANK - 1:BANK]
            sc = dve.do(lambda e, rb=rb, kb=kb, pbuf=pbuf, init=init: e.tensor_tensor_scan(
                rb[:, :], bank[kb][:, :], pbuf[:, :], init, ALU.mult, ALU.add), m, v, rafter)
            last_run = rb
            pfree.append(sc)
            bank_free[kb] = [sc]
            tb = 4 + c % 2
            for j in range(TPC):
                t = flip(bank[tb][:, j * P:(j + 1) * P], rb[:, j * P:(j + 1) * P], sc, bank_free[tb], mark=(j == TPC - 1))
            rfree2.append(t)
            fb, ffree, fafter = flipped.take()
            s = act.do(lambda e, fb=fb, tb=tb: e.copy(fb, bank[tb][:, :]), t, fafter)
            bank_free[tb] = [s]
            ffree.append(act.dma(fl_st[c % 3], hesum_d[c * BANK:(c + 1) * BANK, :].rearrange("(j p) f -> p j f", p=P),
                                 fb.rearrange("p (j f) -> p j f", f=P), s))
            if c + 1 < CH:
                run.free[(run.at)].append(None)
            scan_tok = sc
        run_all = [(s.sem, s.value) for s in fl_st]
        agg = Slots([h])[0] if False else h
        ag = arrival("ag")
        sg = arrival("sg")
        s_node = small[:, 6, :]
        for i in range(NT):
            sg_ok = pool.gather(sg, s_node[:, i:i + 1], exsum_d, end_i[:, i:i + 1], esd_ok, s14)
        for i in range(NT):
            ag_ok = pool.gather(ag, h[:, i, :], hesum_d, end_i[:, i:i + 1], run_all, hT_ok, t)
        for i in odds[200:]:
            scatter_tile(i, False)
        adj_ok = (adj_done.sem, adj_done.value)

        r1 = dve.do(lambda e: e.reciprocal(s_node, s_node), sg_ok)
        r2 = dve.do(lambda e: e.tensor_tensor(s_node, s_node, has[:, :], ALU.mult), r1)
        diag = Slots([same.buffers[i] for i in range(4)])
        for i in range(4):
            diag.free[i] = list(same.free[i])
        for g, (c, w) in enumerate(GROUPS):
            b = g % 2
            for j in range(w // P):
                i = c // P + j
                dbuf, dfree, dafter = diag.take()
                dd = dve.do(lambda e, dbuf=dbuf, i=i: e.tensor_scalar(dbuf[:, :], ident[:, :], s_node[:, i:i + 1], None, ALU.mult),
                            r2, dafter)
                t = pe.do(lambda e, b=b, j=j, i=i, dbuf=dbuf: e.matmul(bank[b][:, j * P:(j + 1) * P], h[:, i, :], dbuf[:, :],
                                                                       start=True, stop=True), dd, ag_ok, bank_free[b])
                dfree.append(t)
            agT_ok = act.do(lambda e, b=b, c=c, w=w: e.copy(featT[:, c:c + w], bank[b][:, 0:w]), t)
            bank_free[b] = [agT_ok]
        agg_read = t
        has_bits = arena[0:1, 0:NP]
        for g, (c, w) in enumerate(GROUPS):
            b = 2 + g % 2
            for j in range(w // P):
                t = pe.do(lambda e, b=b, j=j, c=c: e.matmul(bank[b][0:1, j * P:(j + 1) * P], has[:, c // P + j:c // P + j + 1],
                                                            ident[:, :], start=True, stop=True), s8, bank_free[b],
                          mark=(j == w // P - 1))
            hr_ok = dve.do(lambda e, b=b, c=c, w=w: e.tensor_copy(has_bits[:, c:c + w], bank[b][0:1, 0:w]), t)
            bank_free[b] = [hr_ok]
        wk_free = [[], []]
        for g, (c, w) in enumerate(GROUPS):
            k = g % 2
            b, b2, b3 = k, 2 + k, 4 + k
            ctxT, neg = run.buffers[k], prod.buffers[k]
            t = pe.do(lambda e, b=b, c=c, w=w: e.matmul(bank[b][:, 0:w], W["L0_gnn_Wet"][:, :], featT[:, c:c + w],
                                                        start=True, stop=False), agT_ok, bank_free[b])
            t = pe.do(lambda e, b=b, c=c, w=w: e.matmul(bank[b][:, 0:w], bet_row[0:1, :], has_bits[0:1, c:c + w],
                                                        start=False, stop=True), hr_ok)
            a = dve.do(lambda e, b=b, w=w, neg=neg: e.tensor_scalar(neg[:, 0:w], bank[b][:, 0:w], 0.0, None, ALU.min), t, wk_free[k], scan_tok)
            e_ = act.do(lambda e, w=w, neg=neg: e.activation(neg[:, 0:w], neg[:, 0:w], ACT.Exp), a)
            a = dve.do(lambda e, b=b, w=w, ctxT=ctxT: e.tensor_scalar(ctxT[:, 0:w], bank[b][:, 0:w], 0.0, None, ALU.max))
            bank_free[b] = [a]
            a = dve.do(lambda e, w=w, ctxT=ctxT, neg=neg: e.scalar_tensor_tensor(out=ctxT[:, 0:w], in0=neg[:, 0:w], scalar=-1.0,
                                                                                 in1=ctxT[:, 0:w], op0=ALU.add, op1=ALU.add), a, e_)
            t = pe.do(lambda e, b2=b2, w=w, ctxT=ctxT: e.matmul(bank[b2][:, 0:w], W["W1_context"][:, :], ctxT[:, 0:w],
                                                                start=True, stop=False), a, bank_free[b2])
            t = pe.do(lambda e, b2=b2, c=c, w=w: e.matmul(bank[b2][:, 0:w], W["W1_node"][:, :], hvT[:, c:c + w],
                                                          start=False, stop=True))
            o = act.do(lambda e, b2=b2, w=w, neg=neg: e.activation(neg[:, 0:w], bank[b2][:, 0:w], ACT.Relu,
                                                                   bias=col["L0_gnn_b1"][:, 0:1]), t)
            bank_free[b2] = [o]
            for j in range(w // P):
                t = pe.do(lambda e, b3=b3, j=j, neg=neg: e.matmul(bank[b3][:, j * P:(j + 1) * P], neg[:, j * P:(j + 1) * P],
                                                                  W["L0_gnn_W2"][:, :], start=True, stop=True), o, bank_free[b3],
                          mark=(j == w // P - 1))
            n = w // P
            a = dve.do(lambda e, b3=b3, n=n, k=k: e.tensor_tensor(work[:, k, 0:n * P].rearrange("p (j f) -> p j f", f=P),
                                                                  bank[b3][:, 0:n * P].rearrange("p (j f) -> p j f", f=P),
                                                                  along(row["L0_gnn_b2"][:, :], n), ALU.add), t)
            bank_free[b3] = [a]
            x_ok = dve.do(lambda e, n=n, k=k, c=c: e.scalar_tensor_tensor(
                out=x[:, c // P:c // P + n, :].rearrange("p j f -> p (j f)"), in0=work[:, k, 0:n * P], scalar=0.0,
                in1=x[:, c // P:c // P + n, :].rearrange("p j f -> p (j f)"), op0=ALU.max, op1=ALU.add), a)
            wk_free[k] = [t, a]

        def scaled(dst, scale, after):
            out_tok = []
            for c, w in GROUPS:
                n = w // P
                out_tok.append(dve.do(lambda e, c=c, n=n: e.tensor_tensor(
                    dst[:, c // P:c // P + n, :], dst[:, c // P:c // P + n, :],
                    across(scale[:, c // P:c // P + n], P), ALU.mult), after))
            return out_tok[-1]

        edge_over = [adj_ok, exd_ok, esd_ok, keepd_ok, pe.last(), act.last(), dve.last()]
        used[0] = 0
        mat = Slots([carve(NP) for _ in range(8)])
        mat_sem = [arrival(f"mat{i}") for i in range(8)]
        mat.free = [list(edge_over) for _ in mat.buffers]
        pairs = Slots([arena[:, i * 2 * NP:(i + 1) * 2 * NP].rearrange("p (n c) -> p n c", c=2) for i in range(2)])
        pairs.free = [list(edge_over) for _ in range(2)]
        parts = Slots([arena[:, (4 + i) * NP:(5 + i) * NP] for i in range(4)])
        parts.free = [list(edge_over) for _ in range(4)]
        turned = Slots([he.buffers[i] for i in range(3)])
        turned.free = [list(run_all) for _ in range(3)]
        pair_sem = [arrival(f"pair{i}") for i in range(2)]
        part_st = [arrival(f"part_st{i}") for i in range(4)]
        turn_st = [arrival(f"turn_st{i}") for i in range(3)]

        h_ok = layernorm([x_ok], [agg_read])
        h_ok = scaled(h, dis, [h_ok, dis_ok])

        def product_tile(i, m_ap, m_ok, feat_ok):
            for g, (c, w) in enumerate(GROUPS):
                t = pe.do(lambda e, g=g, c=c, w=w: e.matmul(bank[g][:, 0:w], h[:, i, :], m_ap[:, c:c + w],
                                                            start=(i == 0), stop=(i == NT - 1)),
                          m_ok, feat_ok, bank_free[g] if i == 0 else None, mark=(g == len(GROUPS) - 1))
            return t

        def load_pair(i):
            buf, free, after = pairs.take()
            return buf, free, sp.dma(pair_sem[i % 2], buf, adj[i * P * NP:(i + 1) * P * NP, :].rearrange("(p n) c -> p n c", p=P),
                                     after, adj_ok)

        nxt = load_pair(0)
        for i in range(NT):
            pbuf, pfree, p_ok = nxt
            if i + 1 < NT:
                nxt = load_pair(i + 1)
            wbuf, wfree, wafter = parts.take()
            cbuf, cfree, cafter = parts.take()
            ws, cs = (parts.at - 1) % 4, parts.at
            w_ok = dve.do(lambda e, wbuf=wbuf, pbuf=pbuf: e.tensor_copy(wbuf, pbuf[:, :, 0]), p_ok, wafter)
            c_ok = act.do(lambda e, cbuf=cbuf, pbuf=pbuf: e.copy(cbuf, pbuf[:, :, 1]), p_ok, cafter)
            d1 = dve.do(lambda e, wbuf=wbuf, i=i: e.tensor_tensor(wbuf[:, i * P:(i + 1) * P], wbuf[:, i * P:(i + 1) * P],
                                                                  ident[:, :], ALU.add), w_ok)
            d2 = dve.do(lambda e, cbuf=cbuf, i=i: e.tensor_tensor(cbuf[:, i * P:(i + 1) * P], cbuf[:, i * P:(i + 1) * P],
                                                                  ident[:, :], ALU.add), c_ok)
            st1 = act.dma(part_st[ws], weight_t[i * P:(i + 1) * P, :], wbuf, d1)
            st2 = act.dma(part_st[cs], count_t[i * P:(i + 1) * P, :], cbuf, d2)
            t = product_tile(i, wbuf, d1, h_ok)
            wfree.extend([st1, t])
            cfree.append(st2)
            for g, (c, w) in enumerate(GROUPS):
                for j in range(w // P):
                    t = flip(bank[7][:, j * P:(j + 1) * P], pbuf[:, c + j * P:c + (j + 1) * P, 0], p_ok, bank_free[7], mark=(j == w // P - 1))
                tb, tfree, tafter = turned.take()
                ts = turned.at
                s = (dve if g % 2 else act).do(lambda e, tb=tb, w=w, dv=g % 2: (e.tensor_copy if dv else e.copy)(tb[:, 0:w], bank[7][:, 0:w]), t, tafter)
                bank_free[7] = [s]
                tfree.append(sp.dma(turn_st[ts], weight_n[c:c + w, i * P:(i + 1) * P].rearrange("(j p) s -> p j s", p=P),
                                    tb[:, 0:w].rearrange("p (j s) -> p j s", s=P), s))
            pfree.extend([t, w_ok, c_ok])
        prod_ok = (pe.sem, pe.count)
        weight_t_ok = count_t_ok = [(s.sem, s.value) for s in part_st]
        weight_n_ok = [(s.sem, s.value) for s in turn_st]
        for i in range(4):
            mat.free[i] = pairs.free[0] + pairs.free[1]
            mat.free[4 + i] = parts.free[i]
        mat_queue = []

        def fetch_mat(matrix, i, ready):
            buf, free, after = mat.take()
            mat_queue.append((buf, free, sp.dma(mat_sem[mat.at], buf, matrix[i * P:(i + 1) * P, :], after, ready)))

        plan = [(weight_t, i, weight_t_ok) for _ in range(2) for i in range(NT)] + \
               [(count_t, i, count_t_ok) for _ in range(3) for i in range(NT)] + \
               [(weight_n, i, weight_n_ok) for _ in range(3) for i in range(NT)]
        plan.reverse()
        for _ in range(8):
            fetch_mat(*plan.pop())

        def product(feat_ok):
            for i in range(NT):
                buf, free, ok = mat_queue.pop(0)
                t = product_tile(i, buf, ok, feat_ok)
                free.append(t)
                if plan:
                    fetch_mat(*plan.pop())
            return t

        def evacuate(t):
            for g, (c, w) in enumerate(GROUPS):
                q = (act, dve)[g % 2]
                s = q.do(lambda e, g=g, c=c, w=w: (e.tensor_copy if g % 2 else e.copy)(featT[:, c:c + w], bank[g][:, 0:w]), t)
                bank_free[g] = [s]
            return [act.last(), dve.last()]

        def gcn_out(weight, scale, bias, slope, last):
            toks = []
            for g, (c, w) in enumerate(GROUPS):
                n, b, k = w // P, g, g % 2
                for j in range(n):
                    t = pe.do(lambda e, b=b, j=j, c=c: e.matmul(bank[b][:, j * P:(j + 1) * P], featT[:, c + j * P:c + (j + 1) * P],
                                                                weight[:, :], start=True, stop=True), featT_ok, bank_free[b],
                              mark=(j == n - 1))
                v3 = work[:, k, 0:w].rearrange("p (j f) -> p j f", f=P)
                h3 = h[:, c // P:c // P + n, :]
                sc3 = across(scale[:, c // P:c // P + n], P)
                a = dve.do(lambda e, v3=v3, b=b, w=w, sc3=sc3: e.tensor_tensor(v3, bank[b][:, 0:w].rearrange("p (j f) -> p j f", f=P),
                                                                               sc3, ALU.mult), t)
                bank_free[b] = [a]
                a = dve.do(lambda e, v3=v3, n=n: e.tensor_tensor(v3, v3, along(bias[:, :], n), ALU.add), a)
                if slope is None:
                    if last:
                        x3 = x[:, c // P:c // P + n, :]
                        a = dve.do(lambda e, v3=v3, x3=x3, w=w, k=k: e.scalar_tensor_tensor(
                            out=x3, in0=v3, scalar=0.0, in1=x3, op0=ALU.max, op1=ALU.add), a)
                    else:
                        a = dve.do(lambda e, v3=v3, h3=h3, sc3=sc3: e.scalar_tensor_tensor(
                            out=h3, in0=v3, scalar=0.0, in1=sc3, op0=ALU.max, op1=ALU.mult), a)
                else:
                    a2 = dve.do(lambda e, v3=v3, h3=h3, n=n: e.scalar_tensor_tensor(
                        out=h3, in0=v3, scalar=0.0, in1=along(slope[:, :], n), op0=ALU.min, op1=ALU.mult), a)
                    a = dve.do(lambda e, v3=v3, h3=h3: e.scalar_tensor_tensor(
                        out=h3, in0=v3, scalar=0.0, in1=h3, op0=ALU.max, op1=ALU.add), a2)
                    if last:
                        x3 = x[:, c // P:c // P + n, :]
                        a = dve.do(lambda e, h3=h3, x3=x3: e.tensor_tensor(x3, x3, h3, ALU.add), a)
                    else:
                        a = dve.do(lambda e, h3=h3, sc3=sc3: e.tensor_tensor(h3, h3, sc3, ALU.mult), a)
                toks.append(a)
            return toks[-1]

        featT_ok = evacuate(prod_ok)
        for l in range(3):
            done = gcn_out(W[f"L1_gnn_W{l + 1}"], dis, row[f"L1_gnn_b{l + 1}"], row[f"L1_gnn_a{l + 1}"], l == 2)
            if l < 2:
                featT_ok = evacuate(product(done))
        h_ok = layernorm([done], [pe.last()])
        done = scaled(h, dinv, [h_ok, s20])
        for l in range(3):
            featT_ok = evacuate(product(done))
            done = gcn_out(W[f"L2_gnn_W{l}"], dinv, row[f"L2_gnn_b{l}"], None, l == 2)
        a = dve.do(lambda e: e.tensor_reduce(carry_col[:, :], alpha[:, :], AX_X, ALU.max), tok_small)
        a = dve.do(lambda e: e.tensor_scalar(alpha[:, :], alpha[:, :], carry_col[:, 0:1], None, ALU.subtract), a)
        a = act.do(lambda e: e.activation(alpha[:, :], alpha[:, :], ACT.Exp), a)
        a = dve.do(lambda e: e.tensor_reduce(carry_col[:, :], alpha[:, :], AX_X, ALU.add), a)
        a = dve.do(lambda e: e.reciprocal(carry_col[:, :], carry_col[:, :]), a)
        al_ok = dve.do(lambda e: e.tensor_scalar(alpha[:, :], alpha[:, :], carry_col[:, 0:1], None, ALU.mult), a)
        done = layernorm([done], [pe.last()])
        flat_h, flat_x = h.rearrange("p t f -> p (t f)"), x.rearrange("p t f -> p (t f)")
        for k in range(4):
            if k:
                t = product(done)
                featT_ok = evacuate(t)
                for g, (c, w) in enumerate(GROUPS):
                    for j in range(w // P):
                        t = flip(bank[g][:, j * P:(j + 1) * P], featT[:, c + j * P:c + (j + 1) * P], featT_ok, bank_free[g], mark=(j == w // P - 1))
                    done = act.do(lambda e, g=g, c=c, w=w: e.copy(flat_h[:, c:c + w], bank[g][:, 0:w]), t, xk_ok)
                    bank_free[g] = [done]
            for c, w in GROUPS:
                xk_ok = dve.do(lambda e, c=c, w=w, k=k: e.scalar_tensor_tensor(
                    out=flat_x[:, c:c + w], in0=flat_h[:, c:c + w], scalar=alpha[:, k:k + 1], in1=flat_x[:, c:c + w],
                    op0=ALU.mult, op1=ALU.add), done, al_ok, xk_ok if k else None)
        out_st = arrival("out_st")
        full = N // P
        sp.dma(out_st, out[0:full * P, :].rearrange("(t p) f -> p t f", p=P), x[:, 0:full, :], xk_ok)
        sp.dma(out_st, out[full * P:N, :], x[0:N - full * P, full, :], xk_ok)
        sp.wait((out_st.sem, out_st.value))

        block = ctx.enter_context(nc.Block())
        for attach, queue in ((block.tensor, pe), (block.scalar, act), (block.vector, dve), (block.gpsimd, pool), (block.sync, sp)):
            def body(e, queue=queue):
                for op in queue.ops:
                    op(e)
            attach(body)


def kernel(**inputs):
    import concourse.bacc as bacc
    from concourse.bass_utils import run_bass_kernel_spmd as run

    g = {k: np.asarray(v) for k, v in inputs.items()}
    pad = np.arange(EP - E, dtype=np.int32) // 4 + N
    src = np.concatenate([g["src"], pad])
    dst = np.concatenate([g["dst"], pad])
    weight = np.concatenate([g["edge_weight"], np.zeros(EP - E, np.float32)])
    columns = lambda v: np.ascontiguousarray(v.reshape(ET, P).T)
    arrays = {
        "x": np.concatenate([g["x"], np.zeros((NP - N, P), np.float32)]),
        "src_c": columns(src), "dst_c": columns(dst),
        "w1_c": np.stack([columns(weight), np.ones((P, ET), np.float32)], 2).reshape(P, 2 * ET),
        "dst": np.concatenate([np.full(1, -1, np.int32), dst]),
        "tile_first": dst.reshape(ET, P)[None, :, 0].copy(), "tile_last": dst.reshape(ET, P)[None, :, P - 1].copy(),
        "edgeT": np.concatenate([g["edge_attr_64"].T, np.zeros((EF, EP - E), np.float32)], 1),
        "We1_node": g["L0_gnn_We1"][:P], "We1_edge": g["L0_gnn_We1"][P:],
        "W1_context": g["L0_gnn_W1"][:P], "W1_node": g["L0_gnn_W1"][P:],
        "We2_node": g["L0_gnn_We2"][:P], "We2_edge": g["L0_gnn_We2"][P:],
        "L0_gnn_be2": g["L0_gnn_be2"].reshape(1, 1), "L0_gnn_bet": g["L0_gnn_bet"].reshape(1, P),
        "L3_gnn_alpha_logits": g["L3_gnn_alpha_logits"].reshape(1, 4),
    }
    for n in BIAS_ROWS:
        arrays[n] = g[n].reshape(1, P)
    for n in BIAS_COLUMNS:
        arrays.setdefault(n, g[n].reshape(P, 1) if n in g else None)
    for n in WEIGHTS:
        arrays.setdefault(n, g[n] if n in g else None)
    nc = bacc.Bacc("TRN2", target_bir_lowering=False, num_devices=1)
    given = {}
    arrays = {"in_" + n: np.ascontiguousarray(a) for n, a in arrays.items()}
    for n, a in arrays.items():
        given[n[3:]] = nc.dram_tensor(n, a.shape, mybir.dt.from_np(a.dtype), kind="ExternalInput").ap()
    out = nc.dram_tensor("out", (N, P), F32, kind="ExternalOutput").ap()
    build(nc, given, out)
    r = run(nc, [arrays], core_ids=[0])
    return r.results[0]["out"]
```

```python
from contextlib import ExitStack

import numpy as np

import concourse.bass as bass
from concourse import mybir

F32 = mybir.dt.float32
BF16 = mybir.dt.bfloat16
I32 = mybir.dt.int32
ALU = mybir.AluOpType
ACT = mybir.ActivationFunctionType
AX_X = mybir.AxisListType.X

P = 128
N = 3125
E = 103125
EF = 64
NT = -(-N // P)
NP = NT * P
BANK = 512
CH = -(-E // BANK)
EP = CH * BANK
TPC = BANK // P
ET = EP // P
SEQ = EP // P
GROUPS = [(g * BANK, min(BANK, NP - g * BANK)) for g in range(-(-NP // BANK))]
DUMP = NP * NP
FAR = 1e30
EPS = 1e-5
SLOPE = 0.01

WEIGHTS = ["L0_gnn_Wn", "We1_node", "L0_gnn_Wet", "W1_context", "W1_node", "L0_gnn_W2",
           "L1_gnn_W1", "L1_gnn_W2", "L1_gnn_W3", "L2_gnn_W0", "L2_gnn_W1", "L2_gnn_W2"]
BIAS_COLUMNS = ["L0_gnn_bn", "L0_gnn_be1", "L0_gnn_b1", "We2_node", "We2_edge"]
BIAS_ROWS = ["L0_gnn_b2", "L1_gnn_b1", "L1_gnn_b2", "L1_gnn_b3", "L1_gnn_a1", "L1_gnn_a2", "L1_gnn_a3",
             "L2_gnn_b0", "L2_gnn_b1", "L2_gnn_b2"]


class Queue:

    def __init__(self, sem):
        self.sem, self.count, self.ops, self.seen = sem, 0, [], {}

    def wait(self, *after):
        for tok in after:
            if tok is None:
                continue
            if isinstance(tok, list):
                self.wait(*tok)
                continue
            sem, value = tok
            if self.seen.get(id(sem), 0) < value:
                self.seen[id(sem)] = value
                self.ops.append(lambda e, s=sem, v=value: e.wait_ge(s, v))

    def do(self, issue, *after, mark=True):
        self.wait(*after)
        if not mark:
            self.ops.append(issue)
            return None
        self.count += 1
        self.ops.append(lambda e: issue(e).then_inc(self.sem, 1))
        return (self.sem, self.count)

    def dma(self, arrival, out, in_, *after, **kw):
        self.wait(*after)
        arrival.value += 16
        self.ops.append(lambda e: e.dma_start(out, in_, **kw).then_inc(arrival.sem, 16))
        return (arrival.sem, arrival.value)

    def gather(self, arrival, out, table, index, *after):
        self.wait(*after)
        arrival.value += 16
        self.ops.append(lambda e: e.indirect_dma_start(
            out, None, table, bass.IndirectOffsetOnAxis(ap=index, axis=0)).then_inc(arrival.sem, 16))
        return (arrival.sem, arrival.value)

    def scatter(self, arrival, table, index, in_, *after, add=False):
        self.wait(*after)
        arrival.value += 16
        kw = dict(compute_op=ALU.add) if add else {}
        self.ops.append(lambda e: e.indirect_dma_start(
            table, bass.IndirectOffsetOnAxis(ap=index, axis=0), in_, None, **kw).then_inc(arrival.sem, 16))
        return (arrival.sem, arrival.value)

    def last(self):
        return (self.sem, self.count) if self.count else None


class Arrival:

    def __init__(self, sem):
        self.sem, self.value = sem, 0


class Slots:

    def __init__(self, buffers):
        self.buffers, self.free, self.at = buffers, [[] for _ in buffers], -1

    def take(self):
        self.at = (self.at + 1) % len(self.buffers)
        after, self.free[self.at] = self.free[self.at], []
        return self.buffers[self.at], self.free[self.at], after


def along(ap, n):
    return ap.unsqueeze(1).broadcast_to([ap.shape[0], n, ap.shape[1]])


def across(ap, n):
    return ap.unsqueeze(2).broadcast_to([ap.shape[0], ap.shape[1], n])


def build(nc, given, out):
    with ExitStack() as ctx:
        def sb(name, shape, dt=F32):
            return ctx.enter_context(nc.sbuf_tensor(name, shape, dt))

        def dram(name, shape, dt=F32):
            return nc.dram_tensor(name, shape, dt, kind="Internal").ap()

        def arrival(name):
            return Arrival(ctx.enter_context(nc.semaphore(name)))

        pe, act, dve, pool, sp = (Queue(ctx.enter_context(nc.semaphore(f"done_{n}")))
                                  for n in ("pe", "act", "dve", "pool", "sp"))
        bank = [ctx.enter_context(nc.psum_tensor(f"bank{i}", [P, BANK], F32)) for i in range(8)]
        bank_free = [[] for _ in bank]

        node_table = dram("node_table", [NP, P])
        he_d = dram("he_d", [CH, P, BANK])
        z_d = dram("z_d", [EP, 1])
        key_d = dram("key_d", [3, EP], BF16)
        zmax_d = dram("zmax_d", [EP, 1])
        begin_d = dram("begin_d", [EP + NP, 2])
        ex_d = dram("ex_d", [3, EP], BF16)
        keep_d = dram("keep_d", [EP], BF16)
        exsum_d = dram("exsum_d", [EP, 1])
        hesum_d = dram("hesum_d", [EP, P])
        adj = dram("adj", [NP * NP + EP, 2])
        weight_t = dram("weight_t", [NP, NP])
        count_t = dram("count_t", [NP, NP])
        weight_n = dram("weight_n", [NP, NP])

        ident = sb("ident", [P, P])
        tri_incl = sb("tri_incl", [P, P])
        tri_less = sb("tri_less", [P, P])
        ones = sb("ones", [P, P])
        ones_bf = sb("ones_bf", [3, P], BF16)
        iota_i = sb("iota_i", [P, P], I32)
        iota_b = sb("iota_b", [P, P], BF16)
        eps_col = sb("eps_col", [P, 1])
        W = {n: sb(n, [P, P]) for n in WEIGHTS}
        We1_edge = sb("We1_edge", [EF, P])
        col = {n: sb("c_" + n, [P, 1]) for n in BIAS_COLUMNS}
        row = {n: sb("r_" + n, [P, P]) for n in BIAS_ROWS}
        be2_col = sb("be2_col", [P, 1])
        bet_row = sb("bet_row", [1, P])
        alpha = sb("alpha", [P, 4])
        x = sb("x", [P, NT, P])
        h = sb("h", [P, NT, P])
        featT = sb("featT", [P, NP])
        hvT = sb("hvT", [P, NP])
        stats = sb("stats", [P, NT, 6])
        moments = sb("moments", [P, NT, 2])
        rstd = sb("rstd", [P, NT])
        shift = sb("shift", [P, NT])
        dis = sb("dis", [P, NT])
        dinv = sb("dinv", [P, NT])
        has = sb("has", [P, NT])
        small = sb("small", [P, 8, NT])
        end_i = sb("end_i", [P, NT], I32)
        begin_i = sb("begin_i", [P, NT], I32)
        work = sb("work", [P, 2, BANK])

        ARENA = 26500
        arena = sb("arena", [P, ARENA])
        used = [0]

        def carve(n):
            used[0] += n
            assert used[0] <= ARENA, used[0]
            return arena[:, used[0] - n:used[0]]

        src_c = carve(ET).bitcast(I32)
        dst_c = carve(ET).bitcast(I32)
        w_c = carve(ET)
        w4_c = carve(2 * ET).bitcast(BF16).rearrange("p (t c) -> p t c", c=4)
        key_c = carve(ET)
        lo_c = carve(ET)
        hi_c = carve(ET)
        lohi_bf = carve(ET).bitcast(BF16).rearrange("p (c t) -> p c t", c=2)
        later_c = carve(ET)
        pair_c = carve(2 * ET).rearrange("p (t c) -> p t c", c=2)
        target = carve(ET).bitcast(I32)
        z_c = carve(ET)
        z_t = carve(7 * P).rearrange("p (g e) -> p g e", e=P)
        dst_s = carve(SEQ).bitcast(I32)
        prev_s = carve(SEQ).bitcast(I32)
        keep_s = carve(SEQ)
        reset_s = carve(SEQ)
        a_s = carve(SEQ)
        b_s = carve(SEQ)
        z_s = carve(SEQ)
        tl_space = carve(2 * SEQ)
        tl_s = tl_space.rearrange("p (t c) -> p t c", c=2)
        keep_bf = carve(SEQ // 2).bitcast(BF16)
        piece_bf = [tl_space[:, n * SEQ // 2:(n + 1) * SEQ // 2].bitcast(BF16) for n in range(3)]
        EDGE_COLS = 1024
        edge_space = carve(2 * EDGE_COLS)
        edge_in = Slots([edge_space[0:EF, i * EDGE_COLS:(i + 1) * EDGE_COLS] for i in range(2)])
        key_row = Slots([carve(EDGE_COLS // 2).bitcast(BF16)[0:3, :] for _ in range(2)])

        gath = Slots([sb(f"gath{i}", [P, TPC, P]) for i in range(3)])
        he = Slots([sb(f"he{i}", [P, BANK]) for i in range(3)])
        onehot_space = carve(BANK)
        onehot = Slots([onehot_space[:, i * BANK // 2:(i + 1) * BANK // 2].bitcast(BF16).rearrange("p (a b) -> p a b", b=P)
                        for i in range(2)])
        hi_hot = Slots([carve(TPC * NT // 2).bitcast(BF16).rearrange("p (a b) -> p a b", b=NT) for i in range(2)])
        tile_hot = Slots([carve(TPC * 2 * NT).bitcast(BF16).rearrange("p (a c b) -> p a c b", c=4, b=NT) for _ in range(2)])
        same = Slots([carve(P // 2).bitcast(BF16) for _ in range(8)])
        diag_space = [carve(P) for _ in range(2)]
        rows1 = sb("rows1", [1, 2 * P])
        carry_row = sb("carry_row", [1, P + 1])
        carry_col = sb("carry_col", [P, 1])
        ends = sb("ends", [P, 2])
        flag_row = sb("flag_row", [1, 3, ET])
        flag_f = sb("flag_f", [1, 1])
        flag_i = sb("flag_i", [1, 1], I32)
        node_iota = sb("node_iota", [P, NT], I32)

        loaded = {}

        def load(name, dst_ap, src_ap, q=None, **kw):
            loaded[name] = (q or sp).dma(arrival("ld_" + name), dst_ap, src_ap, **kw)
            return loaded[name]

        in_x = load("x", x[:, :, :], given["x"].rearrange("(t p) f -> p t f", p=P))
        load("src_c", src_c, given["src_c"])
        load("dst_c", dst_c, given["dst_c"])
        load("w_c", w_c, given["w_c"])
        load("src_s", z_s.bitcast(I32), given["src"].rearrange("(p c) -> p c", p=P))
        load("dst_s", dst_s, given["dst"][1:EP + 1].rearrange("(p c) -> p c", p=P))
        load("prev_s", prev_s, given["dst"][0:EP].rearrange("(p c) -> p c", p=P))
        small_load = arrival("ld_small")
        for n in WEIGHTS:
            tok_small = act.dma(small_load, W[n][:, :], given[n])
        act.dma(small_load, We1_edge[:, :], given["We1_edge"])
        for n in BIAS_COLUMNS:
            act.dma(small_load, col[n][:, :], given[n])
        for n in BIAS_ROWS:
            act.dma(small_load, row[n][:, :], given[n].broadcast_to([P, P]))
        act.dma(small_load, be2_col[:, :], given["L0_gnn_be2"].broadcast_to([P, 1]))
        act.dma(small_load, bet_row[:, :], given["L0_gnn_bet"])
        tok_small = act.dma(small_load, alpha[:, :], given["L3_gnn_alpha_logits"].broadcast_to([P, 4]))

        c0 = pool.do(lambda e: e.memset(ident[:, :], 0.0))
        c_ones = pool.do(lambda e: e.memset(ones[:, :], 1.0))
        c1 = pool.do(lambda e: e.affine_select(out=ident[:, :], in_=ident[:, :], compare_op=ALU.not_equal, fill=1.0,
                                               base=0, pattern=[[-1, P]], channel_multiplier=1), c0, c_ones)
        pool.do(lambda e: e.affine_select(out=tri_incl[:, :], in_=ones[:, :], compare_op=ALU.is_ge, fill=0.0,
                                          base=0, pattern=[[1, P]], channel_multiplier=-1))
        pool.do(lambda e: e.affine_select(out=tri_less[:, :], in_=ones[:, :], compare_op=ALU.is_gt, fill=0.0,
                                          base=0, pattern=[[1, P]], channel_multiplier=-1))
        pool.do(lambda e: e.iota(iota_i[:, :], pattern=[[1, P]], base=0, channel_multiplier=0))
        consts = pool.do(lambda e: e.iota(node_iota[:, :], pattern=[[P, NT]], base=EP, channel_multiplier=1))
        dve.do(lambda e: e.tensor_copy(iota_b[:, :], iota_i[:, :]), consts)
        dve.do(lambda e: e.memset(ones_bf[:, :], 1.0))
        v_consts = dve.do(lambda e: e.memset(eps_col[:, :], EPS))

        ZC = 6400
        zeros = carve(ZC // 5)
        z0 = dve.do(lambda e: e.memset(zeros[:, :], 0.0))

        def layernorm(after_x, after_h):
            for t in range(NT):
                a = dve.do(lambda e, t=t: e.bn_stats(stats[:, t, :], x[:, t, :]), after_x)
            for t in range(NT):
                b = dve.do(lambda e, t=t: e.bn_aggr(moments[:, t, :], stats[:, t, :]), a)
            s = act.do(lambda e: e.activation(rstd[:, :], moments[:, :, 1], ACT.Sqrt, bias=eps_col[:, 0:1]), b, v_consts)
            r = dve.do(lambda e: e.reciprocal(rstd[:, :], rstd[:, :]), s)
            m = dve.do(lambda e: e.scalar_tensor_tensor(out=shift[:, :], in0=moments[:, :, 0], scalar=-1.0,
                                                        in1=rstd[:, :], op0=ALU.mult, op1=ALU.mult), r)
            for t in range(NT):
                o = act.do(lambda e, t=t: e.activation(h[:, t, :], x[:, t, :], ACT.Relu, bias=shift[:, t:t + 1],
                                                       scale=rstd[:, t:t + 1]), m, after_h)
            return o

        def leaky(ap, *after):
            return dve.do(lambda e: e.scalar_tensor_tensor(out=ap, in0=ap, scalar=SLOPE, in1=ap, op0=ALU.mult, op1=ALU.max),
                          *after)

        def flip(out_ap, in_ap, *after, mark=False):
            k = in_ap.shape[0]
            return pe.do(lambda e: e.transpose(out_ap, in_ap, ident[0:k, 0:k]), consts, *after, mark=mark)

        h_ok = layernorm([in_x], [])
        for g, (c, w) in enumerate(GROUPS):
            b = g % 2
            for j in range(w // P):
                t = flip(bank[b][:, j * P:(j + 1) * P], h[:, c // P + j, :], h_ok, bank_free[b], mark=(j == w // P - 1))
            hT_ok = act.do(lambda e, b=b, c=c, w=w: e.copy(featT[:, c:c + w], bank[b][:, 0:w]), t)
            bank_free[b] = [hT_ok]
        table_st = [arrival(f"table_st{i}") for i in range(2)]
        gslot = Slots([he.buffers[0], he.buffers[1]])
        for g, (c, w) in enumerate(GROUPS):
            b = 2 + g % 2
            for j in range(w // P):
                t = pe.do(lambda e, b=b, j=j, c=c: e.matmul(bank[b][:, j * P:(j + 1) * P], featT[:, c + j * P:c + (j + 1) * P],
                                                            W["We1_node"][:, :], start=True, stop=True),
                          hT_ok, tok_small, bank_free[b], mark=(j == w // P - 1))
            buf, free, after = gslot.take()
            s = dve.do(lambda e, b=b, w=w, buf=buf: e.tensor_copy(buf[:, 0:w], bank[b][:, 0:w]), t, after)
            bank_free[b] = [s]
            free.append(sp.dma(table_st[g % 2], node_table[c:c + w, :].rearrange("(j p) f -> p j f", p=P),
                               buf[:, 0:w].rearrange("p (j f) -> p j f", f=P), s))
        table_ok = [(s.sem, s.value) for s in table_st]
        he.free[0], he.free[1] = [table_ok], [table_ok]
        for g, (c, w) in enumerate(GROUPS):
            b = 4 + g % 2
            t = pe.do(lambda e, b=b, c=c, w=w: e.matmul(bank[b][:, 0:w], W["L0_gnn_Wn"][:, :], featT[:, c:c + w],
                                                        start=True, stop=True), bank_free[b])
            a = act.do(lambda e, b=b, c=c, w=w: e.activation(hvT[:, c:c + w], bank[b][:, 0:w], ACT.Identity,
                                                             bias=col["L0_gnn_bn"][:, 0:1]), t, tok_small)
            bank_free[b] = [a]
            hv_ok = leaky(hvT[:, c:c + w], a)
        t_node = small[:, 0, :]
        for i in range(NT):
            t = pe.do(lambda e, i=i: e.matmul(bank[6][:, i:i + 1], hvT[:, i * P:(i + 1) * P], col["We2_node"][:, 0:1],
                                              start=True, stop=True), hv_ok, mark=(i == NT - 1))
        tn_ok = dve.do(lambda e: e.tensor_scalar(t_node, bank[6][:, 0:NT], be2_col[:, 0:1], None, ALU.add), t, tok_small)
        bank_free[6] = [tn_ok]

        gather_ok, gather_sem = [], [arrival(f"gath{i}") for i in range(3)]

        for n, a in (("src_c", src_c), ("dst_c", dst_c)):
            pass
        kf = dve.do(lambda e: e.tensor_copy(hi_c, dst_c), loaded["dst_c"])
        sf = dve.do(lambda e: e.tensor_copy(lo_c, src_c), loaded["src_c"])
        key_ok = dve.do(lambda e: e.scalar_tensor_tensor(out=key_c, in0=lo_c, scalar=float(NP), in1=hi_c,
                                                         op0=ALU.mult, op1=ALU.add), kf, sf)
        lo_i = later_c.bitcast(I32)
        a = dve.do(lambda e: e.tensor_scalar(lo_i, dst_c, P - 1, None, ALU.bitwise_and))
        b_ = dve.do(lambda e: e.tensor_copy(lo_c, lo_i), a, key_ok)
        a = dve.do(lambda e: e.tensor_scalar(lo_i, dst_c, 7, None, ALU.arith_shift_right), b_)
        hilo_ok = dve.do(lambda e: e.tensor_copy(hi_c, lo_i), a)
        dve.do(lambda e: e.tensor_copy(lohi_bf[:, 0, :], lo_c))
        hilo_ok = dve.do(lambda e: e.tensor_copy(lohi_bf[:, 1, :], hi_c), hilo_ok)
        dve.do(lambda e: e.memset(w4_c[:, :, 3], 1.0))
        rest, r_ok = w_c, loaded["w_c"]
        for n in range(3):
            p_ok = dve.do(lambda e, n=n, rest=rest: e.tensor_copy(w4_c[:, :, n], rest), r_ok)
            if n < 2:
                r_ok = dve.do(lambda e, n=n, rest=rest: e.tensor_tensor(z_c, rest, w4_c[:, :, n], ALU.subtract), p_ok)
                rest = z_c
        w4_ok = p_ok
        ka = dve.do(lambda e: e.tensor_copy(a_s, z_s.bitcast(I32)), loaded["src_s"])
        kb_ = dve.do(lambda e: e.tensor_copy(b_s, dst_s), loaded["dst_s"])
        kc = dve.do(lambda e: e.scalar_tensor_tensor(out=a_s, in0=a_s, scalar=float(NP), in1=b_s, op0=ALU.mult, op1=ALU.add),
                    ka, kb_)
        kc = dve.do(lambda e: e.tensor_copy(z_s.bitcast(I32), a_s), kc)
        piece_st = arrival("piece_st")
        for n, mask in enumerate((0xFF0000, 0xFF00, 0xFF)):
            kd = dve.do(lambda e, mask=mask: e.tensor_scalar(b_s.bitcast(I32), z_s.bitcast(I32), mask, None, ALU.bitwise_and), kc, kb_)
            kb_ = dve.do(lambda e, n=n: e.tensor_copy(piece_bf[n], b_s.bitcast(I32)), kd)
            keyd_ok = sp.dma(piece_st, key_d[n].rearrange("(p c) -> p c", p=P), piece_bf[n], kb_)
        seq_st = arrival("seq_st")

        def to_edge_order(c_ap, table, after, store):
            done = None
            for g in range(-(-ET // P)):
                w = min(P, ET - g * P)
                b = 7
                t = flip(bank[b][0:w, 0:P], c_ap[:, g * P:g * P + w], after, bank_free[b], mark=True)
                s = dve.do(lambda e, g=g, w=w: e.tensor_copy(z_t[0:w, g, :], bank[7][0:w, 0:P]), t, seq_done)
                bank_free[b] = [s]
            full = ET // P
            sp.dma(store, table[0:full * P * P].rearrange("(g p e) -> p g e", p=P, e=P), z_t[:, 0:full, :], s)
            return sp.dma(store, table[full * P * P:EP].rearrange("(p e) -> p e", e=P), z_t[0:ET - full * P, full, :], s)

        seq_done = []
        cleared = arrival("cleared")
        adj_flat = adj.rearrange("n c -> (n c)")
        span = P * ZC // 5
        clears = [(adj_flat[i * span:(i + 1) * span].rearrange("(p k) -> p k", p=P), zeros[:, :]) for i in range(5 * NT)] + \
                 [(adj_flat[2 * DUMP + c * EP:2 * DUMP + (c + 1) * EP].rearrange("(p k) -> p k", p=P), zeros[:, 0:SEQ])
                  for c in range(2)]
        begin_flat = begin_d.rearrange("n c -> (n c)")
        begin0 = arrival("begin0")
        for c in range(2):
            tok_begin0 = sp.dma(begin0, begin_flat[c * EP:(c + 1) * EP].rearrange("(p k) -> p k", p=P), zeros[:, 0:SEQ], z0)


        edge_sem = [arrival(f"edge{i}") for i in range(2)]
        keyrow_sem = [arrival(f"keyrow{i}") for i in range(2)]
        he_st = [arrival(f"he_st{i}") for i in range(3)]
        big = {}
        LOADC = EDGE_COLS // BANK

        def load_edges(k):
            c = k * EDGE_COLS
            w = min(EDGE_COLS, EP - c)
            buf, free, after = edge_in.take()
            t1 = sp.dma(edge_sem[k % 2], buf[:, 0:w], given["edgeT"][:, c:c + w], after)
            rbuf, rfree, rafter = key_row.take()
            t2 = sp.dma(keyrow_sem[k % 2], rbuf[:, 0:w], key_d[:, c:c + w], rafter, keyd_ok)
            big[k] = (buf, free, t1, rbuf, rfree, t2)

        def gathers(c):
            buf, free, after = gath.take()
            for j in range(TPC):
                t = pool.gather(gather_sem[c % 3], buf[:, j, :], node_table, src_c[:, c * TPC + j:c * TPC + j + 1],
                                after, table_ok, loaded["src_c"])
            gather_ok.append((buf, free, t))

        NBIG = -(-EP // EDGE_COLS)
        for c in range(3):
            gathers(c)
        MERGE = BANK // (4 * TPC)
        spread_key, chunk_ok, merge_in, hot_in = {}, {}, {}, {}

        def spread_keys(c):
            _, _, _, rbuf, rfree, r_ok = big[c // LOADC]
            eo, kb = (c % LOADC) * BANK, 5 + c % 2
            t = pe.do(lambda e: e.matmul(bank[kb][:, :], ones_bf[:, :], rbuf[:, eo:eo + BANK], start=True, stop=True),
                      r_ok, v_consts, bank_free[kb])
            rfree[:] = [t]
            spread_key[c] = (kb, t)

        def edge_hidden(c):
            ebuf, efree, e_ok, _, _, _ = big[c // LOADC]
            eo, b = (c % LOADC) * BANK, c % 2
            gbuf, gfree, g_ok = gather_ok[c]
            te = pe.do(lambda e: e.matmul(bank[0][:, :], We1_edge[:, :], ebuf[:, eo:eo + BANK], start=True, stop=True),
                       e_ok, tok_small, bank_free[0])
            for j in range(TPC):
                t = flip(bank[1][:, j * P:(j + 1) * P], gbuf[:, j, :], g_ok, bank_free[1], mark=(j == TPC - 1))
            gfree.append(t)
            efree[:] = [t]
            hbuf, hfree, hafter = he.take()
            a = act.do(lambda e: e.activation(hbuf[:, :], bank[0][:, :], ACT.Identity, bias=col["L0_gnn_be1"][:, 0:1]), te, hafter)
            bank_free[0] = [a]
            chunk_ok[c] = [hbuf, hfree, a, t]

        def edge_hot(c):
            obuf, ofree, oafter = onehot.take()
            hbuf, hfree, hafter = hi_hot.take()
            tbuf, tfree, tafter = tile_hot.take()
            i0 = c * TPC
            o1 = dve.do(lambda e: e.tensor_tensor(obuf[:, :, :], along(iota_b[:, :], TPC), across(lohi_bf[:, 0, i0:i0 + TPC], P),
                                                  ALU.is_equal), oafter, hilo_ok, v_consts)
            o2 = dve.do(lambda e: e.tensor_tensor(hbuf[:, :, :], along(iota_b[:, 0:NT], TPC),
                                                  across(lohi_bf[:, 1, i0:i0 + TPC], NT), ALU.is_equal), hafter)
            four = [P, TPC, 4, NT]
            o3 = dve.do(lambda e: e.tensor_tensor(tbuf[:, :, :, :], hbuf[:, :, :].unsqueeze(2).broadcast_to(four),
                                                  w4_c[:, i0:i0 + TPC, :].unsqueeze(3).broadcast_to(four), ALU.mult), o2, w4_ok, tafter)
            hfree.append(o3)
            hot_in[c] = (obuf, ofree, tbuf, tfree, o1, o3)

        def degrees(c):
            obuf, ofree, tbuf, tfree, o1, o3 = hot_in.pop(c)
            for j in range(TPC):
                d = pe.do(lambda e, j=j: e.matmul(
                    bank[4][:, 0:4 * NT], obuf[:, j, :], tbuf[:, j, :, :].rearrange("p a b -> p (a b)"),
                    start=(c == 0 and j == 0), stop=(c == CH - 1 and j == TPC - 1)), o1, o3,
                    bank_free[4] if c == 0 else None, mark=(j == TPC - 1))
            ofree.append(d)
            tfree.append(d)
            return d

        def equal_keys(c):
            kb, t = spread_key.pop(c)
            merge_in[c] = []
            for j in range(TPC):
                i = c * TPC + j
                sbuf, sfree, safter = same.take()
                u = dve.do(lambda e, j=j, i=i, sbuf=sbuf: e.scalar_tensor_tensor(
                    out=sbuf[:, :], in0=bank[kb][:, j * P:(j + 1) * P], scalar=key_c[:, i:i + 1], in1=tri_incl[:, :],
                    op0=ALU.is_equal, op1=ALU.mult, accum_out=later_c[:, i:i + 1]), t, safter, hilo_ok)
                merge_in[c].append((sbuf, sfree, u))
            bank_free[kb] = [u]
            return u

        def merge(c):
            for j, (sbuf, sfree, u) in enumerate(merge_in.pop(c)):
                q, i = ((c % MERGE) * TPC + j) * 4, c * TPC + j
                m = pe.do(lambda e, sbuf=sbuf, q=q, i=i: e.matmul(bank[7][:, q:q + 4], sbuf[:, :], w4_c[:, i, :],
                                                                  start=True, stop=True), u, w4_ok, bank_free[7])
                sfree.append(m)
            if c % MERGE == MERGE - 1 or c == CH - 1:
                i0, ni = (c // MERGE) * MERGE * TPC, (c % MERGE + 1) * TPC
                return (i0, ni, m)

        def keep_pairs(i0, ni, m):
            got, to = bank[7][:, 0:4 * ni].rearrange("p (t c) -> p t c", c=4), pair_c[:, i0:i0 + ni, :]
            dve.do(lambda e: e.tensor_copy(to[:, :, 1], got[:, :, 3]), m)
            ok = dve.do(lambda e: e.tensor_copy(to[:, :, 0], got[:, :, 2]))
            for n in (1, 0):
                ok = dve.do(lambda e, n=n: e.tensor_tensor(to[:, :, 0], to[:, :, 0], got[:, :, n], ALU.add), ok)
            bank_free[7] = [ok]
            return ok

        def edge_logit(c):
            hbuf, hfree, he_ok, _ = chunk_ok[c]
            for j in range(TPC):
                i = c * TPC + j
                zb = 2 + i // BANK
                zt = pe.do(lambda e, j=j, i=i, zb=zb: e.matmul(
                    bank[zb][:, i % BANK:i % BANK + 1], hbuf[:, j * P:(j + 1) * P], col["We2_edge"][:, 0:1],
                    start=True, stop=True), he_ok, bank_free[zb] if i % BANK == 0 else None, mark=(j == TPC - 1))
            hfree.append(zt)
            return zt

        load_edges(0)
        load_edges(1)
        spread_keys(0)
        for c in range(CH + 1):
            if c < CH:
                if c % LOADC == 0 and 0 < c // LOADC < NBIG - 1:
                    load_edges(c // LOADC + 1)
                edge_hidden(c)
                if c + 1 < CH:
                    spread_keys(c + 1)
                edge_hot(c)
                u = equal_keys(c)
            if c:
                pending = merge(c - 1)
                d = degrees(c - 1)
                zt = edge_logit(c - 1)
                if pending:
                    pair_ok = keep_pairs(*pending)
            if c < CH:
                hbuf, hfree, a, t = chunk_ok[c]
                a = dve.do(lambda e, hbuf=hbuf: e.tensor_tensor(hbuf[:, :], hbuf[:, :], bank[1][:, :], ALU.add), a, t)
                bank_free[1] = [a]
                chunk_ok[c][2] = leaky(hbuf[:, :], a)
                hfree.append(act.dma(he_st[he.at], he_d[c], hbuf[:, :], chunk_ok[c][2]))
                if c + 3 < CH:
                    gathers(c + 3)
                if clears:
                    tok_adj0 = sp.dma(cleared, *clears.pop(0), z0)
        for zb in range(2):
            w = min(BANK, ET - zb * BANK)
            zc_ok = dve.do(lambda e, zb=zb, w=w: e.tensor_copy(z_c[:, zb * BANK:zb * BANK + w], bank[2 + zb][:, 0:w]), zt)
            bank_free[2 + zb] = [zc_ok]
        zd_ok = to_edge_order(z_c, z_d.rearrange("e c -> (e c)"), zc_ok, seq_st)
        zs_ld = arrival("zs_ld")
        zs_ok = sp.dma(zs_ld, z_s, z_d.rearrange("(p c) o -> p (c o)", p=P), zd_ok)

        cnt, wdeg, tot, pre = small[:, 1, :], small[:, 2, :], small[:, 3, :], small[:, 4, :]
        s1 = dve.do(lambda e: e.tensor_copy(cnt, bank[4][:, 3 * NT:4 * NT]), d)
        s2 = dve.do(lambda e: e.tensor_scalar(wdeg, bank[4][:, 2 * NT:3 * NT], 1.0, None, ALU.add))
        for n in (1, 0):
            s2 = dve.do(lambda e, n=n: e.tensor_tensor(wdeg, wdeg, bank[4][:, n * NT:(n + 1) * NT], ALU.add), s2)
        bank_free[4] = [s2]
        t = pe.do(lambda e: e.matmul(bank[4][:, 0:NT], ones[:, :], cnt, start=True, stop=True), s1, s2)
        t2 = pe.do(lambda e: e.matmul(bank[4][:, NT:2 * NT], tri_less[:, :], cnt, start=True, stop=True))
        s3 = dve.do(lambda e: e.tensor_copy(tot, bank[4][:, 0:NT]), t2)
        s4 = dve.do(lambda e: e.tensor_copy(pre, bank[4][:, NT:2 * NT]))
        bank_free[4] = [s4]
        inc, w5, w6 = small[:, 5, :], small[:, 6, :], small[:, 7, :]
        s5 = dve.do(lambda e: e.tensor_tensor_scan(inc, ones[:, 0:NT], tot, 0.0, ALU.mult, ALU.add), s3)
        s6 = dve.do(lambda e: e.tensor_tensor(inc, inc, tot, ALU.subtract), s5)
        s7 = dve.do(lambda e: e.tensor_tensor(inc, inc, pre, ALU.add), s6, s4)
        s8 = dve.do(lambda e: e.tensor_scalar(has[:, :], cnt, 0.0, None, ALU.is_gt), s1)
        s9 = dve.do(lambda e: e.tensor_tensor(w5, inc, cnt, ALU.add), s7)
        s10 = dve.do(lambda e: e.tensor_scalar(w5, w5, -1.0, 0.0, ALU.add, ALU.max), s9)
        end_ok = dve.do(lambda e: e.tensor_copy(end_i[:, :], w5), s10)
        s11 = dve.do(lambda e: e.tensor_copy(w6, node_iota[:, :]), consts)
        s12 = dve.do(lambda e: e.tensor_tensor(inc, inc, w6, ALU.subtract), s11, s9)
        s13 = dve.do(lambda e: e.tensor_tensor(inc, inc, has[:, :], ALU.mult), s12, s8)
        s14 = dve.do(lambda e: e.tensor_tensor(inc, inc, w6, ALU.add), s13)
        begin_ok = dve.do(lambda e: e.tensor_copy(begin_i[:, :], inc), s14)
        s15 = dve.do(lambda e: e.tensor_scalar(dinv[:, :], cnt, 1.0, None, ALU.add), s14)
        s16 = dve.do(lambda e: e.tensor_scalar(w5, wdeg, 0.0, None, ALU.is_gt), s2, end_ok)
        s17 = dve.do(lambda e: e.tensor_scalar(wdeg, wdeg, 1e-30, None, ALU.max), s16)
        s18 = act.do(lambda e: e.activation(dinv[:, :], dinv[:, :], ACT.Sqrt), s15)
        s19 = act.do(lambda e: e.activation(wdeg, wdeg, ACT.Sqrt), s17)
        s20 = dve.do(lambda e: e.reciprocal(dinv[:, :], dinv[:, :]), s18)
        s21 = dve.do(lambda e: e.reciprocal(dis[:, :], wdeg), s19)
        dis_ok = dve.do(lambda e: e.tensor_tensor(dis[:, :], dis[:, :], w5, ALU.mult), s21)

        dump_i = z_t.rearrange("p g e -> p (g e)")[:, 0:ET].bitcast(I32)
        dump_f = lo_c
        q0 = pool.do(lambda e: e.iota(dump_i, pattern=[[P, ET]], base=DUMP, channel_multiplier=1), zd_ok)
        q1 = dve.do(lambda e: e.tensor_copy(dump_f, dump_i), q0, d)
        q2 = dve.do(lambda e: e.tensor_scalar(later_c, later_c, 1.0, None, ALU.is_equal), u)
        q3 = dve.do(lambda e: e.tensor_tensor(key_c, key_c, dump_f, ALU.subtract), q1)
        q4 = dve.do(lambda e: e.tensor_tensor(key_c, key_c, later_c, ALU.mult), q2, q3)
        q5 = dve.do(lambda e: e.tensor_tensor(key_c, key_c, dump_f, ALU.add), q4)
        target_ok = dve.do(lambda e: e.tensor_copy(target, key_c), q5)
        fl = arrival("fl")
        dst0 = given["dst"][1:EP + 1].rearrange("(t p) -> t p", p=P)
        fi = flag_row[:, 2, :].bitcast(I32)
        pc = Arrival(seq_st.sem)
        f1 = sp.dma(fl, flag_row[:, 0, :].bitcast(I32), given["tile_first"])
        f1 = sp.dma(fl, flag_row[:, 1, :].bitcast(I32), given["tile_last"])
        f2 = dve.do(lambda e: e.tensor_copy(flag_row[:, 2, :], flag_row[:, 0, :].bitcast(I32)), f1)
        f3 = dve.do(lambda e: e.tensor_copy(flag_row[:, 0, :], flag_row[:, 1, :].bitcast(I32)), f2)
        f4 = dve.do(lambda e: e.tensor_tensor(flag_row[:, 1, 0:ET - 2], flag_row[:, 0, 0:ET - 2], flag_row[:, 2, 2:ET],
                                              ALU.is_equal), f3)
        f5 = dve.do(lambda e: e.tensor_reduce(flag_f[:, :], flag_row[:, 1, 0:ET - 2], AX_X, ALU.max), f4)
        flag_ok = dve.do(lambda e: e.tensor_copy(flag_i[:, :], flag_f[:, :]), f5)

        adj_done = arrival("adj_done")
        evens, odds = list(range(0, ET, 2)), list(range(1, ET, 2))
        flag_reg = []

        def start_scatter():
            pool.wait(flag_ok)
            pool.ops.append(lambda e: flag_reg.append(e.value_load(flag_i[0:1, 0:1], min_val=0, max_val=1)))

        def scatter_tile(i):
            before = adj_done.value
            if i == odds[0]:
                pool.wait((adj_done.sem, before))
            elif before:
                def guarded(e, v=before):
                    with e.If(flag_reg[0] > 0):
                        e.wait_ge(adj_done.sem, v)
                pool.ops.append(guarded)
            return pool.scatter(adj_done, adj, target[:, i:i + 1], pair_c[:, i, :], target_ok, pair_ok, tok_adj0, flag_ok,
                                add=True)

        k0 = dve.do(lambda e: e.tensor_copy(a_s, dst_s), loaded["dst_s"])
        k1 = dve.do(lambda e: e.tensor_copy(b_s, prev_s), loaded["prev_s"])
        k2 = dve.do(lambda e: e.tensor_tensor(keep_s, a_s, b_s, ALU.is_equal), k0, k1)
        k3 = dve.do(lambda e: e.tensor_copy(keep_bf, keep_s), k2)
        keepst = arrival("keepst")
        keepd_ok = sp.dma(keepst, keep_d.rearrange("(p c) -> p c", p=P), keep_bf, k3)
        k4 = dve.do(lambda e: e.tensor_scalar(reset_s, keep_s, -1.0, FAR, ALU.add, ALU.mult), k2)

        def segscan(out_ap, data0, data1, op0, op1, neutral, *after):
            i = after
            s = dve.do(lambda e: e.tensor_tensor_scan(out_ap, data0, data1, neutral, op0, op1), k4, *i)
            s = dve.do(lambda e: e.tensor_copy(ends[:, 0:1], out_ap[:, SEQ - 1:SEQ]), s)
            s = dve.do(lambda e: e.tensor_reduce(ends[:, 1:2], data0, AX_X, ALU.min))
            t = pe.do(lambda e: e.matmul(bank[7][0:1, 0:P], ends[:, 0:1], ident[:, :], start=True, stop=True), s, bank_free[7])
            t = pe.do(lambda e: e.matmul(bank[7][0:1, P:2 * P], ends[:, 1:2], ident[:, :], start=True, stop=True))
            s = dve.do(lambda e: e.tensor_copy(rows1[:, :], bank[7][0:1, 0:2 * P]), t)
            s0 = dve.do(lambda e: e.memset(carry_row[:, 0:1], neutral))
            s = dve.do(lambda e: e.tensor_tensor_scan(carry_row[:, 1:P + 1], rows1[:, P:2 * P], rows1[:, 0:P], neutral, op0, op1), s)
            t = pe.do(lambda e: e.matmul(bank[7][:, 2 * P:2 * P + 1], carry_row[0:1, 0:P], ones[0:1, 0:1],
                                         start=True, stop=True), s, s0)
            s = dve.do(lambda e: e.tensor_copy(carry_col[:, :], bank[7][:, 2 * P:2 * P + 1]), t)
            bank_free[7] = [s]
            return dve.do(lambda e: e.tensor_tensor_scan(out_ap, data0, data1, carry_col[:, 0:1], op0, op1), s)

        zm_ok = segscan(a_s, reset_s, z_s, ALU.add, ALU.max, -FAR, zs_ok, k2)
        zmst = arrival("zmst")
        zmd_ok = sp.dma(zmst, zmax_d.rearrange("(p c) o -> p (c o)", p=P), a_s, zm_ok)
        zmg = arrival("zmg")
        z_node = small[:, 5, :]
        start_scatter()
        for i in evens[:70]:
            scatter_tile(i)
        for i in range(NT):
            zg_ok = pool.gather(zmg, z_node[:, i:i + 1], zmax_d, end_i[:, i:i + 1], zmd_ok, end_ok, begin_ok)
        pair_n = sb("pair_n", [P, NT, 2])
        n1 = dve.do(lambda e: e.tensor_copy(pair_n[:, :, 0], t_node), tn_ok)
        n2 = dve.do(lambda e: e.tensor_tensor(z_node, z_node, t_node, ALU.add), zg_ok, n1)
        n3 = dve.do(lambda e: e.scalar_tensor_tensor(out=pair_n[:, :, 1], in0=z_node, scalar=SLOPE, in1=z_node,
                                                     op0=ALU.mult, op1=ALU.max), n2)
        bst = arrival("bst")
        for i in evens[70:120]:
            scatter_tile(i)
        for i in range(NT):
            bd_ok = pool.scatter(bst, begin_d, begin_i[:, i:i + 1], pair_n[:, i, :], n3, n1, begin_ok, tok_begin0)
        tls = arrival("tls")
        tl_ok = sp.dma(tls, tl_s, begin_d[0:EP, :].rearrange("(p k) c -> p k c", p=P), bd_ok, keyd_ok)
        tnode_s = segscan(b_s, keep_s, tl_s[:, :, 0], ALU.mult, ALU.add, 0.0, tl_ok)
        e1 = dve.do(lambda e: e.tensor_tensor(z_s, z_s, b_s, ALU.add), tnode_s)
        e2 = leaky(z_s, e1)
        lmax_s = segscan(b_s, keep_s, tl_s[:, :, 1], ALU.mult, ALU.add, 0.0, e1)
        e3 = dve.do(lambda e: e.tensor_tensor(z_s, z_s, b_s, ALU.subtract), lmax_s, e2)
        e4 = act.do(lambda e: e.activation(z_s, z_s, ACT.Exp), e3)
        exst = arrival("exst")
        rest, r_ok = z_s, e4
        for n in range(3):
            p_ok = dve.do(lambda e, n=n, rest=rest: e.tensor_copy(piece_bf[n], rest), r_ok, keyd_ok)
            exd_ok = sp.dma(exst, ex_d[n].rearrange("(p c) -> p c", p=P), piece_bf[n], p_ok)
            if n < 2:
                r_ok = dve.do(lambda e, n=n, rest=rest: e.tensor_tensor(a_s, rest, piece_bf[n], ALU.subtract), p_ok, zmd_ok)
                rest = a_s
        es_ok = segscan(b_s, keep_s, z_s, ALU.mult, ALU.add, 0.0, e4)
        esst = arrival("esst")
        esd_ok = sp.dma(esst, exsum_d.rearrange("(p c) o -> p (c o)", p=P), b_s, es_ok)

        for i in evens[120:] + odds[:200]:
            scatter_tile(i)

        he_in = Slots([gath.buffers[0].rearrange("p a b -> p (a b)"), gath.buffers[1].rearrange("p a b -> p (a b)"),
                       gath.buffers[2].rearrange("p a b -> p (a b)"), onehot_space])
        for i in range(3):
            he_in.free[i] = [gather_ok[c][1] for c in range(CH - 3, CH)]
        he_in.free[3] = [d]
        he_in_sem = [arrival(f"he_in{i}") for i in range(4)]
        prod = Slots([sb(f"prod{i}", [P, BANK]) for i in range(2)])
        run = Slots([edge_space[:, i * BANK:(i + 1) * BANK] for i in range(3)])
        run.free = [[edge_in.free[0], edge_in.free[1]] for _ in range(3)]
        flipped = Slots([b[:, :] for b in he.buffers])
        for i in range(3):
            flipped.free[i] = [he.free[0], he.free[1], he.free[2]]
        fl_st = [arrival(f"fl_st{i}") for i in range(3)]
        ex_row, keep_row = Slots([b for b in key_row.buffers]), Slots([sb(f"keep_row{i}", [1, EDGE_COLS], BF16) for i in range(2)])
        for i in range(2):
            ex_row.free[i] = [key_row.free[0], key_row.free[1]]
        exr_sem = [arrival(f"exr{i}") for i in range(2)]
        kpr_sem = [arrival(f"kpr{i}") for i in range(2)]
        rows, fetched, spread = {}, {}, {}
        he_all = [(s.sem, s.value) for s in he_st]

        def fetch_rows(k):
            c = k * EDGE_COLS
            w = min(EDGE_COLS, EP - c)
            a, afree, aafter = ex_row.take()
            t1 = sp.dma(exr_sem[k % 2], a[:, 0:w], ex_d[:, c:c + w], aafter, exd_ok)
            b, bfree, bafter = keep_row.take()
            t2 = sp.dma(kpr_sem[k % 2], b[:, 0:w], keep_d[c:c + w].unsqueeze(0), bafter, keepd_ok)
            rows[k] = (a, afree, t1, b, bfree, t2)

        def fetch_he(c):
            buf, free, after = he_in.take()
            fetched[c] = (buf, free, sp.dma(he_in_sem[c % 4], buf, he_d[c], after, he_all))

        def spread_rows(c):
            a, afree, t1, b, bfree, t2 = rows[c // LOADC]
            o = (c % LOADC) * BANK
            eb, kb = c % 2, 2 + c % 2
            u = pe.do(lambda e: e.matmul(bank[eb][:, :], ones_bf[:, :], a[:, o:o + BANK], start=True, stop=True), t1, bank_free[eb])
            v = pe.do(lambda e: e.matmul(bank[kb][:, :], ones_bf[0:1, :], b[0:1, o:o + BANK], start=True, stop=True), t2, bank_free[kb])
            afree[:] = [u]
            bfree[:] = [v]
            spread[c] = (eb, kb, u, v)

        fetch_rows(0)
        fetch_rows(1)
        for c in range(3):
            fetch_he(c)
        spread_rows(0)
        last_run = None
        for c in range(CH):
            k = c // LOADC
            if c % LOADC == 0 and 0 < k and k + 1 < NBIG:
                fetch_rows(k + 1)
            if c + 3 < CH:
                fetch_he(c + 3)
            if c + 1 < CH:
                spread_rows(c + 1)
            hbuf, hfree, h_in = fetched[c]
            eb, kb, u, v = spread[c]
            pbuf, pfree, pafter = prod.take()
            m = dve.do(lambda e, pbuf=pbuf, hbuf=hbuf, eb=eb: e.tensor_tensor(pbuf[:, :], bank[eb][:, :], hbuf, ALU.mult), u, h_in, pafter)
            hfree.append(m)
            bank_free[eb] = [m]
            rb, rfree2, rafter = run.take()
            init = 0.0 if last_run is None else last_run[:, BANK - 1:BANK]
            sc = dve.do(lambda e, rb=rb, kb=kb, pbuf=pbuf, init=init: e.tensor_tensor_scan(
                rb[:, :], bank[kb][:, :], pbuf[:, :], init, ALU.mult, ALU.add), m, v, rafter)
            last_run = rb
            pfree.append(sc)
            bank_free[kb] = [sc]
            tb = 4 + c % 2
            for j in range(TPC):
                t = flip(bank[tb][:, j * P:(j + 1) * P], rb[:, j * P:(j + 1) * P], sc, bank_free[tb], mark=(j == TPC - 1))
            rfree2.append(t)
            fb, ffree, fafter = flipped.take()
            s = act.do(lambda e, fb=fb, tb=tb: e.copy(fb, bank[tb][:, :]), t, fafter)
            bank_free[tb] = [s]
            ffree.append(act.dma(fl_st[c % 3], hesum_d[c * BANK:(c + 1) * BANK, :].rearrange("(j p) f -> p j f", p=P),
                                 fb.rearrange("p (j f) -> p j f", f=P), s))
            scan_tok = sc
        run_all = [(s.sem, s.value) for s in fl_st]
        agg = Slots([h])[0] if False else h
        ag = arrival("ag")
        sg = arrival("sg")
        s_node = small[:, 6, :]
        for i in range(NT):
            sg_ok = pool.gather(sg, s_node[:, i:i + 1], exsum_d, end_i[:, i:i + 1], esd_ok, s14)
        for i in range(NT):
            ag_ok = pool.gather(ag, h[:, i, :], hesum_d, end_i[:, i:i + 1], run_all, hT_ok, t)
        for i in odds[200:]:
            scatter_tile(i)
        adj_ok = (adj_done.sem, adj_done.value)

        r1 = dve.do(lambda e: e.reciprocal(s_node, s_node), sg_ok)
        r2 = dve.do(lambda e: e.tensor_tensor(s_node, s_node, has[:, :], ALU.mult), r1)
        diag = Slots(diag_space)
        for g, (c, w) in enumerate(GROUPS):
            b = g % 2
            for j in range(w // P):
                i = c // P + j
                dbuf, dfree, dafter = diag.take()
                dd = dve.do(lambda e, dbuf=dbuf, i=i: e.tensor_scalar(dbuf[:, :], ident[:, :], s_node[:, i:i + 1], None, ALU.mult),
                            r2, dafter)
                t = pe.do(lambda e, b=b, j=j, i=i, dbuf=dbuf: e.matmul(bank[b][:, j * P:(j + 1) * P], h[:, i, :], dbuf[:, :],
                                                                       start=True, stop=True), dd, ag_ok, bank_free[b])
                dfree.append(t)
            agT_ok = act.do(lambda e, b=b, c=c, w=w: e.copy(featT[:, c:c + w], bank[b][:, 0:w]), t)
            bank_free[b] = [agT_ok]
        agg_read = t
        has_bits = arena[0:1, 0:NP]
        for g, (c, w) in enumerate(GROUPS):
            b = 2 + g % 2
            for j in range(w // P):
                t = pe.do(lambda e, b=b, j=j, c=c: e.matmul(bank[b][0:1, j * P:(j + 1) * P], has[:, c // P + j:c // P + j + 1],
                                                            ident[:, :], start=True, stop=True), s8, bank_free[b],
                          mark=(j == w // P - 1))
            hr_ok = dve.do(lambda e, b=b, c=c, w=w: e.tensor_copy(has_bits[:, c:c + w], bank[b][0:1, 0:w]), t)
            bank_free[b] = [hr_ok]
        wk_free = [[], []]
        for g, (c, w) in enumerate(GROUPS):
            k = g % 2
            b, b2, b3 = k, 2 + k, 4 + k
            ctxT, neg = run.buffers[k], prod.buffers[k]
            t = pe.do(lambda e, b=b, c=c, w=w: e.matmul(bank[b][:, 0:w], W["L0_gnn_Wet"][:, :], featT[:, c:c + w],
                                                        start=True, stop=False), agT_ok, bank_free[b])
            t = pe.do(lambda e, b=b, c=c, w=w: e.matmul(bank[b][:, 0:w], bet_row[0:1, :], has_bits[0:1, c:c + w],
                                                        start=False, stop=True), hr_ok)
            a = dve.do(lambda e, b=b, w=w, neg=neg: e.tensor_scalar(neg[:, 0:w], bank[b][:, 0:w], 0.0, None, ALU.min), t, wk_free[k], scan_tok)
            e_ = act.do(lambda e, w=w, neg=neg: e.activation(neg[:, 0:w], neg[:, 0:w], ACT.Exp), a)
            a = dve.do(lambda e, b=b, w=w, ctxT=ctxT: e.tensor_scalar(ctxT[:, 0:w], bank[b][:, 0:w], 0.0, None, ALU.max))
            bank_free[b] = [a]
            a = dve.do(lambda e, w=w, ctxT=ctxT, neg=neg: e.scalar_tensor_tensor(out=ctxT[:, 0:w], in0=neg[:, 0:w], scalar=-1.0,
                                                                                 in1=ctxT[:, 0:w], op0=ALU.add, op1=ALU.add), a, e_)
            t = pe.do(lambda e, b2=b2, w=w, ctxT=ctxT: e.matmul(bank[b2][:, 0:w], W["W1_context"][:, :], ctxT[:, 0:w],
                                                                start=True, stop=False), a, bank_free[b2])
            t = pe.do(lambda e, b2=b2, c=c, w=w: e.matmul(bank[b2][:, 0:w], W["W1_node"][:, :], hvT[:, c:c + w],
                                                          start=False, stop=True))
            o = act.do(lambda e, b2=b2, w=w, neg=neg: e.activation(neg[:, 0:w], bank[b2][:, 0:w], ACT.Relu,
                                                                   bias=col["L0_gnn_b1"][:, 0:1]), t)
            bank_free[b2] = [o]
            for j in range(w // P):
                t = pe.do(lambda e, b3=b3, j=j, neg=neg: e.matmul(bank[b3][:, j * P:(j + 1) * P], neg[:, j * P:(j + 1) * P],
                                                                  W["L0_gnn_W2"][:, :], start=True, stop=True), o, bank_free[b3],
                          mark=(j == w // P - 1))
            n = w // P
            a = dve.do(lambda e, b3=b3, n=n, k=k: e.tensor_tensor(work[:, k, 0:n * P].rearrange("p (j f) -> p j f", f=P),
                                                                  bank[b3][:, 0:n * P].rearrange("p (j f) -> p j f", f=P),
                                                                  along(row["L0_gnn_b2"][:, :], n), ALU.add), t)
            bank_free[b3] = [a]
            x_ok = dve.do(lambda e, n=n, k=k, c=c: e.scalar_tensor_tensor(
                out=x[:, c // P:c // P + n, :].rearrange("p j f -> p (j f)"), in0=work[:, k, 0:n * P], scalar=0.0,
                in1=x[:, c // P:c // P + n, :].rearrange("p j f -> p (j f)"), op0=ALU.max, op1=ALU.add), a)
            wk_free[k] = [t, a]

        def scaled(dst, scale, after):
            out_tok = []
            for c, w in GROUPS:
                n = w // P
                out_tok.append(dve.do(lambda e, c=c, n=n: e.tensor_tensor(
                    dst[:, c // P:c // P + n, :], dst[:, c // P:c // P + n, :],
                    across(scale[:, c // P:c // P + n], P), ALU.mult), after))
            return out_tok[-1]

        edge_over = [adj_ok, exd_ok, esd_ok, keepd_ok, pe.last(), act.last(), dve.last()]
        used[0] = 0
        mat = Slots([carve(NP) for _ in range(8)])
        mat_sem = [arrival(f"mat{i}") for i in range(8)]
        mat.free = [list(edge_over) for _ in mat.buffers]
        pairs = Slots([arena[:, i * 2 * NP:(i + 1) * 2 * NP].rearrange("p (n c) -> p n c", c=2) for i in range(2)])
        pairs.free = [list(edge_over) for _ in range(2)]
        parts = Slots([arena[:, (4 + i) * NP:(5 + i) * NP] for i in range(4)])
        parts.free = [list(edge_over) for _ in range(4)]
        turned = Slots([he.buffers[i] for i in range(3)])
        turned.free = [list(run_all) for _ in range(3)]
        pair_sem = [arrival(f"pair{i}") for i in range(2)]
        part_st = [arrival(f"part_st{i}") for i in range(4)]
        turn_st = [arrival(f"turn_st{i}") for i in range(3)]

        h_ok = layernorm([x_ok], [agg_read])
        h_ok = scaled(h, dis, [h_ok, dis_ok])

        def product_tile(i, m_ap, m_ok, feat_ok):
            for g, (c, w) in enumerate(GROUPS):
                t = pe.do(lambda e, g=g, c=c, w=w: e.matmul(bank[g][:, 0:w], h[:, i, :], m_ap[:, c:c + w],
                                                            start=(i == 0), stop=(i == NT - 1)),
                          m_ok, feat_ok, bank_free[g] if i == 0 else None, mark=(g == len(GROUPS) - 1))
            return t

        def load_pair(i):
            buf, free, after = pairs.take()
            return buf, free, sp.dma(pair_sem[i % 2], buf, adj[i * P * NP:(i + 1) * P * NP, :].rearrange("(p n) c -> p n c", p=P),
                                     after, adj_ok)

        nxt = load_pair(0)
        for i in range(NT):
            pbuf, pfree, p_ok = nxt
            if i + 1 < NT:
                nxt = load_pair(i + 1)
            wbuf, wfree, wafter = parts.take()
            cbuf, cfree, cafter = parts.take()
            ws, cs = (parts.at - 1) % 4, parts.at
            w_ok = dve.do(lambda e, wbuf=wbuf, pbuf=pbuf: e.tensor_copy(wbuf, pbuf[:, :, 0]), p_ok, wafter)
            c_ok = act.do(lambda e, cbuf=cbuf, pbuf=pbuf: e.copy(cbuf, pbuf[:, :, 1]), p_ok, cafter)
            d1 = dve.do(lambda e, wbuf=wbuf, i=i: e.tensor_tensor(wbuf[:, i * P:(i + 1) * P], wbuf[:, i * P:(i + 1) * P],
                                                                  ident[:, :], ALU.add), w_ok)
            d2 = dve.do(lambda e, cbuf=cbuf, i=i: e.tensor_tensor(cbuf[:, i * P:(i + 1) * P], cbuf[:, i * P:(i + 1) * P],
                                                                  ident[:, :], ALU.add), c_ok)
            st1 = act.dma(part_st[ws], weight_t[i * P:(i + 1) * P, :], wbuf, d1)
            st2 = act.dma(part_st[cs], count_t[i * P:(i + 1) * P, :], cbuf, d2)
            t = product_tile(i, wbuf, d1, h_ok)
            wfree.extend([st1, t])
            cfree.append(st2)
            for g, (c, w) in enumerate(GROUPS):
                for j in range(w // P):
                    t = flip(bank[7][:, j * P:(j + 1) * P], pbuf[:, c + j * P:c + (j + 1) * P, 0], p_ok, bank_free[7], mark=(j == w // P - 1))
                tb, tfree, tafter = turned.take()
                ts = turned.at
                s = (dve if g % 2 else act).do(lambda e, tb=tb, w=w, dv=g % 2: (e.tensor_copy if dv else e.copy)(tb[:, 0:w], bank[7][:, 0:w]), t, tafter)
                bank_free[7] = [s]
                tfree.append(sp.dma(turn_st[ts], weight_n[c:c + w, i * P:(i + 1) * P].rearrange("(j p) s -> p j s", p=P),
                                    tb[:, 0:w].rearrange("p (j s) -> p j s", s=P), s))
            pfree.extend([t, w_ok, c_ok])
        prod_ok = (pe.sem, pe.count)
        weight_t_ok = count_t_ok = [(s.sem, s.value) for s in part_st]
        weight_n_ok = [(s.sem, s.value) for s in turn_st]
        for i in range(4):
            mat.free[i] = pairs.free[0] + pairs.free[1]
            mat.free[4 + i] = parts.free[i]
        mat_queue = []

        def fetch_mat(matrix, i, ready):
            buf, free, after = mat.take()
            mat_queue.append((buf, free, sp.dma(mat_sem[mat.at], buf, matrix[i * P:(i + 1) * P, :], after, ready)))

        plan = [(weight_t, i, weight_t_ok) for _ in range(2) for i in range(NT)] + \
               [(count_t, i, count_t_ok) for _ in range(3) for i in range(NT)] + \
               [(weight_n, i, weight_n_ok) for _ in range(3) for i in range(NT)]
        plan.reverse()
        for _ in range(8):
            fetch_mat(*plan.pop())

        def product(feat_ok):
            for i in range(NT):
                buf, free, ok = mat_queue.pop(0)
                t = product_tile(i, buf, ok, feat_ok)
                free.append(t)
                if plan:
                    fetch_mat(*plan.pop())
            return t

        def evacuate(t):
            for g, (c, w) in enumerate(GROUPS):
                q = (act, dve)[g % 2]
                s = q.do(lambda e, g=g, c=c, w=w: (e.tensor_copy if g % 2 else e.copy)(featT[:, c:c + w], bank[g][:, 0:w]), t)
                bank_free[g] = [s]
            return [act.last(), dve.last()]

        def gcn_out(weight, scale, bias, slope, last):
            toks = []
            for g, (c, w) in enumerate(GROUPS):
                n, b, k = w // P, g, g % 2
                for j in range(n):
                    t = pe.do(lambda e, b=b, j=j, c=c: e.matmul(bank[b][:, j * P:(j + 1) * P], featT[:, c + j * P:c + (j + 1) * P],
                                                                weight[:, :], start=True, stop=True), featT_ok, bank_free[b],
                              mark=(j == n - 1))
                v3 = work[:, k, 0:w].rearrange("p (j f) -> p j f", f=P)
                h3 = h[:, c // P:c // P + n, :]
                sc3 = across(scale[:, c // P:c // P + n], P)
                a = dve.do(lambda e, v3=v3, b=b, w=w, sc3=sc3: e.tensor_tensor(v3, bank[b][:, 0:w].rearrange("p (j f) -> p j f", f=P),
                                                                               sc3, ALU.mult), t)
                bank_free[b] = [a]
                a = dve.do(lambda e, v3=v3, n=n: e.tensor_tensor(v3, v3, along(bias[:, :], n), ALU.add), a)
                if slope is None:
                    if last:
                        x3 = x[:, c // P:c // P + n, :]
                        a = dve.do(lambda e, v3=v3, x3=x3, w=w, k=k: e.scalar_tensor_tensor(
                            out=x3, in0=v3, scalar=0.0, in1=x3, op0=ALU.max, op1=ALU.add), a)
                    else:
                        a = dve.do(lambda e, v3=v3, h3=h3, sc3=sc3: e.scalar_tensor_tensor(
                            out=h3, in0=v3, scalar=0.0, in1=sc3, op0=ALU.max, op1=ALU.mult), a)
                else:
                    a2 = dve.do(lambda e, v3=v3, h3=h3, n=n: e.scalar_tensor_tensor(
                        out=h3, in0=v3, scalar=0.0, in1=along(slope[:, :], n), op0=ALU.min, op1=ALU.mult), a)
                    a = dve.do(lambda e, v3=v3, h3=h3: e.scalar_tensor_tensor(
                        out=h3, in0=v3, scalar=0.0, in1=h3, op0=ALU.max, op1=ALU.add), a2)
                    if last:
                        x3 = x[:, c // P:c // P + n, :]
                        a = dve.do(lambda e, h3=h3, x3=x3: e.tensor_tensor(x3, x3, h3, ALU.add), a)
                    else:
                        a = dve.do(lambda e, h3=h3, sc3=sc3: e.tensor_tensor(h3, h3, sc3, ALU.mult), a)
                toks.append(a)
            return toks[-1]

        featT_ok = evacuate(prod_ok)
        for l in range(3):
            done = gcn_out(W[f"L1_gnn_W{l + 1}"], dis, row[f"L1_gnn_b{l + 1}"], row[f"L1_gnn_a{l + 1}"], l == 2)
            if l < 2:
                featT_ok = evacuate(product(done))
        h_ok = layernorm([done], [pe.last()])
        done = scaled(h, dinv, [h_ok, s20])
        for l in range(3):
            featT_ok = evacuate(product(done))
            done = gcn_out(W[f"L2_gnn_W{l}"], dinv, row[f"L2_gnn_b{l}"], None, l == 2)
        a = dve.do(lambda e: e.tensor_reduce(carry_col[:, :], alpha[:, :], AX_X, ALU.max), tok_small)
        a = dve.do(lambda e: e.tensor_scalar(alpha[:, :], alpha[:, :], carry_col[:, 0:1], None, ALU.subtract), a)
        a = act.do(lambda e: e.activation(alpha[:, :], alpha[:, :], ACT.Exp), a)
        a = dve.do(lambda e: e.tensor_reduce(carry_col[:, :], alpha[:, :], AX_X, ALU.add), a)
        a = dve.do(lambda e: e.reciprocal(carry_col[:, :], carry_col[:, :]), a)
        al_ok = dve.do(lambda e: e.tensor_scalar(alpha[:, :], alpha[:, :], carry_col[:, 0:1], None, ALU.mult), a)
        done = layernorm([done], [pe.last()])
        flat_h, flat_x = h.rearrange("p t f -> p (t f)"), x.rearrange("p t f -> p (t f)")
        for k in range(4):
            if k:
                t = product(done)
                featT_ok = evacuate(t)
                for g, (c, w) in enumerate(GROUPS):
                    for j in range(w // P):
                        t = flip(bank[g][:, j * P:(j + 1) * P], featT[:, c + j * P:c + (j + 1) * P], featT_ok, bank_free[g], mark=(j == w // P - 1))
                    done = act.do(lambda e, g=g, c=c, w=w: e.copy(flat_h[:, c:c + w], bank[g][:, 0:w]), t, xk_ok)
                    bank_free[g] = [done]
            for c, w in GROUPS:
                xk_ok = dve.do(lambda e, c=c, w=w, k=k: e.scalar_tensor_tensor(
                    out=flat_x[:, c:c + w], in0=flat_h[:, c:c + w], scalar=alpha[:, k:k + 1], in1=flat_x[:, c:c + w],
                    op0=ALU.mult, op1=ALU.add), done, al_ok, xk_ok if k else None)
        out_st = arrival("out_st")
        full = N // P
        sp.dma(out_st, out[0:full * P, :].rearrange("(t p) f -> p t f", p=P), x[:, 0:full, :], xk_ok)
        sp.dma(out_st, out[full * P:N, :], x[0:N - full * P, full, :], xk_ok)
        sp.wait((out_st.sem, out_st.value))

        block = ctx.enter_context(nc.Block())
        for attach, queue in ((block.tensor, pe), (block.scalar, act), (block.vector, dve), (block.gpsimd, pool), (block.sync, sp)):
            def body(e, queue=queue):
                for op in queue.ops:
                    op(e)
            attach(body)


def kernel(**inputs):
    import concourse.bacc as bacc
    from concourse.bass_utils import run_bass_kernel_spmd as run

    g = {k: np.asarray(v) for k, v in inputs.items()}
    pad = np.arange(EP - E, dtype=np.int32) // 4 + N
    src = np.concatenate([g["src"], pad])
    dst = np.concatenate([g["dst"], pad])
    weight = np.concatenate([g["edge_weight"], np.zeros(EP - E, np.float32)])
    columns = lambda v: np.ascontiguousarray(v.reshape(ET, P).T)
    arrays = {
        "x": np.concatenate([g["x"], np.zeros((NP - N, P), np.float32)]),
        "src_c": columns(src), "dst_c": columns(dst),
        "w_c": columns(weight),
        "src": src, "dst": np.concatenate([np.full(1, -1, np.int32), dst]),
        "tile_first": dst.reshape(ET, P)[None, :, 0].copy(), "tile_last": dst.reshape(ET, P)[None, :, P - 1].copy(),
        "edgeT": np.concatenate([g["edge_attr_64"].T, np.zeros((EF, EP - E), np.float32)], 1),
        "We1_node": g["L0_gnn_We1"][:P], "We1_edge": g["L0_gnn_We1"][P:],
        "W1_context": g["L0_gnn_W1"][:P], "W1_node": g["L0_gnn_W1"][P:],
        "We2_node": g["L0_gnn_We2"][:P], "We2_edge": g["L0_gnn_We2"][P:],
        "L0_gnn_be2": g["L0_gnn_be2"].reshape(1, 1), "L0_gnn_bet": g["L0_gnn_bet"].reshape(1, P),
        "L3_gnn_alpha_logits": g["L3_gnn_alpha_logits"].reshape(1, 4),
    }
    for n in BIAS_ROWS:
        arrays[n] = g[n].reshape(1, P)
    for n in BIAS_COLUMNS:
        arrays.setdefault(n, g[n].reshape(P, 1) if n in g else None)
    for n in WEIGHTS:
        arrays.setdefault(n, g[n] if n in g else None)
    nc = bacc.Bacc("TRN2", target_bir_lowering=False, num_devices=1)
    given = {}
    arrays = {"in_" + n: np.ascontiguousarray(a) for n, a in arrays.items()}
    for n, a in arrays.items():
        given[n[3:]] = nc.dram_tensor(n, a.shape, mybir.dt.from_np(a.dtype), kind="ExternalInput").ap()
    out = nc.dram_tensor("out", (N, P), F32, kind="ExternalOutput").ap()
    build(nc, given, out)
    r = run(nc, [arrays], core_ids=[0])
    return r.results[0]["out"]
```

```python
from contextlib import ExitStack

import numpy as np

import concourse.bass as bass
from concourse import mybir

F32 = mybir.dt.float32
BF16 = mybir.dt.bfloat16
I32 = mybir.dt.int32
ALU = mybir.AluOpType
ACT = mybir.ActivationFunctionType
AX_X = mybir.AxisListType.X

P = 128
N = 3125
E = 103125
EF = 64
NT = -(-N // P)
NP = NT * P
BANK = 512
CH = -(-E // BANK)
EP = CH * BANK
TPC = BANK // P
ET = EP // P
SEQ = EP // P
GROUPS = [(g * BANK, min(BANK, NP - g * BANK)) for g in range(-(-NP // BANK))]
DUMP = NP * NP
GROUP = 32
NG = -(-ET // GROUP)
MARGIN = 1024
READY = [min(NG - 1, -(-((E * min(P * (r + 1), N)) // N + MARGIN) // (GROUP * P)) - 1) for r in range(NT)]
READY_AT = [(r, READY[r]) for r in range(NT) if READY[r] < NG - 1]
AFTER = 30
EXACT = 256
FAR = 1e30
EPS = 1e-5
SLOPE = 0.01

WEIGHTS = ["L0_gnn_Wn", "We1_node", "L0_gnn_Wet", "W1_context", "W1_node", "L0_gnn_W2",
           "L1_gnn_W1", "L1_gnn_W2", "L1_gnn_W3", "L2_gnn_W0", "L2_gnn_W1", "L2_gnn_W2"]
BIAS_COLUMNS = ["L0_gnn_bn", "L0_gnn_be1", "L0_gnn_b1", "We2_node", "We2_edge"]
BIAS_ROWS = ["L0_gnn_b2", "L1_gnn_b1", "L1_gnn_b2", "L1_gnn_b3", "L1_gnn_a1", "L1_gnn_a2", "L1_gnn_a3",
             "L2_gnn_b0", "L2_gnn_b1", "L2_gnn_b2"]


class Queue:

    def __init__(self, sem):
        self.sem, self.count, self.ops, self.seen = sem, 0, [], {}

    def wait(self, *after):
        for tok in after:
            if tok is None:
                continue
            if isinstance(tok, list):
                self.wait(*tok)
                continue
            sem, value = tok
            if self.seen.get(id(sem), 0) < value:
                self.seen[id(sem)] = value
                self.ops.append(lambda e, s=sem, v=value: e.wait_ge(s, v))

    def do(self, issue, *after, mark=True):
        self.wait(*after)
        if not mark:
            self.ops.append(issue)
            return None
        self.count += 1
        self.ops.append(lambda e, sem=self.sem: issue(e).then_inc(sem, 1))
        return (self.sem, self.count)

    def dma(self, arrival, out, in_, *after, **kw):
        self.wait(*after)
        arrival.value += 16
        self.ops.append(lambda e: e.dma_start(out, in_, **kw).then_inc(arrival.sem, 16))
        return (arrival.sem, arrival.value)

    def gather(self, arrival, out, table, index, *after):
        self.wait(*after)
        arrival.value += 16
        self.ops.append(lambda e: e.indirect_dma_start(
            out, None, table, bass.IndirectOffsetOnAxis(ap=index, axis=0)).then_inc(arrival.sem, 16))
        return (arrival.sem, arrival.value)

    def scatter(self, arrival, table, index, in_, *after, add=False):
        self.wait(*after)
        arrival.value += 16
        kw = dict(compute_op=ALU.add) if add else {}
        self.ops.append(lambda e: e.indirect_dma_start(
            table, bass.IndirectOffsetOnAxis(ap=index, axis=0), in_, None, **kw).then_inc(arrival.sem, 16))
        return (arrival.sem, arrival.value)

    def begin(self, flag, sem):
        self.outside = (self.sem, self.count, dict(self.seen))
        self.sem, self.count = sem, 0
        self.ops.append(lambda e: flag["open"].enter_context(e.If(flag["value"] > 0)))
        self.flag = flag

    def end(self):
        self.ops.append(lambda e, f=self.flag: f["open"].close())
        self.sem, self.count, self.seen = self.outside

    def either(self, flag, usual, rare):
        ops, count, seen = self.ops, self.count, self.seen
        ways = []
        for way in (usual, rare):
            self.ops, self.count, self.seen = [], count, dict(seen)
            result = way()
            ways.append((self.ops, self.count, self.seen))
        assert ways[0][1] == ways[1][1]
        self.ops = ops
        self.seen = {k: min(v, ways[0][2][k]) for k, v in self.seen.items() if k in ways[0][2]}

        def op(e):
            with e.If(flag["value"] < 1):
                for o in ways[0][0]:
                    o(e)
            with e.If(flag["value"] > 0):
                for o in ways[1][0]:
                    o(e)
        self.ops.append(op)
        return result

    def last(self):
        return (self.sem, self.count) if self.count else None


class Arrival:

    def __init__(self, sem):
        self.sem, self.value = sem, 0


class Slots:

    def __init__(self, buffers):
        self.buffers, self.free, self.at = buffers, [[] for _ in buffers], -1

    def take(self):
        self.at = (self.at + 1) % len(self.buffers)
        after, self.free[self.at] = self.free[self.at], []
        return self.buffers[self.at], self.free[self.at], after


def along(ap, n):
    return ap.unsqueeze(1).broadcast_to([ap.shape[0], n, ap.shape[1]])


def across(ap, n):
    return ap.unsqueeze(2).broadcast_to([ap.shape[0], ap.shape[1], n])


def build(nc, given, out):
    with ExitStack() as ctx:
        def sb(name, shape, dt=F32):
            return ctx.enter_context(nc.sbuf_tensor(name, shape, dt))

        def dram(name, shape, dt=F32):
            return nc.dram_tensor(name, shape, dt, kind="Internal").ap()

        def arrival(name):
            return Arrival(ctx.enter_context(nc.semaphore(name)))

        pe, act, dve, pool, sp = (Queue(ctx.enter_context(nc.semaphore(f"done_{n}")))
                                  for n in ("pe", "act", "dve", "pool", "sp"))
        bank = [ctx.enter_context(nc.psum_tensor(f"bank{i}", [P, BANK], F32)) for i in range(8)]
        bank_free = [[] for _ in bank]

        node_table = dram("node_table", [NP, P])
        he_d = dram("he_d", [CH, P, BANK])
        z_d = dram("z_d", [EP, 1])
        key_d = dram("key_d", [3, EP], BF16)
        zmax_d = dram("zmax_d", [EP, 1])
        begin_d = dram("begin_d", [EP + NP, 2])
        ex_d = dram("ex_d", [3, EP], BF16)
        keep_d = dram("keep_d", [EP], BF16)
        exsum_d = dram("exsum_d", [EP, 1])
        hesum_d = dram("hesum_d", [EP, P])
        record_d = dram("record_d", [EP + 1, 3])
        edge_d = dram("edge_d", [EP, EF])
        next_d = dram("next_d", [NP + P, 1])
        adj = dram("adj", [NP * NP + EP, 2])
        weight_t = dram("weight_t", [NP, NP])
        count_t = dram("count_t", [NP, NP], BF16)
        count_full = dram("count_full", [NP, NP])
        weight_n = dram("weight_n", [NP, NP])

        ident = sb("ident", [P, P])
        tri_incl = sb("tri_incl", [P, P])
        tri_less = sb("tri_less", [P, P])
        ones = sb("ones", [P, P])
        ones_bf = sb("ones_bf", [3, P], BF16)
        iota_i = sb("iota_i", [P, P], I32)
        iota_b = sb("iota_b", [P, P], BF16)
        eps_col = sb("eps_col", [P, 1])
        W = {n: sb(n, [P, P]) for n in WEIGHTS}
        We1_edge = sb("We1_edge", [EF, P])
        col = {n: sb("c_" + n, [P, 1]) for n in BIAS_COLUMNS}
        row = {n: sb("r_" + n, [P, P]) for n in BIAS_ROWS}
        be2_col = sb("be2_col", [P, 1])
        bet_row = sb("bet_row", [1, P])
        alpha = sb("alpha", [P, 4])
        x = sb("x", [P, NT, P])
        h = sb("h", [P, NT, P])
        featT = sb("featT", [P, NP])
        hvT = sb("hvT", [P, NP])
        stats = sb("stats", [P, NT, 6])
        moments = sb("moments", [P, NT, 2])
        rstd = sb("rstd", [P, NT])
        shift = sb("shift", [P, NT])
        dis = sb("dis", [P, NT])
        dinv = sb("dinv", [P, NT])
        has = sb("has", [P, NT])
        small = sb("small", [P, 8, NT])
        end_i = sb("end_i", [P, NT], I32)
        begin_i = sb("begin_i", [P, NT], I32)
        work = sb("work", [P, 2, BANK])

        ARENA = 26500
        arena = sb("arena", [P, ARENA])
        used = [0]

        def carve(n):
            used[0] += n
            assert used[0] <= ARENA - 3 * ET, used[0]
            return arena[:, used[0] - n:used[0]]

        src_c = carve(ET).bitcast(I32)
        dst_c = carve(ET).bitcast(I32)
        w_c = carve(ET)
        w4_c = carve(2 * ET).bitcast(BF16).rearrange("p (t c) -> p t c", c=4)
        key_c = carve(ET)
        lo_c = carve(ET)
        hi_c = carve(ET)
        lohi_bf = carve(ET).bitcast(BF16).rearrange("p (c t) -> p c t", c=2)
        later_c = carve(ET)
        MATRIX_END = ARENA - 3 * ET
        pair_c = arena[:, MATRIX_END:MATRIX_END + 2 * ET].rearrange("p (t c) -> p t c", c=2)
        target = arena[:, MATRIX_END + 2 * ET:].bitcast(I32)
        part_c = carve(ET)
        dump_c = carve(ET)
        z_row = Slots([part_c[0:1, 0:BANK], dump_c[0:1, 0:BANK]])
        dst_s = carve(SEQ).bitcast(I32)
        prev_s = carve(SEQ).bitcast(I32)
        keep_s = carve(SEQ)
        reset_s = carve(SEQ)
        a_s = carve(SEQ)
        b_s = carve(SEQ)
        z_s = carve(SEQ)
        tl_space = carve(2 * SEQ)
        tl_s = tl_space.rearrange("p (t c) -> p t c", c=2)
        keep_bf = carve(SEQ // 2).bitcast(BF16)
        piece_bf = [tl_space[:, n * SEQ // 2:(n + 1) * SEQ // 2].bitcast(BF16) for n in range(3)]
        EDGE_COLS = 1024
        edge_space = carve(2 * EDGE_COLS)
        edge_in = Slots([edge_space[0:EF, i * EDGE_COLS:(i + 1) * EDGE_COLS] for i in range(2)])
        key_row = Slots([carve(EDGE_COLS // 2).bitcast(BF16)[0:3, :] for _ in range(2)])

        gath = Slots([sb(f"gath{i}", [P, TPC, P]) for i in range(3)])
        he = Slots([sb(f"he{i}", [P, BANK]) for i in range(3)])
        onehot_space = carve(BANK)
        onehot = Slots([onehot_space[:, i * BANK // 2:(i + 1) * BANK // 2].bitcast(BF16).rearrange("p (a b) -> p a b", b=P)
                        for i in range(2)])
        hi_hot = Slots([carve(TPC * NT // 2).bitcast(BF16).rearrange("p (a b) -> p a b", b=NT) for i in range(2)])
        tile_hot = Slots([carve(TPC * 2 * NT).bitcast(BF16).rearrange("p (a c b) -> p a c b", c=4, b=NT) for _ in range(2)])
        same = Slots([carve(P // 2).bitcast(BF16) for _ in range(8)])
        diag_space = [carve(P) for _ in range(2)]
        rows1 = sb("rows1", [1, 2 * P])
        carry_row = sb("carry_row", [1, P + 1])
        carry_col = sb("carry_col", [P, 1])
        ends = sb("ends", [P, 2])
        flag_row = sb("flag_row", [1, 3, ET])
        flag_f = sb("flag_f", [1, 1])
        flag_i = sb("flag_i", [1, 2], I32)
        unsorted_i = sb("unsorted_i", [1, 1], I32)
        crowded_f = sb("crowded_f", [1, 1])
        crowded_i = sb("crowded_i", [1, 1], I32)
        ready_row = sb("ready_row", [1, 4, NT])
        node_iota = sb("node_iota", [P, NT], I32)

        loaded = {}

        def load(name, dst_ap, src_ap, q=None, **kw):
            loaded[name] = (q or sp).dma(arrival("ld_" + name), dst_ap, src_ap, **kw)
            return loaded[name]

        in_x = load("x", x[:, :, :], given["x"].rearrange("(t p) f -> p t f", p=P))
        load("raw_s", dst_s, given["dst"][1:EP + 1].rearrange("(p c) -> p c", p=P))
        load("raw_prev", prev_s, given["dst"][0:EP].rearrange("(p c) -> p c", p=P))
        small_load = arrival("ld_small")
        for n in WEIGHTS:
            tok_small = act.dma(small_load, W[n][:, :], given[n])
        act.dma(small_load, We1_edge[:, :], given["We1_edge"])
        for n in BIAS_COLUMNS:
            act.dma(small_load, col[n][:, :], given[n])
        for n in BIAS_ROWS:
            act.dma(small_load, row[n][:, :], given[n].broadcast_to([P, P]))
        act.dma(small_load, be2_col[:, :], given["L0_gnn_be2"].broadcast_to([P, 1]))
        act.dma(small_load, bet_row[:, :], given["L0_gnn_bet"])
        tok_small = act.dma(small_load, alpha[:, :], given["L3_gnn_alpha_logits"].broadcast_to([P, 4]))

        c0 = pool.do(lambda e: e.memset(ident[:, :], 0.0))
        c_ones = pool.do(lambda e: e.memset(ones[:, :], 1.0))
        c1 = pool.do(lambda e: e.affine_select(out=ident[:, :], in_=ident[:, :], compare_op=ALU.not_equal, fill=1.0,
                                               base=0, pattern=[[-1, P]], channel_multiplier=1), c0, c_ones)
        pool.do(lambda e: e.affine_select(out=tri_incl[:, :], in_=ones[:, :], compare_op=ALU.is_ge, fill=0.0,
                                          base=0, pattern=[[1, P]], channel_multiplier=-1))
        pool.do(lambda e: e.affine_select(out=tri_less[:, :], in_=ones[:, :], compare_op=ALU.is_gt, fill=0.0,
                                          base=0, pattern=[[1, P]], channel_multiplier=-1))
        pool.do(lambda e: e.iota(iota_i[:, :], pattern=[[1, P]], base=0, channel_multiplier=0))
        consts = pool.do(lambda e: e.iota(node_iota[:, :], pattern=[[P, NT]], base=EP, channel_multiplier=1))
        dve.do(lambda e: e.tensor_copy(iota_b[:, :], iota_i[:, :]), consts)
        dve.do(lambda e: e.memset(ones_bf[:, :], 1.0))
        v_consts = dve.do(lambda e: e.memset(eps_col[:, :], EPS))

        k0 = dve.do(lambda e: e.tensor_copy(a_s, dst_s), loaded["raw_s"])
        k1 = dve.do(lambda e: e.tensor_copy(b_s, prev_s), loaded["raw_prev"])
        k2 = dve.do(lambda e: e.tensor_tensor(a_s, a_s, b_s, ALU.is_lt), k0, k1)
        k3 = dve.do(lambda e: e.tensor_reduce(carry_col[:, :], a_s, AX_X, ALU.max), k2)
        t = pe.do(lambda e: e.matmul(bank[7][0:1, 0:P], carry_col[:, 0:1], ident[:, :], start=True, stop=True), k3, consts)
        k4 = dve.do(lambda e: e.tensor_reduce(flag_f[:, :], bank[7][0:1, 0:P], AX_X, ALU.max), t)
        bank_free[7] = [k4]
        unsorted_ok = dve.do(lambda e: e.tensor_copy(unsorted_i[:, :], flag_f[:, :]), k4)
        unsorted = {q: {} for q in (pe, dve, pool, sp)}
        crowded = {q: {} for q in (pe, dve, sp)}

        def read_flag(q, flag, cell, ok):
            def op(e):
                flag[q]["value"] = e.value_load(cell, min_val=0, max_val=1)
                flag[q]["open"] = ExitStack()
            q.wait(ok)
            q.ops.append(op)

        def load_either(arrived, dst_ap, as_given, as_sorted, after=(), after_sort=()):
            sp.wait(*after)
            arrived.value += 16

            def op(e):
                r = unsorted[sp]["value"]
                with e.If(r < 1):
                    e.dma_start(dst_ap, as_given).then_inc(arrived.sem, 16)
                with e.If(r > 0):
                    e.dma_start(dst_ap, as_sorted, allow_slow_non_contiguous=True).then_inc(arrived.sem, 16)
            sp.ops.append(op)
            return (arrived.sem, arrived.value)

        ZC = 6400
        zeros = carve(ZC // 5)
        z0 = dve.do(lambda e: e.memset(zeros[:, :], 0.0))

        def layernorm_group(g, x_ok, h_free=None, scale=None):
            c, w = GROUPS[g]
            t0, t1 = c // P, (c + w) // P
            m, r, sh = moments[:, t0:t1, :], rstd[:, t0:t1], shift[:, t0:t1]
            for t in range(t0, t1):
                a = dve.do(lambda e, t=t: e.bn_stats(stats[:, t, :], x[:, t, :]), x_ok)
            for t in range(t0, t1):
                b = dve.do(lambda e, t=t: e.bn_aggr(moments[:, t, :], stats[:, t, :]), a)
            a = act.do(lambda e: e.activation(r, m[:, :, 1], ACT.Sqrt, bias=eps_col[:, 0:1]), b, v_consts)
            a = dve.do(lambda e: e.reciprocal(r, r), a)
            if scale is not None:
                a = dve.do(lambda e: e.tensor_tensor(r, r, scale[:, t0:t1], ALU.mult), a)
            a = dve.do(lambda e: e.scalar_tensor_tensor(out=sh, in0=m[:, :, 0], scalar=-1.0, in1=r,
                                                        op0=ALU.mult, op1=ALU.mult), a)
            for t in range(t0, t1):
                o = act.do(lambda e, t=t: e.activation(h[:, t, :], x[:, t, :], ACT.Relu, bias=shift[:, t:t + 1],
                                                       scale=rstd[:, t:t + 1]), a, h_free)
            return o

        def layernorm(x_ok, h_free=None, scale=None):
            return [layernorm_group(g, x_ok[g], h_free, scale) for g in range(len(GROUPS))]

        def leaky(ap, *after):
            return dve.do(lambda e: e.scalar_tensor_tensor(out=ap, in0=ap, scalar=SLOPE, in1=ap, op0=ALU.mult, op1=ALU.max),
                          *after)

        def flip(out_ap, in_ap, *after, mark=False):
            k = in_ap.shape[0]
            return pe.do(lambda e: e.transpose(out_ap, in_ap, ident[0:k, 0:k]), consts, *after, mark=mark)

        h_ok = layernorm([in_x] * len(GROUPS))
        for g, (c, w) in enumerate(GROUPS):
            b = g % 2
            for j in range(w // P):
                t = flip(bank[b][:, j * P:(j + 1) * P], h[:, c // P + j, :], h_ok[g], bank_free[b], mark=(j == w // P - 1))
            hT_ok = act.do(lambda e, b=b, c=c, w=w: e.copy(featT[:, c:c + w], bank[b][:, 0:w]), t)
            bank_free[b] = [hT_ok]
        table_st = [arrival(f"table_st{i}") for i in range(2)]
        gslot = Slots([he.buffers[0], he.buffers[1]])
        for g, (c, w) in enumerate(GROUPS):
            b = 2 + g % 2
            for j in range(w // P):
                t = pe.do(lambda e, b=b, j=j, c=c: e.matmul(bank[b][:, j * P:(j + 1) * P], featT[:, c + j * P:c + (j + 1) * P],
                                                            W["We1_node"][:, :], start=True, stop=True),
                          hT_ok, tok_small, bank_free[b], mark=(j == w // P - 1))
            buf, free, after = gslot.take()
            s = dve.do(lambda e, b=b, w=w, buf=buf: e.tensor_copy(buf[:, 0:w], bank[b][:, 0:w]), t, after)
            bank_free[b] = [s]
            free.append(act.dma(table_st[g % 2], node_table[c:c + w, :].rearrange("(j p) f -> p j f", p=P),
                               buf[:, 0:w].rearrange("p (j f) -> p j f", f=P), s))
        table_ok = [(s.sem, s.value) for s in table_st]
        he.free[0], he.free[1] = [table_ok], [table_ok]
        for g, (c, w) in enumerate(GROUPS):
            b = 4 + g % 2
            t = pe.do(lambda e, b=b, c=c, w=w: e.matmul(bank[b][:, 0:w], W["L0_gnn_Wn"][:, :], featT[:, c:c + w],
                                                        start=True, stop=True), bank_free[b])
            a = act.do(lambda e, b=b, c=c, w=w: e.activation(hvT[:, c:c + w], bank[b][:, 0:w], ACT.Identity,
                                                             bias=col["L0_gnn_bn"][:, 0:1]), t, tok_small)
            bank_free[b] = [a]
            hv_ok = leaky(hvT[:, c:c + w], a)
        t_node = small[:, 0, :]
        for i in range(NT):
            t = pe.do(lambda e, i=i: e.matmul(bank[6][:, i:i + 1], hvT[:, i * P:(i + 1) * P], col["We2_node"][:, 0:1],
                                              start=True, stop=True), hv_ok, mark=(i == NT - 1))
        tn_ok = dve.do(lambda e: e.tensor_scalar(t_node, bank[6][:, 0:NT], be2_col[:, 0:1], None, ALU.add), t, tok_small)
        bank_free[6] = [tn_ok]

        gather_ok, gather_sem = [], [arrival(f"gath{i}") for i in range(3)]

        def sort_edges():
            in_branch = {q: ctx.enter_context(nc.semaphore(f"sort_{n}"))
                         for q, n in ((pe, "pe"), (dve, "dve"), (pool, "pool"), (sp, "sp"))}
            held = [list(bank_free[b]) for b in (4, 5, 7)]
            before = [hv_ok, tn_ok, z0]
            for q in (pe, dve, pool, sp):
                read_flag(q, unsorted, unsorted_i[0:1, 0:1], unsorted_ok)
                q.begin(unsorted[q], in_branch[q])
            raw = arrival("raw")
            sp.dma(raw, src_c, given["src_c"])
            sp.dma(raw, dst_c, given["dst_c"])
            raw_ok = sp.dma(raw, w_c, given["w_c"])
            rec = arena[:, MATRIX_END:].rearrange("p (t c) -> p t c", c=3)
            dve.do(lambda e: e.tensor_copy(rec[:, :, 0].bitcast(I32), dst_c), raw_ok, *before)
            dve.do(lambda e: e.tensor_copy(rec[:, :, 1].bitcast(I32), src_c))
            r_ok = dve.do(lambda e: e.tensor_copy(rec[:, :, 2], w_c))
            f_ok = dve.do(lambda e: e.tensor_copy(key_c, dst_c))
            lo_i = later_c.bitcast(I32)
            a = dve.do(lambda e: e.tensor_scalar(lo_i, dst_c, P - 1, None, ALU.bitwise_and), f_ok)
            a = dve.do(lambda e: e.tensor_copy(lo_c, lo_i), a)
            a = dve.do(lambda e: e.tensor_scalar(lo_i, dst_c, 7, None, ALU.arith_shift_right), a)
            a = dve.do(lambda e: e.tensor_copy(hi_c, lo_i), a)
            t = None
            for i in range(ET):
                o = dve.do(lambda e, i=i: e.tensor_scalar(same.buffers[0], iota_b[:, :], lo_c[:, i:i + 1], None, ALU.is_equal),
                           a, v_consts, t)
                o = dve.do(lambda e, i=i: e.tensor_scalar(same.buffers[1][:, 0:NT], iota_b[:, 0:NT], hi_c[:, i:i + 1], None,
                                                          ALU.is_equal))
                t = pe.do(lambda e, i=i: e.matmul(bank[4][:, 0:NT], same.buffers[0], same.buffers[1][:, 0:NT],
                                                  start=(i == 0), stop=(i == ET - 1)), o, held)
            cnt, tot, pre, inc = small[:, 1, :], small[:, 3, :], small[:, 4, :], small[:, 5, :]
            a = dve.do(lambda e: e.tensor_copy(cnt, bank[4][:, 0:NT]), t)
            t = pe.do(lambda e: e.matmul(bank[4][:, 0:NT], ones[:, :], cnt, start=True, stop=True), a)
            t = pe.do(lambda e: e.matmul(bank[4][:, NT:2 * NT], tri_less[:, :], cnt, start=True, stop=True))
            a = dve.do(lambda e: e.tensor_copy(tot, bank[4][:, 0:NT]), t)
            b = dve.do(lambda e: e.tensor_copy(pre, bank[4][:, NT:2 * NT]))
            a = dve.do(lambda e: e.tensor_tensor_scan(inc, ones[:, 0:NT], tot, 0.0, ALU.mult, ALU.add), a)
            a = dve.do(lambda e: e.tensor_tensor(inc, inc, tot, ALU.subtract), a)
            a = dve.do(lambda e: e.tensor_tensor(inc, inc, pre, ALU.add), a, b)
            first = arrival("first_place")
            landed = sp.dma(first, next_d[0:NP, :].rearrange("(t p) o -> p (t o)", p=P), inc, a,
                            allow_slow_non_contiguous=True)
            sp.dma(first, next_d[NP:NP + P, :], zeros[:, 0:1], z0)
            a = dve.do(lambda e: e.memset(small[0:1, 6, 0:3].bitcast(I32), NP))
            sp.dma(first, record_d[0:1, :], small[0:1, 6, 0:3], a)
            landed = (first.sem, first.value)
            sp_i, sp_f = small[:, 6, 8:9].bitcast(I32), small[:, 6, 9:10]
            a = pool.do(lambda e: e.iota(sp_i, pattern=[[0, 1]], base=NP, channel_multiplier=1), r_ok)
            spare_ok = dve.do(lambda e: e.tensor_copy(sp_f, sp_i), a)
            place, cell = small[:, 7, 0:1], small[:, 7, 1:2]
            place_i, put_i, cell_i = small[:, 7, 2:3].bitcast(I32), small[:, 7, 3:4].bitcast(I32), small[:, 7, 4:5].bitcast(I32)
            base = small[:, 7, 5:6]
            erow = edge_space[:, 0:EF]
            got, put, er, cs = arrival("sort_base"), arrival("sort_put"), arrival("sort_rows"), arrival("sort_next")
            diag = diag_space[0]
            d = t = placed = None
            for i in range(ET):
                e_in = sp.dma(er, erow, given["edge_rows"][i * P:(i + 1) * P, :], placed)
                g_ = pool.gather(got, base, next_d, dst_c[:, i:i + 1], landed, raw_ok, d)
                a = dve.do(lambda e, i=i: e.tensor_scalar(diag, ident[:, :], key_c[:, i:i + 1], None, ALU.mult), t, r_ok)
                t = pe.do(lambda e: e.matmul(bank[5][:, 0:P], ones[:, :], diag, start=True, stop=True), a, held, d)
                a = dve.do(lambda e, i=i: e.scalar_tensor_tensor(out=diag, in0=bank[5][:, 0:P], scalar=key_c[:, i:i + 1],
                                                                 in1=tri_incl[:, :], op0=ALU.is_equal, op1=ALU.mult,
                                                                 accum_out=later_c[:, i:i + 1]), t)
                t = pe.do(lambda e: e.matmul(bank[7][:, 0:1], diag, ones[:, 0:1], start=True, stop=True), a, d)
                a = dve.do(lambda e: e.tensor_tensor(place, base, bank[7][:, 0:1], ALU.add), t, g_, placed, landed)
                b = dve.do(lambda e: e.tensor_copy(put_i, place), a)
                b = dve.do(lambda e: e.tensor_scalar(cell, place, -1.0, None, ALU.add), b)
                b = dve.do(lambda e: e.tensor_copy(place_i, cell), b)
                b = dve.do(lambda e, i=i: e.tensor_scalar(later_c[:, i:i + 1], later_c[:, i:i + 1], 1.0, None, ALU.is_equal), b)
                b = dve.do(lambda e, i=i: e.tensor_tensor(cell, key_c[:, i:i + 1], sp_f, ALU.subtract), b, spare_ok)
                b = dve.do(lambda e, i=i: e.tensor_tensor(cell, cell, later_c[:, i:i + 1], ALU.mult), b)
                b = dve.do(lambda e: e.tensor_tensor(cell, cell, sp_f, ALU.add), b)
                d = dve.do(lambda e: e.tensor_copy(cell_i, cell), b)
                landed = pool.scatter(cs, next_d, cell_i, place, d)
                pool.scatter(put, record_d, put_i, rec[:, i, :], d, r_ok)
                placed = pool.scatter(put, edge_d, place_i, erow, d, e_in)
            sp.wait(placed, landed)
            for q in (pe, dve, pool, sp):
                q.end()

        sort_edges()
        record_i = record_d.bitcast(I32)
        sorted_dst, sorted_src = record_i[1:EP + 1, 0], record_i[1:EP + 1, 1]

        def load_edges_array(name, dst_ap, as_given, as_sorted):
            loaded[name] = load_either(arrival("ld_" + name), dst_ap, as_given, as_sorted, (unsorted_ok,))

        load_edges_array("src_c", src_c, given["src_c"], sorted_src.rearrange("(t p) -> p t", p=P))
        load_edges_array("dst_s", dst_s, given["dst"][1:EP + 1].rearrange("(p c) -> p c", p=P),
                         sorted_dst.rearrange("(p c) -> p c", p=P))
        load_edges_array("src_s", z_s.bitcast(I32), given["src"].rearrange("(p c) -> p c", p=P),
                         sorted_src.rearrange("(p c) -> p c", p=P))
        load_edges_array("dst_c", dst_c, given["dst_c"], sorted_dst.rearrange("(t p) -> p t", p=P))
        load_edges_array("w_c", w_c, given["w_c"], record_d[1:EP + 1, 2].rearrange("(t p) -> p t", p=P))
        load_edges_array("prev_s", prev_s, given["dst"][0:EP].rearrange("(p c) -> p c", p=P),
                         record_i[0:EP, 0].rearrange("(p c) -> p c", p=P))
        sorted_edgeT = edge_d.rearrange("e f -> f e")

        kf = dve.do(lambda e: e.tensor_copy(hi_c, dst_c), loaded["dst_c"])
        sf = dve.do(lambda e: e.tensor_copy(lo_c, src_c), loaded["src_c"])
        key_ok = dve.do(lambda e: e.scalar_tensor_tensor(out=key_c, in0=hi_c, scalar=float(NP), in1=lo_c,
                                                         op0=ALU.mult, op1=ALU.add), kf, sf)
        lo_i = later_c.bitcast(I32)
        a = dve.do(lambda e: e.tensor_scalar(lo_i, dst_c, P - 1, None, ALU.bitwise_and))
        b_ = dve.do(lambda e: e.tensor_copy(lo_c, lo_i), a, key_ok)
        a = dve.do(lambda e: e.tensor_scalar(lo_i, dst_c, 7, None, ALU.arith_shift_right), b_)
        hilo_ok = dve.do(lambda e: e.tensor_copy(hi_c, lo_i), a)
        dve.do(lambda e: e.tensor_copy(lohi_bf[:, 0, :], lo_c))
        hilo_ok = dve.do(lambda e: e.tensor_copy(lohi_bf[:, 1, :], hi_c), hilo_ok)
        dve.do(lambda e: e.memset(w4_c[:, :, 3], 1.0))
        rest, r_ok = w_c, loaded["w_c"]
        for n in range(3):
            p_ok = dve.do(lambda e, n=n, rest=rest: e.tensor_copy(w4_c[:, :, n], rest), r_ok)
            if n < 2:
                r_ok = dve.do(lambda e, n=n, rest=rest: e.tensor_tensor(part_c, rest, w4_c[:, :, n], ALU.subtract), p_ok)
                rest = part_c
        w4_ok = p_ok
        ka = dve.do(lambda e: e.tensor_copy(a_s, z_s.bitcast(I32)), loaded["src_s"])
        kb_ = dve.do(lambda e: e.tensor_copy(b_s, dst_s), loaded["dst_s"])
        kc = dve.do(lambda e: e.scalar_tensor_tensor(out=a_s, in0=b_s, scalar=float(NP), in1=a_s, op0=ALU.mult, op1=ALU.add),
                    ka, kb_)
        kc = dve.do(lambda e: e.tensor_copy(z_s.bitcast(I32), a_s), kc)
        piece_st = arrival("piece_st")
        for n, mask in enumerate((0xFF0000, 0xFF00, 0xFF)):
            kd = dve.do(lambda e, mask=mask: e.tensor_scalar(b_s.bitcast(I32), z_s.bitcast(I32), mask, None, ALU.bitwise_and), kc, kb_)
            kb_ = dve.do(lambda e, n=n: e.tensor_copy(piece_bf[n], b_s.bitcast(I32)), kd)
            keyd_ok = sp.dma(piece_st, key_d[n].rearrange("(p c) -> p c", p=P), piece_bf[n], kb_)
        cleared = arrival("cleared")
        adj_flat = adj.rearrange("n c -> (n c)")
        span = P * ZC // 5
        clears = [(adj_flat[i * span:(i + 1) * span].rearrange("(p k) -> p k", p=P), zeros[:, :]) for i in range(5 * NT)] + \
                 [(adj_flat[2 * DUMP + c * EP:2 * DUMP + (c + 1) * EP].rearrange("(p k) -> p k", p=P), zeros[:, 0:SEQ])
                  for c in range(2)]
        begin_flat = begin_d.rearrange("n c -> (n c)")
        begin0 = arrival("begin0")
        for c in range(2):
            tok_begin0 = sp.dma(begin0, begin_flat[c * EP:(c + 1) * EP].rearrange("(p k) -> p k", p=P), zeros[:, 0:SEQ], z0)

        edge_sem = [arrival(f"edge{i}") for i in range(2)]
        keyrow_sem = [arrival(f"keyrow{i}") for i in range(2)]
        he_st = [arrival(f"he_st{i}") for i in range(3)]
        big = {}
        LOADC = EDGE_COLS // BANK

        def load_edges(k):
            c = k * EDGE_COLS
            w = min(EDGE_COLS, EP - c)
            buf, free, after = edge_in.take()
            t1 = load_either(edge_sem[k % 2], buf[:, 0:w], given["edgeT"][:, c:c + w], sorted_edgeT[:, c:c + w], after)
            rbuf, rfree, rafter = key_row.take()
            t2 = sp.dma(keyrow_sem[k % 2], rbuf[:, 0:w], key_d[:, c:c + w], rafter, keyd_ok)
            big[k] = (buf, free, t1, rbuf, rfree, t2)

        def gathers(c):
            buf, free, after = gath.take()
            for j in range(TPC):
                t = pool.gather(gather_sem[c % 3], buf[:, j, :], node_table, src_c[:, c * TPC + j:c * TPC + j + 1],
                                after, table_ok, loaded["src_c"])
            gather_ok.append((buf, free, t))

        NBIG = -(-EP // EDGE_COLS)
        for c in range(3):
            gathers(c)
        MERGE = BANK // (4 * TPC)
        spread_key, chunk_ok, merge_in, hot_in = {}, {}, {}, {}

        def spread_keys(c):
            _, _, _, rbuf, rfree, r_ok = big[c // LOADC]
            eo, kb = (c % LOADC) * BANK, 5 + c % 2
            t = pe.do(lambda e: e.matmul(bank[kb][:, :], ones_bf[:, :], rbuf[:, eo:eo + BANK], start=True, stop=True),
                      r_ok, v_consts, bank_free[kb])
            rfree[:] = [t]
            spread_key[c] = (kb, t)

        def edge_hidden(c):
            ebuf, efree, e_ok, _, _, _ = big[c // LOADC]
            eo, b = (c % LOADC) * BANK, c % 2
            gbuf, gfree, g_ok = gather_ok[c]
            te = pe.do(lambda e: e.matmul(bank[0][:, :], We1_edge[:, :], ebuf[:, eo:eo + BANK], start=True, stop=True),
                       e_ok, tok_small, bank_free[0])
            for j in range(TPC):
                t = flip(bank[1][:, j * P:(j + 1) * P], gbuf[:, j, :], g_ok, bank_free[1], mark=(j == TPC - 1))
            gfree.append(t)
            efree[:] = [t]
            hbuf, hfree, hafter = he.take()
            a = act.do(lambda e: e.activation(hbuf[:, :], bank[0][:, :], ACT.Identity, bias=col["L0_gnn_be1"][:, 0:1]), te, hafter)
            bank_free[0] = [a]
            chunk_ok[c] = [hbuf, hfree, a, t]

        def edge_hot(c):
            obuf, ofree, oafter = onehot.take()
            hbuf, hfree, hafter = hi_hot.take()
            tbuf, tfree, tafter = tile_hot.take()
            i0 = c * TPC
            o1 = dve.do(lambda e: e.tensor_tensor(obuf[:, :, :], along(iota_b[:, :], TPC), across(lohi_bf[:, 0, i0:i0 + TPC], P),
                                                  ALU.is_equal), oafter, hilo_ok, v_consts)
            o2 = dve.do(lambda e: e.tensor_tensor(hbuf[:, :, :], along(iota_b[:, 0:NT], TPC),
                                                  across(lohi_bf[:, 1, i0:i0 + TPC], NT), ALU.is_equal), hafter)
            four = [P, TPC, 4, NT]
            o3 = dve.do(lambda e: e.tensor_tensor(tbuf[:, :, :, :], hbuf[:, :, :].unsqueeze(2).broadcast_to(four),
                                                  w4_c[:, i0:i0 + TPC, :].unsqueeze(3).broadcast_to(four), ALU.mult), o2, w4_ok, tafter)
            hfree.append(o3)
            hot_in[c] = (obuf, ofree, tbuf, tfree, o1, o3)

        def degrees(c):
            obuf, ofree, tbuf, tfree, o1, o3 = hot_in.pop(c)
            for j in range(TPC):
                d = pe.do(lambda e, j=j: e.matmul(
                    bank[4][:, 0:4 * NT], obuf[:, j, :], tbuf[:, j, :, :].rearrange("p a b -> p (a b)"),
                    start=(c == 0 and j == 0), stop=(c == CH - 1 and j == TPC - 1)), o1, o3,
                    bank_free[4] if c == 0 else None, mark=(j == TPC - 1))
            ofree.append(d)
            tfree.append(d)
            return d

        def equal_keys(c):
            kb, t = spread_key.pop(c)
            merge_in[c] = []
            for j in range(TPC):
                i = c * TPC + j
                sbuf, sfree, safter = same.take()
                u = dve.do(lambda e, j=j, i=i, sbuf=sbuf: e.scalar_tensor_tensor(
                    out=sbuf[:, :], in0=bank[kb][:, j * P:(j + 1) * P], scalar=key_c[:, i:i + 1], in1=tri_incl[:, :],
                    op0=ALU.is_equal, op1=ALU.mult, accum_out=later_c[:, i:i + 1]), t, safter, hilo_ok)
                merge_in[c].append((sbuf, sfree, u))
            bank_free[kb] = [u]
            return u

        def merge(c):
            for j, (sbuf, sfree, u) in enumerate(merge_in.pop(c)):
                q, i = ((c % MERGE) * TPC + j) * 4, c * TPC + j
                m = pe.do(lambda e, sbuf=sbuf, q=q, i=i: e.matmul(bank[7][:, q:q + 4], sbuf[:, :], w4_c[:, i, :],
                                                                  start=True, stop=True), u, w4_ok, bank_free[7])
                sfree.append(m)
            if c % MERGE == MERGE - 1 or c == CH - 1:
                i0, ni = (c // MERGE) * MERGE * TPC, (c % MERGE + 1) * TPC
                return (i0, ni, m)

        def keep_pairs(i0, ni, m):
            got, to = bank[7][:, 0:4 * ni].rearrange("p (t c) -> p t c", c=4), pair_c[:, i0:i0 + ni, :]
            dve.do(lambda e: e.tensor_copy(to[:, :, 1], got[:, :, 3]), m)
            ok = dve.do(lambda e: e.tensor_copy(to[:, :, 0], got[:, :, 2]))
            for n in (1, 0):
                ok = dve.do(lambda e, n=n: e.tensor_tensor(to[:, :, 0], to[:, :, 0], got[:, :, n], ALU.add), ok)
            bank_free[7] = [ok]
            return ok

        z_st = [arrival(f"z_st{i}") for i in range(2)]
        z_row.free[0].append(w4_ok)

        def edge_logit(c):
            hbuf, hfree, he_ok, _ = chunk_ok[c]
            zb = 2 + c % 2
            t = pe.do(lambda e: e.matmul(bank[zb][0:1, :], col["We2_edge"][:, 0:1], hbuf[:, :], start=True, stop=True),
                      he_ok, bank_free[zb])
            hfree.append(t)
            z_due.append((c, zb, t))

        def keep_logit():
            c, zb, t = z_due.pop(0)
            buf, free, after = z_row.take()
            s = act.do(lambda e: e.copy(buf, bank[zb][0:1, :]), t, after)
            bank_free[zb] = [s]
            free.append(sp.dma(z_st[c % 2], z_d[c * BANK:(c + 1) * BANK, :].rearrange("e o -> o e"), buf, s))

        z_due = []
        load_edges(0)
        load_edges(1)
        spread_keys(0)
        for c in range(CH + 1):
            if c < CH:
                if c % LOADC == 0 and 0 < c // LOADC < NBIG - 1:
                    load_edges(c // LOADC + 1)
                edge_hidden(c)
                if c + 1 < CH:
                    spread_keys(c + 1)
                edge_hot(c)
                u = equal_keys(c)
            if c:
                pending = merge(c - 1)
                d = degrees(c - 1)
                edge_logit(c - 1)
                if pending:
                    pair_ok = keep_pairs(*pending)
            if c < CH:
                hbuf, hfree, a, t = chunk_ok[c]
                a = dve.do(lambda e, hbuf=hbuf: e.tensor_tensor(hbuf[:, :], hbuf[:, :], bank[1][:, :], ALU.add), a, t)
                bank_free[1] = [a]
                chunk_ok[c][2] = leaky(hbuf[:, :], a)
                hfree.append(act.dma(he_st[he.at], he_d[c], hbuf[:, :], chunk_ok[c][2]))
            if z_due:
                keep_logit()
            if c < CH:
                if c + 3 < CH:
                    gathers(c + 3)
                if clears:
                    tok_adj0 = sp.dma(cleared, *clears.pop(0), z0)
        chunk_read = pe.last()
        zd_ok = [(a.sem, a.value) for a in z_st]
        zs_ld = arrival("zs_ld")
        zs_ok = sp.dma(zs_ld, z_s, z_d.rearrange("(p c) o -> p (c o)", p=P), zd_ok)

        cnt, wdeg, tot, pre = small[:, 1, :], small[:, 2, :], small[:, 3, :], small[:, 4, :]
        s1 = dve.do(lambda e: e.tensor_copy(cnt, bank[4][:, 3 * NT:4 * NT]), d)
        s2 = dve.do(lambda e: e.tensor_scalar(wdeg, bank[4][:, 2 * NT:3 * NT], 1.0, None, ALU.add))
        for n in (1, 0):
            s2 = dve.do(lambda e, n=n: e.tensor_tensor(wdeg, wdeg, bank[4][:, n * NT:(n + 1) * NT], ALU.add), s2)
        bank_free[4] = [s2]
        t = pe.do(lambda e: e.matmul(bank[4][:, 0:NT], ones[:, :], cnt, start=True, stop=True), s1, s2)
        t2 = pe.do(lambda e: e.matmul(bank[4][:, NT:2 * NT], tri_less[:, :], cnt, start=True, stop=True))
        s3 = dve.do(lambda e: e.tensor_copy(tot, bank[4][:, 0:NT]), t2)
        s4 = dve.do(lambda e: e.tensor_copy(pre, bank[4][:, NT:2 * NT]))
        bank_free[4] = [s4]
        cw = dve.do(lambda e: e.tensor_reduce(ends[:, 0:1], cnt, AX_X, ALU.max), s1)
        t = pe.do(lambda e: e.matmul(bank[4][0:1, 0:P], ends[:, 0:1], ident[:, :], start=True, stop=True), cw, s4)
        cw = dve.do(lambda e: e.tensor_reduce(crowded_f[:, :], bank[4][0:1, 0:P], AX_X, ALU.max), t)
        bank_free[4] = [cw]
        cw = dve.do(lambda e: e.tensor_scalar(crowded_f[:, :], crowded_f[:, :], float(EXACT - 1), None, ALU.is_gt), cw)
        crowded_ok = dve.do(lambda e: e.tensor_copy(crowded_i[:, :], crowded_f[:, :]), cw)
        inc, w5, w6 = small[:, 5, :], small[:, 6, :], small[:, 7, :]
        s5 = dve.do(lambda e: e.tensor_tensor_scan(inc, ones[:, 0:NT], tot, 0.0, ALU.mult, ALU.add), s3)
        s6 = dve.do(lambda e: e.tensor_tensor(inc, inc, tot, ALU.subtract), s5)
        s7 = dve.do(lambda e: e.tensor_tensor(inc, inc, pre, ALU.add), s6, s4)
        s8 = dve.do(lambda e: e.tensor_scalar(has[:, :], cnt, 0.0, None, ALU.is_gt), s1)
        s9 = dve.do(lambda e: e.tensor_tensor(w5, inc, cnt, ALU.add), s7)
        s10 = dve.do(lambda e: e.tensor_scalar(w5, w5, -1.0, 0.0, ALU.add, ALU.max), s9)
        end_ok = dve.do(lambda e: e.tensor_copy(end_i[:, :], w5), s10)
        s11 = dve.do(lambda e: e.tensor_copy(w6, node_iota[:, :]), consts)
        s12 = dve.do(lambda e: e.tensor_tensor(inc, inc, w6, ALU.subtract), s11, s9)
        s13 = dve.do(lambda e: e.tensor_tensor(inc, inc, has[:, :], ALU.mult), s12, s8)
        s14 = dve.do(lambda e: e.tensor_tensor(inc, inc, w6, ALU.add), s13)
        begin_ok = dve.do(lambda e: e.tensor_copy(begin_i[:, :], inc), s14)
        s15 = dve.do(lambda e: e.tensor_scalar(dinv[:, :], cnt, 1.0, None, ALU.add), s14)
        s16 = dve.do(lambda e: e.tensor_scalar(w5, wdeg, 0.0, None, ALU.is_gt), s2, end_ok)
        s17 = dve.do(lambda e: e.tensor_scalar(wdeg, wdeg, 1e-30, None, ALU.max), s16)
        s18 = act.do(lambda e: e.activation(dinv[:, :], dinv[:, :], ACT.Sqrt), s15)
        s19 = act.do(lambda e: e.activation(wdeg, wdeg, ACT.Sqrt), s17)
        s20 = dve.do(lambda e: e.reciprocal(dinv[:, :], dinv[:, :]), s18)
        s21 = dve.do(lambda e: e.reciprocal(dis[:, :], wdeg), s19)
        dis_ok = dve.do(lambda e: e.tensor_tensor(dis[:, :], dis[:, :], w5, ALU.mult), s21)

        dump_i = dump_c.bitcast(I32)
        dump_f = lo_c
        q0 = pool.do(lambda e: e.iota(dump_i, pattern=[[P, ET]], base=DUMP, channel_multiplier=1), zd_ok)
        q1 = dve.do(lambda e: e.tensor_copy(dump_f, dump_i), q0, d)
        q2 = dve.do(lambda e: e.tensor_scalar(later_c, later_c, 1.0, None, ALU.is_equal), u)
        q3 = dve.do(lambda e: e.tensor_tensor(key_c, key_c, dump_f, ALU.subtract), q1)
        q4 = dve.do(lambda e: e.tensor_tensor(key_c, key_c, later_c, ALU.mult), q2, q3)
        q5 = dve.do(lambda e: e.tensor_tensor(key_c, key_c, dump_f, ALU.add), q4)
        target_ok = dve.do(lambda e: e.tensor_copy(target, key_c), q5)
        fl = arrival("fl")
        tiles_of_dst = sorted_dst.rearrange("(o t p) -> o t p", o=1, p=P)
        f1 = load_either(fl, flag_row[:, 0, :].bitcast(I32), given["tile_first"], tiles_of_dst[:, :, 0])
        f1 = load_either(fl, flag_row[:, 1, :].bitcast(I32), given["tile_last"], tiles_of_dst[:, :, P - 1])
        f2 = dve.do(lambda e: e.tensor_copy(flag_row[:, 2, :], flag_row[:, 0, :].bitcast(I32)), f1)
        f3 = dve.do(lambda e: e.tensor_copy(flag_row[:, 0, :], flag_row[:, 1, :].bitcast(I32)), f2)
        f4 = dve.do(lambda e: e.tensor_tensor(flag_row[:, 1, 0:ET - 2], flag_row[:, 0, 0:ET - 2], flag_row[:, 2, 2:ET],
                                              ALU.is_equal), f3)
        f5 = dve.do(lambda e: e.tensor_reduce(flag_f[:, :], flag_row[:, 1, 0:ET - 2], AX_X, ALU.max), f4)
        flag_ok = dve.do(lambda e: e.tensor_copy(flag_i[:, 0:1], flag_f[:, :]), f5)
        n = len(READY_AT)
        r_ld = arrival("r_ld")
        for m, (_, at) in enumerate(READY_AT):
            load_either(r_ld, ready_row[:, 0, m:m + 1].bitcast(I32), given["ready_dst"][:, m:m + 1],
                        sorted_dst[GROUP * P * (at + 1):GROUP * P * (at + 1) + 1].unsqueeze(0))
        g1 = sp.dma(r_ld, ready_row[:, 1, 0:n].bitcast(I32), given["ready_bound"])
        g2 = dve.do(lambda e: e.tensor_copy(ready_row[:, 2, 0:n], ready_row[:, 0, 0:n].bitcast(I32)), g1)
        g3 = dve.do(lambda e: e.tensor_copy(ready_row[:, 3, 0:n], ready_row[:, 1, 0:n].bitcast(I32)), g1)
        g4 = dve.do(lambda e: e.tensor_tensor(ready_row[:, 2, 0:n], ready_row[:, 2, 0:n], ready_row[:, 3, 0:n], ALU.is_lt), g2, g3)
        g5 = dve.do(lambda e: e.tensor_reduce(flag_f[:, :], ready_row[:, 2, 0:n], AX_X, ALU.max), g4, flag_ok)
        late_ok = dve.do(lambda e: e.tensor_copy(flag_i[:, 1:2], flag_f[:, :]), g5)

        even_done = [arrival(f"even_done{k}") for k in range(NG)]
        odd_done = [arrival(f"odd_done{k}") for k in range(NG)]
        flag_reg = []
        scatter_before = [None]

        def start_scatter():
            pool.wait(flag_ok)
            pool.ops.append(lambda e: flag_reg.append(e.value_load(flag_i[0:1, 0:1], min_val=0, max_val=1)))

        def group_tiles(k, odd):
            return [i for i in range(k * GROUP, min((k + 1) * GROUP, ET)) if i % 2 == odd]

        scatter_plan = []
        for step in range(-2, NG):
            if step + 2 < NG:
                scatter_plan += [(i, even_done[step + 2]) for i in group_tiles(step + 2, 0)]
            if step >= 0:
                scatter_plan += [(i, odd_done[step]) for i in group_tiles(step, 1)]
        scatter_plan.reverse()

        def scatter_tiles(n):
            for _ in range(min(n, len(scatter_plan))):
                i, done = scatter_plan.pop()
                k = i // GROUP
                if i % 2:
                    for d_ in even_done[k:k + 2]:
                        pool.wait((d_.sem, d_.value))
                if scatter_before[0]:
                    def guarded(e, before=scatter_before[0]):
                        with e.If(flag_reg[0] > 0):
                            e.wait_ge(*before)
                    pool.ops.append(guarded)
                scatter_before[0] = pool.scatter(done, adj, target[:, i:i + 1], pair_c[:, i, :], target_ok, pair_ok,
                                                 tok_adj0, flag_ok, add=True)

        k0 = dve.do(lambda e: e.tensor_copy(a_s, dst_s), loaded["dst_s"])
        k1 = dve.do(lambda e: e.tensor_copy(b_s, prev_s), loaded["prev_s"])
        k2 = dve.do(lambda e: e.tensor_tensor(keep_s, a_s, b_s, ALU.is_equal), k0, k1)
        k3 = dve.do(lambda e: e.tensor_copy(keep_bf, keep_s), k2)
        keepst = arrival("keepst")
        keepd_ok = sp.dma(keepst, keep_d.rearrange("(p c) -> p c", p=P), keep_bf, k3)
        k4 = dve.do(lambda e: e.tensor_scalar(reset_s, keep_s, -1.0, FAR, ALU.add, ALU.mult), k2)

        def segscan(out_ap, data0, data1, op0, op1, neutral, *after):
            i = after
            s = dve.do(lambda e: e.tensor_tensor_scan(out_ap, data0, data1, neutral, op0, op1), k4, *i)
            s = dve.do(lambda e: e.tensor_copy(ends[:, 0:1], out_ap[:, SEQ - 1:SEQ]), s)
            s = dve.do(lambda e: e.tensor_reduce(ends[:, 1:2], data0, AX_X, ALU.min))
            t = pe.do(lambda e: e.matmul(bank[7][0:1, 0:P], ends[:, 0:1], ident[:, :], start=True, stop=True), s, bank_free[7])
            t = pe.do(lambda e: e.matmul(bank[7][0:1, P:2 * P], ends[:, 1:2], ident[:, :], start=True, stop=True))
            s = dve.do(lambda e: e.tensor_copy(rows1[:, :], bank[7][0:1, 0:2 * P]), t)
            s0 = dve.do(lambda e: e.memset(carry_row[:, 0:1], neutral))
            s = dve.do(lambda e: e.tensor_tensor_scan(carry_row[:, 1:P + 1], rows1[:, P:2 * P], rows1[:, 0:P], neutral, op0, op1), s)
            t = pe.do(lambda e: e.matmul(bank[7][:, 2 * P:2 * P + 1], carry_row[0:1, 0:P], ones[0:1, 0:1],
                                         start=True, stop=True), s, s0)
            s = dve.do(lambda e: e.tensor_copy(carry_col[:, :], bank[7][:, 2 * P:2 * P + 1]), t)
            bank_free[7] = [s]
            return dve.do(lambda e: e.tensor_tensor_scan(out_ap, data0, data1, carry_col[:, 0:1], op0, op1), s)

        zm_ok = segscan(a_s, reset_s, z_s, ALU.add, ALU.max, -FAR, zs_ok, k2)
        zmst = arrival("zmst")
        zmd_ok = sp.dma(zmst, zmax_d.rearrange("(p c) o -> p (c o)", p=P), a_s, zm_ok)
        zmg = arrival("zmg")
        z_node = small[:, 5, :]
        start_scatter()
        scatter_tiles(20)
        for i in range(NT):
            zg_ok = pool.gather(zmg, z_node[:, i:i + 1], zmax_d, end_i[:, i:i + 1], zmd_ok, end_ok, begin_ok)
        pair_n = sb("pair_n", [P, NT, 2])
        n1 = dve.do(lambda e: e.tensor_copy(pair_n[:, :, 0], t_node), tn_ok)
        n2 = dve.do(lambda e: e.tensor_tensor(z_node, z_node, t_node, ALU.add), zg_ok, n1)
        n3 = dve.do(lambda e: e.scalar_tensor_tensor(out=pair_n[:, :, 1], in0=z_node, scalar=SLOPE, in1=z_node,
                                                     op0=ALU.mult, op1=ALU.max), n2)
        bst = arrival("bst")
        scatter_tiles(12)
        for i in range(NT):
            bd_ok = pool.scatter(bst, begin_d, begin_i[:, i:i + 1], pair_n[:, i, :], n3, n1, begin_ok, tok_begin0)
        tls = arrival("tls")
        tl_ok = sp.dma(tls, tl_s, begin_d[0:EP, :].rearrange("(p k) c -> p k c", p=P), bd_ok, keyd_ok)
        tnode_s = segscan(b_s, keep_s, tl_s[:, :, 0], ALU.mult, ALU.add, 0.0, tl_ok)
        e1 = dve.do(lambda e: e.tensor_tensor(z_s, z_s, b_s, ALU.add), tnode_s)
        e2 = leaky(z_s, e1)
        lmax_s = segscan(b_s, keep_s, tl_s[:, :, 1], ALU.mult, ALU.add, 0.0, e1)
        e3 = dve.do(lambda e: e.tensor_tensor(z_s, z_s, b_s, ALU.subtract), lmax_s, e2)
        e4 = act.do(lambda e: e.activation(z_s, z_s, ACT.Exp), e3)
        exst = arrival("exst")
        rest, r_ok = z_s, e4
        for n in range(3):
            p_ok = dve.do(lambda e, n=n, rest=rest: e.tensor_copy(piece_bf[n], rest), r_ok, keyd_ok)
            exd_ok = sp.dma(exst, ex_d[n].rearrange("(p c) -> p c", p=P), piece_bf[n], p_ok)
            if n < 2:
                r_ok = dve.do(lambda e, n=n, rest=rest: e.tensor_tensor(a_s, rest, piece_bf[n], ALU.subtract), p_ok, zmd_ok)
                rest = a_s
        es_ok = segscan(b_s, keep_s, z_s, ALU.mult, ALU.add, 0.0, e4)
        esst = arrival("esst")
        esd_ok = sp.dma(esst, exsum_d.rearrange("(p c) o -> p (c o)", p=P), b_s, es_ok)

        scatter_tiles(300)
        sg = arrival("sg")
        s_node = small[:, 6, :]
        for i in range(NT):
            sg_ok = pool.gather(sg, s_node[:, i:i + 1], exsum_d, end_i[:, i:i + 1], esd_ok, s14)
        scatter_tiles(AFTER)

        has_bits = arena[0:1, 0:NP]
        for g, (c, w) in enumerate(GROUPS):
            b = 2 + g % 2
            for j in range(w // P):
                t = pe.do(lambda e, b=b, j=j, c=c: e.matmul(bank[b][0:1, j * P:(j + 1) * P], has[:, c // P + j:c // P + j + 1],
                                                            ident[:, :], start=True, stop=True), s8, bank_free[b],
                          mark=(j == w // P - 1))
            hr_ok = dve.do(lambda e, b=b, c=c, w=w: e.tensor_copy(has_bits[:, c:c + w], bank[b][0:1, 0:w]), t, pair_ok, chunk_read)
            bank_free[b] = [hr_ok]

        he_in = Slots([gath.buffers[0].rearrange("p a b -> p (a b)"), gath.buffers[1].rearrange("p a b -> p (a b)"),
                       gath.buffers[2].rearrange("p a b -> p (a b)"), onehot_space])
        for i in range(3):
            he_in.free[i] = [gather_ok[c][1] for c in range(CH - 3, CH)]
        he_in.free[3] = [d]
        he_in_sem = [arrival(f"he_in{i}") for i in range(4)]
        prod = Slots([sb(f"prod{i}", [P, BANK]) for i in range(2)])
        run = Slots([edge_space[:, i * BANK:(i + 1) * BANK] for i in range(3)])
        run.free = [[edge_in.free[0], edge_in.free[1]] for _ in range(3)]
        flipped = Slots([b[:, :] for b in he.buffers])
        for i in range(3):
            flipped.free[i] = [he.free[0], he.free[1], he.free[2]]
        fl_st = [arrival(f"fl_st{i}") for i in range(3)]
        ex_row, keep_row = Slots([b for b in key_row.buffers]), Slots([sb(f"keep_row{i}", [1, EDGE_COLS], BF16) for i in range(2)])
        for i in range(2):
            ex_row.free[i] = [key_row.free[0], key_row.free[1]]
        exr_sem = [arrival(f"exr{i}") for i in range(2)]
        kpr_sem = [arrival(f"kpr{i}") for i in range(2)]
        rows, fetched, spread = {}, {}, {}
        he_all = [(s.sem, s.value) for s in he_st]

        def fetch_rows(k):
            c = k * EDGE_COLS
            w = min(EDGE_COLS, EP - c)
            a, afree, aafter = ex_row.take()
            t1 = sp.dma(exr_sem[k % 2], a[:, 0:w], ex_d[:, c:c + w], aafter, exd_ok)
            b, bfree, bafter = keep_row.take()
            t2 = sp.dma(kpr_sem[k % 2], b[:, 0:w], keep_d[c:c + w].unsqueeze(0), bafter, keepd_ok)
            rows[k] = (a, afree, t1, b, bfree, t2)

        def fetch_he(c):
            buf, free, after = he_in.take()
            fetched[c] = (buf, free, sp.dma(he_in_sem[c % 4], buf, he_d[c], after, he_all))

        def spread_rows(c):
            a, afree, t1, b, bfree, t2 = rows[c // LOADC]
            o = (c % LOADC) * BANK
            eb, kb = c % 2, 2 + c % 2
            u = pe.do(lambda e: e.matmul(bank[eb][:, :], ones_bf[:, :], a[:, o:o + BANK], start=True, stop=True), t1, bank_free[eb])
            v = pe.do(lambda e: e.matmul(bank[kb][:, :], ones_bf[0:1, :], b[0:1, o:o + BANK], start=True, stop=True), t2, bank_free[kb])
            afree[:] = [u]
            bfree[:] = [v]
            spread[c] = (eb, kb, u, v)

        fetch_rows(0)
        fetch_rows(1)
        for c in range(3):
            fetch_he(c)
        spread_rows(0)
        last_run = None
        for c in range(CH):
            k = c // LOADC
            if c % LOADC == 0 and 0 < k and k + 1 < NBIG:
                fetch_rows(k + 1)
            if c + 3 < CH:
                fetch_he(c + 3)
            if c + 1 < CH:
                spread_rows(c + 1)
            hbuf, hfree, h_in = fetched[c]
            eb, kb, u, v = spread[c]
            pbuf, pfree, pafter = prod.take()
            m = dve.do(lambda e, pbuf=pbuf, hbuf=hbuf, eb=eb: e.tensor_tensor(pbuf[:, :], bank[eb][:, :], hbuf, ALU.mult), u, h_in, pafter)
            hfree.append(m)
            bank_free[eb] = [m]
            rb, rfree2, rafter = run.take()
            init = 0.0 if last_run is None else last_run[:, BANK - 1:BANK]
            sc = dve.do(lambda e, rb=rb, kb=kb, pbuf=pbuf, init=init: e.tensor_tensor_scan(
                rb[:, :], bank[kb][:, :], pbuf[:, :], init, ALU.mult, ALU.add), m, v, rafter)
            last_run = rb
            pfree.append(sc)
            bank_free[kb] = [sc]
            tb = 4 + c % 2
            for j in range(TPC):
                t = pe.do(lambda e, j=j, tb=tb, rb=rb: e.matmul(bank[tb][:, j * P:(j + 1) * P], rb[:, j * P:(j + 1) * P],
                                                                ident[:, :], start=True, stop=True), sc, bank_free[tb],
                          mark=(j == TPC - 1))
            rfree2.append(t)
            fb, ffree, fafter = flipped.take()
            s = act.do(lambda e, fb=fb, tb=tb: e.copy(fb, bank[tb][:, :]), t, fafter)
            bank_free[tb] = [s]
            ffree.append(act.dma(fl_st[c % 3], hesum_d[c * BANK:(c + 1) * BANK, :].rearrange("(j p) f -> p j f", p=P),
                                 fb.rearrange("p (j f) -> p j f", f=P), s))
            scan_tok = sc
        run_all = [(s.sem, s.value) for s in fl_st]
        ag_ok = []
        for g, (c, w) in enumerate(GROUPS):
            ag = arrival(f"ag{g}")
            for i in range(c // P, (c + w) // P):
                a = pool.gather(ag, h[:, i, :], hesum_d, end_i[:, i:i + 1], run_all, hT_ok, t)
            ag_ok.append(a)
        scatter_tiles(ET)
        adj_ok = [(d_.sem, d_.value) for d_ in even_done + odd_done]

        pass2_over = [run_all, exd_ok, esd_ok, keepd_ok, pe.last(), act.last(), dve.last()]

        r1 = dve.do(lambda e: e.reciprocal(s_node, s_node), sg_ok)
        r2 = dve.do(lambda e: e.tensor_tensor(s_node, s_node, has[:, :], ALU.mult), r1, dis_ok)
        diag, agg_read = Slots(diag_space), None
        wk_free, x_ok = [[], []], []
        aggT_ok, ctx_ok, hid_ok = {}, {}, {}
        neg_free = [[run_all] for _ in range(3)]
        ctx_free = [[scan_tok] for _ in range(3)]

        def divide(g, c, w):
            b = 6 + g % 2
            for j in range(w // P):
                i = c // P + j
                dbuf, dfree, dafter = diag.take()
                dd = dve.do(lambda e, dbuf=dbuf, i=i: e.tensor_scalar(dbuf[:, :], ident[:, :], s_node[:, i:i + 1], None, ALU.mult), r2, dafter)
                t = pe.do(lambda e, j=j, i=i, dbuf=dbuf: e.matmul(bank[b][:, j * P:(j + 1) * P], h[:, i, :], dbuf[:, :],
                                                                          start=True, stop=True), dd, ag_ok[g], bank_free[b])
                dfree.append(t)
            aggT_ok[g] = act.do(lambda e: e.copy(featT[:, c:c + w], bank[b][:, 0:w]), t)
            bank_free[b] = [aggT_ok[g]]
            return t

        def context(g, c, w):
            b, ctxT, neg = g % 2, run.buffers[g % 3], he.buffers[g % 3]
            pe.do(lambda e: e.matmul(bank[b][:, 0:w], W["L0_gnn_Wet"][:, :], featT[:, c:c + w],
                                     start=True, stop=False), aggT_ok[g], bank_free[b])
            t = pe.do(lambda e: e.matmul(bank[b][:, 0:w], bet_row[0:1, :], has_bits[0:1, c:c + w],
                                         start=False, stop=True), hr_ok)
            a = dve.do(lambda e: e.tensor_scalar(neg[:, 0:w], bank[b][:, 0:w], 0.0, None, ALU.min), t, neg_free[g % 3])
            e_ = act.do(lambda e: e.activation(neg[:, 0:w], neg[:, 0:w], ACT.Exp), a)
            a = dve.do(lambda e: e.tensor_scalar(ctxT[:, 0:w], bank[b][:, 0:w], 0.0, None, ALU.max), ctx_free[g % 3])
            bank_free[b] = [a]
            ctx_ok[g] = dve.do(lambda e: e.scalar_tensor_tensor(out=ctxT[:, 0:w], in0=neg[:, 0:w], scalar=-1.0,
                                                                in1=ctxT[:, 0:w], op0=ALU.add, op1=ALU.add), a, e_)

        def hidden(g, c, w):
            b, ctxT, neg = 2 + g % 2, run.buffers[g % 3], he.buffers[g % 3]
            pe.do(lambda e: e.matmul(bank[b][:, 0:w], W["W1_context"][:, :], ctxT[:, 0:w],
                                     start=True, stop=False), ctx_ok[g], bank_free[b])
            t = pe.do(lambda e: e.matmul(bank[b][:, 0:w], W["W1_node"][:, :], hvT[:, c:c + w], start=False, stop=True))
            ctx_free[g % 3] = [t]
            hid_ok[g] = act.do(lambda e: e.activation(neg[:, 0:w], bank[b][:, 0:w], ACT.Relu,
                                                      bias=col["L0_gnn_b1"][:, 0:1]), t)
            bank_free[b] = [hid_ok[g]]

        def residual(g, c, w):
            k, b, n, neg = g % 2, 4 + g % 2, w // P, he.buffers[g % 3]
            for j in range(n):
                t = pe.do(lambda e, j=j: e.matmul(bank[b][:, j * P:(j + 1) * P], neg[:, j * P:(j + 1) * P],
                                                  W["L0_gnn_W2"][:, :], start=True, stop=True), hid_ok[g], bank_free[b],
                          mark=(j == n - 1))
            neg_free[g % 3] = [t]
            a = dve.do(lambda e: e.tensor_tensor(work[:, k, 0:w].rearrange("p (j f) -> p j f", f=P),
                                                 bank[b][:, 0:w].rearrange("p (j f) -> p j f", f=P),
                                                 along(row["L0_gnn_b2"][:, :], n), ALU.add), t, wk_free[k])
            bank_free[b] = [a]
            x_g = x[:, c // P:c // P + n, :].rearrange("p j f -> p (j f)")
            a = dve.do(lambda e: e.scalar_tensor_tensor(out=x_g, in0=work[:, k, 0:w], scalar=0.0, in1=x_g,
                                                        op0=ALU.max, op1=ALU.add), a)
            x_ok.append(a)
            wk_free[k] = [a]

        steps = (divide, context, hidden, residual)
        for k in range(len(GROUPS) + len(steps) - 1):
            for n, step in enumerate(steps):
                if 0 <= k - n < len(GROUPS):
                    t = step(k - n, *GROUPS[k - n])
                    agg_read = t if step is divide else agg_read

        edge_over = [pe.last(), act.last(), dve.last()]
        MATS = 7
        used[0] = 0
        first = carve(NP)
        pairs = Slots([carve(2 * NP).rearrange("p (n c) -> p n c", c=2) for i in range(2)])
        plain = Slots([first, carve(NP)])
        double = [carve(BANK).bitcast(BF16).rearrange("p (j h s) -> p j h s", h=2, s=P) for _ in GROUPS]
        double_free = [[edge_over, run_all] for _ in GROUPS]
        double_st = [arrival(f"double_st{g}") for g in range(len(GROUPS))]
        turned = Slots([carve(BANK) for _ in range((MATRIX_END - used[0]) // BANK)] + [b[:, :] for b in he.buffers] +
                       [b.rearrange("p a b -> p (a b)") for b in gath.buffers])
        for sl in (plain, turned):
            sl.free = [[edge_over, run_all] for _ in sl.buffers]
        pairs.free = [[pass2_over] for _ in pairs.buffers]
        pair_sem = [arrival(f"pair{i}") for i in range(2)]
        plain_st = [arrival(f"plain_st{i}") for i in range(2)]
        turn_st = [arrival(f"turn_st{i}") for i in range(len(turned.buffers))]

        h_ok = layernorm(x_ok, agg_read, dis)

        def product_tile(i, m_ap, m_ok, feat_ok):
            done = []
            for g, (c, w) in enumerate(GROUPS):
                w = min(w, N - c)
                done.append(pe.do(lambda e, g=g, c=c, w=w: e.matmul(bank[g][:, 0:w], h[:, i, :], m_ap[:, c:c + w],
                                                                    start=(i == 0), stop=(i == NT - 1)),
                                  m_ok, feat_ok[i // TPC], bank_free[g] if i == 0 else None,
                                  mark=(g == len(GROUPS) - 1 or i == NT - 1)))
            return done

        def late(e):
            r = e.value_load(flag_i[0:1, 1:2], min_val=0, max_val=1)
            with e.If(r > 0):
                for sem, value in adj_ok:
                    e.wait_ge(sem, value)
        sp.wait(late_ok)
        sp.ops.append(late)

        def load_pair(i):
            buf, free, after = pairs.take()
            landed = [(d_.sem, d_.value) for d_ in even_done[:READY[i] + 1] + odd_done[:READY[i] + 1]]
            return buf, free, sp.dma(pair_sem[i % 2], buf, adj[i * P * NP:(i + 1) * P * NP, :].rearrange("(p n) c -> p n c", p=P),
                                     after, landed)

        flip_banks = Slots([2, 3, 4, 5, 6, 7])
        flip_banks.free = [list(bank_free[b]) for b in flip_banks.buffers]
        count_flip = [0]

        def turn(pbuf, p_ok, i, g, part, to, after):
            c, w = GROUPS[g]
            b, bfree, bafter = flip_banks.take()
            for j in range(w // P):
                t = flip(bank[b][:, j * P:(j + 1) * P], pbuf[:, c + j * P:c + (j + 1) * P, part], p_ok, bafter,
                         mark=(j == w // P - 1))
            count_flip[0] += 1
            on_dve = count_flip[0] % 5 in (1, 3)
            s_ = (dve if on_dve else act).do(lambda e: (e.tensor_copy if on_dve else e.copy)(
                to, bank[b][:, 0:w].rearrange("p (j s) -> p j s", s=P)), t, after)
            bfree.append(s_)
            if c <= i * P < c + w:
                block = to[:, i - c // P, :]
                s_ = dve.do(lambda e: e.tensor_tensor(block, block, ident[:, :], ALU.add), s_)
            return t, s_

        def turn_weights(pbuf, p_ok, i, g):
            c, w = GROUPS[g]
            tb, tfree, tafter = turned.take()
            blocks = tb[:, 0:w].rearrange("p (j s) -> p j s", s=P)
            t, s_ = turn(pbuf, p_ok, i, g, 0, blocks, tafter)
            tfree.append(sp.dma(turn_st[turned.at], weight_t[c:c + w, i * P:(i + 1) * P].rearrange("(j p) s -> p j s", p=P),
                                blocks, s_))
            return tb, tfree, s_

        def turn_counts(pbuf, p_ok, i, g):
            c, w = GROUPS[g]
            half = i % 2
            t, s_ = turn(pbuf, p_ok, i, g, 1, double[g][:, 0:w // P, half, :], double_free[g])
            double_free[g].append(s_)
            if half or i == NT - 1:
                double_free[g] = [sp.dma(
                    double_st[g], count_t[c:c + w, (i - half) * P:(i + 1) * P].rearrange("(j p) s -> p j s", p=P),
                    double[g][:, 0:w // P, 0:half + 1, :].rearrange("p j h s -> p j (h s)"), double_free[g])]
            return t

        def multiply_turned(i, g, tb, tfree, ok):
            c, w = GROUPS[g]
            acc = i % 2
            for j in range(w // P):
                n = c // P + j
                t = pe.do(lambda e, n=n, j=j: e.matmul(bank[acc][:, 0:P], h[:, n, :], tb[:, j * P:(j + 1) * P],
                                                       start=(n == 0), stop=(n == NT - 1)),
                          ok, h_ok[g], bank_free[acc] if n == 0 else None, mark=(j == w // P - 1))
            tfree.append(t)
            return t

        nxt = load_pair(0)
        for i in range(NT):
            pbuf, pfree, p_ok = nxt
            if i + 1 < NT:
                nxt = load_pair(i + 1)
            wbuf, wfree, wafter = plain.take()
            w_ok = dve.do(lambda e, wbuf=wbuf, pbuf=pbuf: e.tensor_copy(wbuf, pbuf[:, :, 0]), p_ok, wafter)
            wfree.append(sp.dma(plain_st[plain.at], weight_n[i * P:(i + 1) * P, :], wbuf, w_ok))
            held = None
            for g in range(len(GROUPS)):
                tb, tfree, ok = turn_weights(pbuf, p_ok, i, g)
                if held:
                    multiply_turned(i, *held)
                held = (g, tb, tfree, ok)
                t = turn_counts(pbuf, p_ok, i, g)
            t2 = multiply_turned(i, *held)
            pfree.extend([t, w_ok])
            s_ = act.do(lambda e, i=i: e.copy(featT[:, i * P:(i + 1) * P], bank[i % 2][:, 0:P]), t2)
            bank_free[i % 2] = [s_]
        featT_ok = [s_] * len(GROUPS)
        for b, free in zip(flip_banks.buffers, flip_banks.free):
            bank_free[b] = free
        weight_t_ok = [(s.sem, s.value) for s in turn_st]
        count_t_ok = [(s.sem, s.value) for s in double_st]

        def counts_in_full():
            for q, n in ((pe, "pe"), (dve, "dve"), (sp, "sp")):
                read_flag(q, crowded, crowded_i[0:1, 0:1], crowded_ok)
                q.begin(crowded[q], ctx.enter_context(nc.semaphore(f"full_{n}")))
            pbuf, tb, b = pairs.buffers[0], turned.buffers[0], flip_banks.buffers[0]
            pair_again, full_st = arrival("pair_again"), arrival("full_st")
            t = s_ = stored = None
            for i in range(NT):
                p_ok = sp.dma(pair_again, pbuf, adj[i * P * NP:(i + 1) * P * NP, :].rearrange("(p n) c -> p n c", p=P),
                              adj_ok, pairs.free[0], t)
                for c, w in GROUPS:
                    for j in range(w // P):
                        t = flip(bank[b][:, j * P:(j + 1) * P], pbuf[:, c + j * P:c + (j + 1) * P, 1], p_ok, bank_free[b], s_,
                                 mark=(j == w // P - 1))
                    s_ = dve.do(lambda e, w=w: e.tensor_copy(tb[:, 0:w], bank[b][:, 0:w]), t, stored, turned.free[0])
                    if c <= i * P < c + w:
                        s_ = dve.do(lambda e, o=i * P - c: e.tensor_tensor(tb[:, o:o + P], tb[:, o:o + P], ident[:, :], ALU.add), s_)
                    stored = sp.dma(full_st, count_full[c:c + w, i * P:(i + 1) * P].rearrange("(j p) s -> p j s", p=P),
                                    tb[:, 0:w].rearrange("p (j s) -> p j s", s=P), s_)
            pe.wait(s_)
            sp.wait(stored)
            for q in (pe, dve, sp):
                q.end()

        counts_in_full()
        weight_n_ok = [(s.sem, s.value) for s in plain_st]
        mat = Slots([arena[:, k * NP:(k + 1) * NP] for k in range(MATS)])
        mat_sem = [arrival(f"mat{i}") for i in range(MATS)]
        over = pairs.free + plain.free + turned.free + double_free
        mat.free = [list(over) for _ in range(MATS)]
        mat_queue = []

        def fetch_mat(matrix, i, ready):
            buf, free, after = mat.take()
            arrived, rows_i = mat_sem[mat.at], slice(i * P, (i + 1) * P)
            if matrix is count_t:
                sp.wait(*after, *ready)
                arrived.value += 16

                def op(e, buf=buf, sem=arrived.sem):
                    with e.If(crowded[sp]["value"] < 1):
                        e.dma_start(buf.bitcast(BF16)[:, 0:N], count_t[rows_i, 0:N]).then_inc(sem, 16)
                    with e.If(crowded[sp]["value"] > 0):
                        e.dma_start(buf[:, 0:N], count_full[rows_i, 0:N]).then_inc(sem, 16)
                sp.ops.append(op)
                ok = (arrived.sem, arrived.value)
            else:
                ok = sp.dma(arrived, buf[:, 0:N], matrix[rows_i, 0:N], after, ready)
            mat_queue.append((buf, free, ok))

        plan = [(weight_t, i, weight_t_ok) for _ in range(2) for i in range(NT)] + \
               [(count_t, i, count_t_ok) for _ in range(3) for i in range(NT)] + \
               [(weight_n, i, weight_n_ok) for _ in range(3) for i in range(NT)]
        plan.reverse()
        for _ in range(MATS):
            fetch_mat(*plan.pop())

        def product(feat_ok):
            for i in range(NT):
                buf, free, ok = mat_queue.pop(0)
                t = product_tile(i, buf, ok, feat_ok)
                free.append(t[-1])
                if plan:
                    fetch_mat(*plan.pop())
            return t

        piece = [hvT[:, 0:NP // 2].bitcast(BF16), hvT[:, NP // 2:NP].bitcast(BF16),
                 arena[:, MATS * NP:MATS * NP + NP // 2].bitcast(BF16)]

        def split_group(g, feat_ok):
            c, w = GROUPS[g]
            v, vfree, vafter = vbuf.take()
            rest, ok = h.rearrange("p t f -> p (t f)")[:, c:c + w], feat_ok
            for n in range(3):
                p_ok = dve.do(lambda e, n=n, rest=rest: e.tensor_copy(piece[n][:, c:c + w], rest), ok, over, adj_ok)
                if n < 2:
                    ok = dve.do(lambda e, n=n, rest=rest: e.tensor_tensor(
                        v[:, 0:w], rest, piece[n][:, c:c + w], ALU.subtract), p_ok, vafter)
                    rest = v[:, 0:w]
            vfree.append(p_ok)
            return p_ok

        def count_product(pieces_ok):
            tiles = []

            def pieces():
                for i in range(NT):
                    buf, free, ok = mat_queue.pop(0)
                    tiles.append((buf, ok))
                    counts, t = buf.bitcast(BF16), []
                    for n in range(3):
                        for g, (c, w) in enumerate(GROUPS):
                            w = min(w, N - c)
                            t.append(pe.do(lambda e, i=i, n=n, g=g, c=c, w=w, counts=counts: e.matmul(
                                bank[g][:, 0:w], piece[n][:, i * P:(i + 1) * P], counts[:, c:c + w],
                                start=(i == 0 and n == 0), stop=(i == NT - 1 and n == 2)),
                                ok, pieces_ok[i // TPC], bank_free[g] if i == 0 and n == 0 else None,
                                mark=(n == 2 and (g == len(GROUPS) - 1 or i == NT - 1))))
                    free.append(t[-1])
                    if plan:
                        fetch_mat(*plan.pop())
                return t[-len(GROUPS):]

            def full():
                for i, (buf, ok) in enumerate(tiles):
                    t = product_tile(i, buf, ok, pieces_ok)
                return t
            return pe.either(crowded[pe], pieces, full)

        vbuf = Slots([work[:, 0, :], work[:, 1, :]] + [b[:, :] for b in he.buffers + prod.buffers])
        vbuf.free = [[over, wk_free[0], wk_free[1]] for _ in vbuf.buffers]

        def evacuate(t):
            done = []
            for g, (c, w) in enumerate(GROUPS):
                q, w = (act, dve)[g % 2], min(w, N - c)
                s = q.do(lambda e, g=g, c=c, w=w: (e.tensor_copy if g % 2 else e.copy)(featT[:, c:c + w], bank[g][:, 0:w]), t[g])
                bank_free[g] = [s]
                done.append(s)
            return done

        def gcn_out(weight, scale, bias, slope, last, follow=None):
            toks = []
            for g, (c, w) in enumerate(GROUPS):
                n, b = w // P, g
                for j in range(n):
                    t = pe.do(lambda e, b=b, j=j, c=c: e.matmul(bank[b][:, j * P:(j + 1) * P], featT[:, c + j * P:c + (j + 1) * P],
                                                                weight[:, :], start=True, stop=True), featT_ok[g], bank_free[b],
                              mark=(j == n - 1))
                v, vfree, vafter = vbuf.take()
                for j in range(n):
                    a = act.do(lambda e, v=v, b=b, j=j, c=c: e.activation(
                        v[:, j * P:(j + 1) * P], bank[b][:, j * P:(j + 1) * P], ACT.Copy,
                        scale=scale[:, c // P + j:c // P + j + 1]), t, vafter)
                bank_free[b] = [a]
                v3 = v[:, 0:w].rearrange("p (j f) -> p j f", f=P)
                h3, x3 = h[:, c // P:c // P + n, :], x[:, c // P:c // P + n, :]
                sc3 = across(scale[:, c // P:c // P + n], P)
                a = dve.do(lambda e, v3=v3, n=n: e.tensor_tensor(v3, v3, along(bias[:, :], n), ALU.add), a)
                if slope is None:
                    if last:
                        a = dve.do(lambda e, v3=v3, x3=x3: e.scalar_tensor_tensor(
                            out=x3, in0=v3, scalar=0.0, in1=x3, op0=ALU.max, op1=ALU.add), a)
                    else:
                        a = dve.do(lambda e, v3=v3, h3=h3, sc3=sc3: e.scalar_tensor_tensor(
                            out=h3, in0=v3, scalar=0.0, in1=sc3, op0=ALU.max, op1=ALU.mult), a)
                else:
                    a2 = dve.do(lambda e, v3=v3, h3=h3, n=n: e.scalar_tensor_tensor(
                        out=h3, in0=v3, scalar=0.0, in1=along(slope[:, :], n), op0=ALU.min, op1=ALU.mult), a)
                    a = dve.do(lambda e, v3=v3, h3=h3: e.scalar_tensor_tensor(
                        out=h3, in0=v3, scalar=0.0, in1=h3, op0=ALU.max, op1=ALU.add), a2)
                    if last:
                        a = pool.do(lambda e, h3=h3, x3=x3: e.tensor_tensor(x3, x3, h3, ALU.add), a)
                    else:
                        a = pool.do(lambda e, h3=h3, sc3=sc3: e.tensor_tensor(h3, h3, sc3, ALU.mult), a)
                vfree.append(a)
                toks.append(a)
                if follow and g:
                    toks[g - 1] = follow(g - 1, toks[g - 1])
            if follow:
                toks[-1] = follow(len(GROUPS) - 1, toks[-1])
            return toks

        a = dve.do(lambda e: e.tensor_reduce(carry_col[:, :], alpha[:, :], AX_X, ALU.max), tok_small)
        a = dve.do(lambda e: e.tensor_scalar(alpha[:, :], alpha[:, :], carry_col[:, 0:1], None, ALU.subtract), a)
        a = act.do(lambda e: e.activation(alpha[:, :], alpha[:, :], ACT.Exp), a)
        a = dve.do(lambda e: e.tensor_reduce(carry_col[:, :], alpha[:, :], AX_X, ALU.add), a)
        a = dve.do(lambda e: e.reciprocal(carry_col[:, :], carry_col[:, :]), a)
        al_ok = dve.do(lambda e: e.tensor_scalar(alpha[:, :], alpha[:, :], carry_col[:, 0:1], None, ALU.mult), a)

        for l in range(3):
            done = gcn_out(W[f"L1_gnn_W{l + 1}"], dis, row[f"L1_gnn_b{l + 1}"], row[f"L1_gnn_a{l + 1}"], l == 2)
            if l < 2:
                featT_ok = evacuate(product(done))
        done = [split_group(g, ok) for g, ok in enumerate(layernorm(done, None, dinv))]
        for l in range(3):
            featT_ok = evacuate(count_product(done))
            done = gcn_out(W[f"L2_gnn_W{l}"], dinv, row[f"L2_gnn_b{l}"], None, l == 2,
                           None if l == 2 else split_group)
        done = layernorm(done)
        flat_h, flat_x = h.rearrange("p t f -> p (t f)"), x.rearrange("p t f -> p (t f)")
        xk_ok = [None] * len(GROUPS)
        for k in range(4):
            if k:
                featT_ok = evacuate(product(done))
                done = []
                for g, (c, w) in enumerate(GROUPS):
                    for j in range(w // P):
                        t = flip(bank[g][:, j * P:(j + 1) * P], featT[:, c + j * P:c + (j + 1) * P], featT_ok[g], bank_free[g],
                                 mark=(j == w // P - 1))
                    done.append(act.do(lambda e, g=g, c=c, w=w: e.copy(flat_h[:, c:c + w], bank[g][:, 0:w]), t, xk_ok[g]))
                    bank_free[g] = [done[-1]]
            for g, (c, w) in enumerate(GROUPS):
                xk_ok[g] = dve.do(lambda e, c=c, w=w, k=k: e.scalar_tensor_tensor(
                    out=flat_x[:, c:c + w], in0=flat_h[:, c:c + w], scalar=alpha[:, k:k + 1], in1=flat_x[:, c:c + w],
                    op0=ALU.mult, op1=ALU.add), done[g], al_ok, xk_ok[g])
        out_st = arrival("out_st")
        full = N // P
        sp.dma(out_st, out[0:full * P, :].rearrange("(t p) f -> p t f", p=P), x[:, 0:full, :], xk_ok)
        sp.dma(out_st, out[full * P:N, :], x[0:N - full * P, full, :], xk_ok)
        sp.wait((out_st.sem, out_st.value))

        block = ctx.enter_context(nc.Block())
        for attach, queue in ((block.tensor, pe), (block.scalar, act), (block.vector, dve), (block.gpsimd, pool), (block.sync, sp)):
            def body(e, queue=queue):
                for op in queue.ops:
                    op(e)
            attach(body)


def kernel(**inputs):
    import concourse.bacc as bacc
    from concourse.bass_utils import run_bass_kernel_spmd as run

    g = {k: np.asarray(v) for k, v in inputs.items()}
    pad = np.arange(EP - E, dtype=np.int32) // 4 + N
    src = np.concatenate([g["src"], pad])
    dst = np.concatenate([g["dst"], pad])
    weight = np.concatenate([g["edge_weight"], np.zeros(EP - E, np.float32)])
    columns = lambda v: np.ascontiguousarray(v.reshape(ET, P).T)
    arrays = {
        "x": np.concatenate([g["x"], np.zeros((NP - N, P), np.float32)]),
        "src_c": columns(src), "dst_c": columns(dst),
        "edge_rows": np.concatenate([g["edge_attr_64"], np.zeros((EP - E, EF), np.float32)]),
        "w_c": columns(weight),
        "ready_dst": np.stack([dst[GROUP * P * (k + 1)] for _, k in READY_AT])[None, :],
        "ready_bound": np.array([[P * (r + 1) for r, _ in READY_AT]], np.int32),
        "src": src, "dst": np.concatenate([np.full(1, -1, np.int32), dst]),
        "tile_first": dst.reshape(ET, P)[None, :, 0].copy(), "tile_last": dst.reshape(ET, P)[None, :, P - 1].copy(),
        "edgeT": np.concatenate([g["edge_attr_64"].T, np.zeros((EF, EP - E), np.float32)], 1),
        "We1_node": g["L0_gnn_We1"][:P], "We1_edge": g["L0_gnn_We1"][P:],
        "W1_context": g["L0_gnn_W1"][:P], "W1_node": g["L0_gnn_W1"][P:],
        "We2_node": g["L0_gnn_We2"][:P], "We2_edge": g["L0_gnn_We2"][P:],
        "L0_gnn_be2": g["L0_gnn_be2"].reshape(1, 1), "L0_gnn_bet": g["L0_gnn_bet"].reshape(1, P),
        "L3_gnn_alpha_logits": g["L3_gnn_alpha_logits"].reshape(1, 4),
    }
    for n in BIAS_ROWS:
        arrays[n] = g[n].reshape(1, P)
    for n in BIAS_COLUMNS:
        arrays.setdefault(n, g[n].reshape(P, 1) if n in g else None)
    for n in WEIGHTS:
        arrays.setdefault(n, g[n] if n in g else None)
    nc = bacc.Bacc("TRN2", target_bir_lowering=False, num_devices=1)
    given = {}
    arrays = {"in_" + n: np.ascontiguousarray(a) for n, a in arrays.items()}
    for n, a in arrays.items():
        given[n[3:]] = nc.dram_tensor(n, a.shape, mybir.dt.from_np(a.dtype), kind="ExternalInput").ap()
    out = nc.dram_tensor("out", (N, P), F32, kind="ExternalOutput").ap()
    build(nc, given, out)
    r = run(nc, [arrays], core_ids=[0])
    return r.results[0]["out"]
```
